# Optimizing a Trainium2 kernel written in Bass

```python
import numpy as np
import jax
import jax.numpy as jnp

def _softmax(x, axis=-1):
    return jax.nn.softmax(x, axis=axis)

def _gelu(x):
    return jax.nn.gelu(x, approximate=True)

def _silu(x):
    return jax.nn.silu(x)

def _sigmoid(x):
    return jax.nn.sigmoid(x)

def _layernorm(x, axis=-1, eps=1e-05):
    m = jnp.mean(x, axis=axis, keepdims=True)
    v = jnp.var(x, axis=axis, keepdims=True)
    return (x - m) / jnp.sqrt(v + eps)

def _scatter_add(tgt, idx, src, axis=0):
    return tgt.at[idx].add(src)

def _segment_sum(src, seg, n):
    return jax.ops.segment_sum(src, seg, n)
kernel_name = 'mk_seq_preln_d4_jaxref_r8_04e8bd'

def setup_inputs(seed: int=0):
    np.random.seed(seed)
    _w = jnp.asarray

    def _L0_attn_setup():
        import math
        import jax, jax.numpy as jnp
        import numpy as np
        B, T, D_MODEL = (4, 256, 128)
        H, HD = (16, 64)
        NF = 128
        EPS = 1e-06
        INV_SQRT_NF = 1.0 / math.sqrt(NF)

        def make_orf(key, head_dim, n_features, dtype=jnp.float32):
            n_blocks = math.ceil(n_features / head_dim)
            keys = jax.random.split(key, n_blocks)
            blocks = []
            for k in keys:
                g = jax.random.normal(k, (head_dim, head_dim), dtype)
                qm, _ = jnp.linalg.qr(g)
                blocks.append(qm)
            W = jnp.concatenate(blocks, axis=1)[:, :n_features]
            return W * jnp.asarray(math.sqrt(head_dim), dtype)

        def _favor_plus(x, W):
            sq = 0.5 * jnp.sum(x * x, axis=-1, keepdims=True)
            return jnp.exp(x @ W - sq) * INV_SQRT_NF

        def _causal_linear_attention(qp, kp, v):
            Bb, Hh = (qp.shape[0], qp.shape[1])

            def step(carry, qkv):
                S, z = carry
                q_t, k_t, v_t = qkv
                S = S + jnp.einsum('bhd,bhe->bhde', k_t, v_t)
                z = z + k_t
                num = jnp.einsum('bhd,bhde->bhe', q_t, S)
                den = jnp.einsum('bhd,bhd->bh', q_t, z) + EPS
                return ((S, z), num / den[..., None])
            S0 = jnp.zeros((Bb, Hh, NF, HD), qp.dtype)
            z0 = jnp.zeros((Bb, Hh, NF), qp.dtype)
            xs = (jnp.moveaxis(qp, 2, 0), jnp.moveaxis(kp, 2, 0), jnp.moveaxis(v, 2, 0))
            _, ys = jax.lax.scan(step, (S0, z0), xs)
            return jnp.moveaxis(ys, 0, 2)
        key = jax.random.key(seed)
        k0, k1, k2, k3, k4, k5 = jax.random.split(key, 6)
        s = 1.0 / math.sqrt(D_MODEL)
        x = jax.random.normal(k0, (B, T, D_MODEL), jnp.float32)
        Wq = jax.random.uniform(k1, (D_MODEL, H * HD), jnp.float32, -s, s)
        Wk = jax.random.uniform(k2, (D_MODEL, H * HD), jnp.float32, -s, s)
        Wv = jax.random.uniform(k3, (D_MODEL, H * HD), jnp.float32, -s, s)
        Wo = jax.random.uniform(k4, (H * HD, D_MODEL), jnp.float32, -s, s)
        W_feat = make_orf(k5, HD, NF)
        return {'x': x, 'Wq': Wq, 'Wk': Wk, 'Wv': Wv, 'Wo': Wo, 'W_feat': W_feat}
    _L0_attn_in = _L0_attn_setup()

    def _L0_ffn_setup():
        import jax, jax.numpy as jnp
        import numpy as np
        TAU = 10.0
        EPS = 1e-06
        TOP_K = 8

        def _layernorm(x, g, b):
            mu = jnp.mean(x, axis=-1, keepdims=True)
            var = jnp.var(x, axis=-1, keepdims=True)
            return (x - mu) * jax.lax.rsqrt(var + 1e-05) * g + b

        def _unit_rows(W):
            n = jnp.linalg.norm(W, axis=1, keepdims=True)
            return W / jnp.maximum(n, EPS)
        key = jax.random.key(seed)
        ks = jax.random.split(key, 5)
        D, NB, H = (128, 64, 512)
        B, S = (4, 256)
        x = jax.random.normal(ks[0], (B, S, D), dtype=jnp.float32)
        W1 = jax.random.normal(ks[1], (H, D), dtype=jnp.float32) * (1.0 / np.sqrt(D))
        W2 = jax.random.normal(ks[2], (D, H), dtype=jnp.float32) * (1.0 / np.sqrt(H))
        ln_g = jnp.ones((D,), jnp.float32)
        ln_b = jnp.zeros((D,), jnp.float32)
        router_W = jax.random.normal(ks[3], (NB, D), dtype=jnp.float32) * 0.01
        router_b = jnp.zeros((NB,), jnp.float32)
        raw_U = jax.random.normal(ks[4], (NB, D), dtype=jnp.float32) * 0.02
        raw_V = jax.random.normal(jax.random.fold_in(key, 7), (NB, D), dtype=jnp.float32) * 0.02
        gamma = jnp.ones((1, 1, D), jnp.float32) * 0.1
        return {'x': x, 'W1': W1, 'W2': W2, 'ln_g': ln_g, 'ln_b': ln_b, 'router_W': router_W, 'router_b': router_b, 'raw_U': raw_U, 'raw_V': raw_V, 'gamma': gamma}
    _L0_ffn_in = _L0_ffn_setup()

    def _L1_attn_setup():
        import math
        import jax, jax.numpy as jnp
        import numpy as np
        B, S, D, H, DH = (2, 256, 128, 16, 64)
        INNER = H * DH

        def _l2norm(t):
            n = jnp.linalg.norm(t, axis=-1, keepdims=True)
            return t / jnp.maximum(n, 1e-12)
        key = jax.random.key(seed)
        k0, k1, k2, k3 = jax.random.split(key, 4)
        x = jax.random.normal(k0, (B, S, D), dtype=jnp.float32)
        w_q = jax.random.normal(k1, (D, INNER), dtype=jnp.float32) * 0.02
        w_kv = jax.random.normal(k2, (D, 2 * INNER), dtype=jnp.float32) * 0.02
        w_out = jax.random.normal(k3, (INNER, D), dtype=jnp.float32) * 0.02
        b_out = jnp.zeros((D,), dtype=jnp.float32)
        scale_init = -math.log(math.log2(S ** 2 - S))
        scale = jnp.full((1, H, 1, 1), scale_init, dtype=jnp.float32)
        return {'x': x, 'w_q': w_q, 'w_kv': w_kv, 'w_out': w_out, 'b_out': b_out, 'scale': scale}
    _L1_attn_in = _L1_attn_setup()

    def _L1_ffn_setup():
        import jax, jax.numpy as jnp
        import numpy as np
        INT4_QMAX = 7.0

        def simulate_quantize_int4(w):
            scale = jnp.max(jnp.abs(w)) / INT4_QMAX
            q = jnp.clip(jnp.round(w / scale), -8.0, 7.0)
            return q * scale
        key = jax.random.key(seed)
        k_x, k_w, k_bias, k_a, k_b = jax.random.split(key, 5)
        d_in, features, rank = (128, 128, 16)
        x = jax.random.normal(k_x, (4, 1024, d_in), dtype=jnp.float32)
        kernel = jax.random.normal(k_w, (d_in, features), dtype=jnp.float32)
        bias = jax.random.normal(k_bias, (features,), dtype=jnp.float32)
        a = jax.random.normal(k_a, (d_in, rank), dtype=jnp.float32) * (1.0 / np.sqrt(d_in))
        b = jax.random.normal(k_b, (rank, features), dtype=jnp.float32) * 0.01
        return {'x': x, 'kernel': kernel, 'bias': bias, 'a': a, 'b': b}
    _L1_ffn_in = _L1_ffn_setup()

    def _L2_attn_setup():
        import jax, jax.numpy as jnp
        import numpy as np
        D_MODEL, D_STATE, EXPAND = (128, 16, 2)
        D_INNER = D_MODEL * EXPAND
        DT_RANK = int(np.ceil(D_MODEL / 16))
        BATCH, SEQ = (2, 256)

        def _ssm_scan(xs, A, Bs, Cs, delta):
            batch, _, d_inner = xs.shape
            n = A.shape[1]

            def step(h, inp):
                x_t, d_t, B_t, C_t = inp
                dA = jnp.exp(d_t[:, :, None] * A)
                h = dA * h + (d_t * x_t)[:, :, None] * B_t[:, None, :]
                y = jnp.einsum('bdn,bn->bd', h, C_t)
                return (h, y)
            h0 = jnp.zeros((batch, d_inner, n), jnp.float32)
            inps = (xs.transpose(1, 0, 2), delta.transpose(1, 0, 2), Bs.transpose(1, 0, 2), Cs.transpose(1, 0, 2))
            _, ys = jax.lax.scan(step, h0, inps)
            return ys.transpose(1, 0, 2)

        def _reference_tuple_inner(x, Win, bin, Wx, bx, Wdt, bdt, A_log, Dp, Wout, bout):
            xz = x @ Win + bin
            xs, z = jnp.split(xz, 2, axis=-1)
            xs = jax.nn.silu(xs)
            xp = xs @ Wx + bx
            dp = xp[..., :DT_RANK]
            Bs = xp[..., DT_RANK:DT_RANK + D_STATE]
            Cs = xp[..., DT_RANK + D_STATE:]
            delta = jax.nn.softplus(dp @ Wdt + bdt)
            A = -jnp.exp(A_log.astype(jnp.float32))
            hidden = _ssm_scan(xs, A, Bs, Cs, delta)
            y = (hidden + xs * Dp) * jax.nn.silu(z)
            out = y @ Wout + bout
            return (out, hidden)
        key = jax.random.key(seed)
        ks = jax.random.split(key, 12)
        s_in = 1.0 / np.sqrt(D_MODEL)
        s_x = 1.0 / np.sqrt(D_INNER)
        s_dt = 1.0 / np.sqrt(DT_RANK)
        return {'x': jax.random.normal(ks[0], (BATCH, SEQ, D_MODEL), jnp.float32), 'Win': jax.random.uniform(ks[1], (D_MODEL, 2 * D_INNER), jnp.float32, -s_in, s_in), 'bin': jax.random.uniform(ks[2], (2 * D_INNER,), jnp.float32, -s_in, s_in), 'Wx': jax.random.uniform(ks[3], (D_INNER, DT_RANK + 2 * D_STATE), jnp.float32, -s_x, s_x), 'bx': jax.random.uniform(ks[4], (DT_RANK + 2 * D_STATE,), jnp.float32, -s_x, s_x), 'Wdt': jax.random.uniform(ks[5], (DT_RANK, D_INNER), jnp.float32, -s_dt, s_dt), 'bdt': jax.random.uniform(ks[6], (D_INNER,), jnp.float32, -s_dt, s_dt), 'A_log': jax.random.normal(ks[7], (D_INNER, D_STATE), jnp.float32), 'Dp': jax.random.normal(ks[8], (D_INNER,), jnp.float32), 'Wout': jax.random.uniform(ks[9], (D_INNER, D_MODEL), jnp.float32, -s_x, s_x), 'bout': jax.random.uniform(ks[10], (D_MODEL,), jnp.float32, -s_x, s_x)}
    _L2_attn_in = _L2_attn_setup()

    def _L2_ffn_setup():
        import jax, jax.numpy as jnp
        import numpy as np
        B, S, D = (2, 256, 128)
        E, K, DFF = (8, 2, 4 * 128)
        EPS_GATE = 1e-08
        EPS_LN = 1e-05
        key = jax.random.key(seed)
        ks = jax.random.split(key, 4)
        scaled = lambda k, shape, fan: jax.random.normal(k, shape, jnp.float32) / np.sqrt(fan).astype(np.float32)
        return {'x': jax.random.normal(ks[0], (B, S, D), jnp.float32), 'Wg': scaled(ks[1], (D, E), D), 'bg': jnp.zeros((E,), jnp.float32), 'W1': scaled(ks[2], (E, D, DFF), D), 'b1': jnp.zeros((E, DFF), jnp.float32), 'W2': scaled(ks[3], (E, DFF, D), DFF), 'b2': jnp.zeros((E, D), jnp.float32), 'gamma': jnp.ones((D,), jnp.float32), 'beta': jnp.zeros((D,), jnp.float32)}
    _L2_ffn_in = _L2_ffn_setup()

    def _L3_attn_setup():
        import jax, jax.numpy as jnp
        import numpy as np
        E = 128
        D = 64
        H = E // D
        EPS = 1e-05
        key = jax.random.key(seed)
        ks = jax.random.split(key, 8)
        std = 0.02
        x = jax.random.normal(ks[0], (2, 128, E), jnp.float32)
        Wq = jax.random.normal(ks[1], (E, E), jnp.float32) * std
        Wk = jax.random.normal(ks[2], (E, E), jnp.float32) * std
        Wv = jax.random.normal(ks[3], (E, E), jnp.float32) * std
        Wo = jax.random.normal(ks[4], (E, E), jnp.float32) * std
        delta = jnp.full((E,), float(np.log(0.99 / 0.01)), jnp.float32)
        G1 = jax.random.normal(ks[5], (E, D), jnp.float32) * std
        G2 = jax.random.normal(ks[6], (D, E), jnp.float32) * std
        norm_w = jnp.ones((E,), jnp.float32)
        return {'x': x, 'Wq': Wq, 'Wk': Wk, 'Wv': Wv, 'Wo': Wo, 'delta': delta, 'G1': G1, 'G2': G2, 'norm_w': norm_w}
    _L3_attn_in = _L3_attn_setup()

    def _L3_ffn_setup():
        import jax, jax.numpy as jnp
        import numpy as np
        DIM = 128
        DEPTH = 6
        HEADS = 16
        DIM_HEAD = 64
        WINDOW = 32
        INNER = HEADS * DIM_HEAD
        DIM_INNER = int(DIM * 4 * 2 / 3)
        QK_SCALE = 8.0

        def shift_tokens(t):
            a, s = jnp.split(t, 2, -1)
            s = jnp.pad(s, ((0, 0), (1, 0), (0, 0)))[:, :-1]
            return jnp.concatenate([a, s], -1)

        def l2norm(t):
            return t / jnp.maximum(jnp.linalg.norm(t, axis=-1, keepdims=True), 1e-12)

        def rotate_half(x):
            x1, x2 = jnp.split(x, 2, -1)
            return jnp.concatenate([-x2, x1], -1)

        def rotary_tables(n):
            half = jnp.arange(0, DIM_HEAD, 2, dtype=jnp.float32)
            inv_freq = 1.0 / 10000.0 ** (half / DIM_HEAD)
            t = jnp.arange(n, dtype=jnp.float32)
            freqs = t[:, None] * inv_freq[None, :]
            freqs = jnp.concatenate([freqs, freqs], -1)
            base_scale = (half + 0.4 * DIM_HEAD) / (1.4 * DIM_HEAD)
            power = (t - n // 2) / (WINDOW // 2)
            scale = base_scale[None, :] ** power[:, None]
            scale = jnp.concatenate([scale, scale], -1)
            return (freqs, scale)

        def local_attention(q, k, v):
            b, h, n, d = q.shape
            w = WINDOW
            nw = n // w
            bq = q.reshape(b, h, nw, w, d)
            bk = k.reshape(b, h, nw, w, d)
            bv = v.reshape(b, h, nw, w, d)

            def look(t):
                p = jnp.pad(t, ((0, 0), (0, 0), (1, 0), (0, 0), (0, 0)))
                return jnp.concatenate([p[:, :, :nw], p[:, :, 1:]], axis=3)
            bk2, bv2 = (look(bk), look(bv))
            seq = jnp.arange(n).reshape(nw, w)
            seq_p = jnp.pad(seq, ((1, 0), (0, 0)), constant_values=-1)
            jt = jnp.concatenate([seq_p[:nw], seq_p[1:]], axis=1)
            it = seq[:, :, None]
            jb = jt[:, None, :]
            mask = (it < jb) | (it > jb + w) | (jb == -1)
            sim = jnp.einsum('bhwie,bhwje->bhwij', bq, bk2) * QK_SCALE
            sim = jnp.where(mask, -jnp.finfo(sim.dtype).max, sim)
            attn = jax.nn.softmax(sim, -1)
            out = jnp.einsum('bhwij,bhwje->bhwie', attn, bv2)
            return out.reshape(b, h, n, d)

        def attn_layer(x, Wqkv, qs, ksc, Wo):
            b, n, _ = x.shape
            qkv = x @ Wqkv
            q, k, v = jnp.split(qkv, 3, -1)
            sh = lambda t: t.reshape(b, n, HEADS, DIM_HEAD).transpose(0, 2, 1, 3)
            q, k, v = (sh(q), sh(k), sh(v))
            q = l2norm(q) * qs
            k = l2norm(k) * ksc
            freqs, scale = rotary_tables(n)
            cos, sin = (jnp.cos(freqs), jnp.sin(freqs))
            q = q * cos * scale + rotate_half(q) * sin * scale
            inv = 1.0 / scale
            k = k * cos * inv + rotate_half(k) * sin * inv
            out = local_attention(q, k, v)
            out = out.transpose(0, 2, 1, 3).reshape(b, n, INNER)
            return out @ Wo

        def ffn_layer(x, g, bln, W1, b1, W2, b2):
            mu = x.mean(-1, keepdims=True)
            var = ((x - mu) ** 2).mean(-1, keepdims=True)
            xn = (x - mu) / jnp.sqrt(var + 1e-05) * g + bln
            hg = xn @ W1 + b1
            a, gate = jnp.split(hg, 2, -1)
            return a * jax.nn.gelu(gate, approximate=False) @ W2 + b2
        key = jax.random.key(seed)
        ks = jax.random.split(key, 8)
        B, N = (2, 256)
        init = lambda k, shape: jax.random.normal(k, shape, jnp.float32) * 0.02
        return {'x': jax.random.normal(ks[0], (B, N, DIM), jnp.float32), 'Wqkv': init(ks[1], (DEPTH, DIM, 3 * INNER)), 'q_scale': jnp.ones((DEPTH, DIM_HEAD), jnp.float32), 'k_scale': jnp.ones((DEPTH, DIM_HEAD), jnp.float32), 'Wo': init(ks[2], (DEPTH, INNER, DIM)), 'ln_g': jnp.ones((DEPTH, DIM), jnp.float32), 'ln_b': jnp.zeros((DEPTH, DIM), jnp.float32), 'W1': init(ks[3], (DEPTH, DIM, 2 * DIM_INNER)), 'b1': jnp.zeros((DEPTH, 2 * DIM_INNER), jnp.float32), 'W2': init(ks[4], (DEPTH, DIM_INNER, DIM)), 'b2': jnp.zeros((DEPTH, DIM), jnp.float32)}
    _L3_ffn_in = _L3_ffn_setup()
    _d = {'L0_attn_x': _L0_attn_in['x'], 'L0_attn_Wq': _L0_attn_in['Wq'], 'L0_attn_Wk': _L0_attn_in['Wk'], 'L0_attn_Wv': _L0_attn_in['Wv'], 'L0_attn_Wo': _L0_attn_in['Wo'], 'L0_attn_W_feat': _L0_attn_in['W_feat'], 'L0_ffn_W1': _L0_ffn_in['W1'], 'L0_ffn_W2': _L0_ffn_in['W2'], 'L0_ffn_ln_g': _L0_ffn_in['ln_g'], 'L0_ffn_ln_b': _L0_ffn_in['ln_b'], 'L0_ffn_router_W': _L0_ffn_in['router_W'], 'L0_ffn_router_b': _L0_ffn_in['router_b'], 'L0_ffn_raw_U': _L0_ffn_in['raw_U'], 'L0_ffn_raw_V': _L0_ffn_in['raw_V'], 'L0_ffn_gamma': _L0_ffn_in['gamma'], 'L1_attn_w_q': _L1_attn_in['w_q'], 'L1_attn_w_kv': _L1_attn_in['w_kv'], 'L1_attn_w_out': _L1_attn_in['w_out'], 'L1_attn_b_out': _L1_attn_in['b_out'], 'L1_attn_scale': _L1_attn_in['scale'], 'L1_ffn_kernel': _L1_ffn_in['kernel'], 'L1_ffn_bias': _L1_ffn_in['bias'], 'L1_ffn_a': _L1_ffn_in['a'], 'L1_ffn_b': _L1_ffn_in['b'], 'L2_attn_Win': _L2_attn_in['Win'], 'L2_attn_bin': _L2_attn_in['bin'], 'L2_attn_Wx': _L2_attn_in['Wx'], 'L2_attn_bx': _L2_attn_in['bx'], 'L2_attn_Wdt': _L2_attn_in['Wdt'], 'L2_attn_bdt': _L2_attn_in['bdt'], 'L2_attn_A_log': _L2_attn_in['A_log'], 'L2_attn_Dp': _L2_attn_in['Dp'], 'L2_attn_Wout': _L2_attn_in['Wout'], 'L2_attn_bout': _L2_attn_in['bout'], 'L2_ffn_Wg': _L2_ffn_in['Wg'], 'L2_ffn_bg': _L2_ffn_in['bg'], 'L2_ffn_W1': _L2_ffn_in['W1'], 'L2_ffn_b1': _L2_ffn_in['b1'], 'L2_ffn_W2': _L2_ffn_in['W2'], 'L2_ffn_b2': _L2_ffn_in['b2'], 'L2_ffn_gamma': _L2_ffn_in['gamma'], 'L2_ffn_beta': _L2_ffn_in['beta'], 'L3_attn_Wq': _L3_attn_in['Wq'], 'L3_attn_Wk': _L3_attn_in['Wk'], 'L3_attn_Wv': _L3_attn_in['Wv'], 'L3_attn_Wo': _L3_attn_in['Wo'], 'L3_attn_delta': _L3_attn_in['delta'], 'L3_attn_G1': _L3_attn_in['G1'], 'L3_attn_G2': _L3_attn_in['G2'], 'L3_attn_norm_w': _L3_attn_in['norm_w'], 'L3_ffn_Wqkv': _L3_ffn_in['Wqkv'], 'L3_ffn_q_scale': _L3_ffn_in['q_scale'], 'L3_ffn_k_scale': _L3_ffn_in['k_scale'], 'L3_ffn_Wo': _L3_ffn_in['Wo'], 'L3_ffn_ln_g': _L3_ffn_in['ln_g'], 'L3_ffn_ln_b': _L3_ffn_in['ln_b'], 'L3_ffn_W1': _L3_ffn_in['W1'], 'L3_ffn_b1': _L3_ffn_in['b1'], 'L3_ffn_W2': _L3_ffn_in['W2'], 'L3_ffn_b2': _L3_ffn_in['b2']}
    _x0 = _d['L0_attn_x']
    _d['L0_attn_x'] = jax.random.normal(jax.random.fold_in(jax.random.key(seed), 1), (16, 256, 128), dtype=_x0.dtype)
    del _x0
    return _d

def reference(L0_attn_x, L0_attn_Wq, L0_attn_Wk, L0_attn_Wv, L0_attn_Wo, L0_attn_W_feat, L0_ffn_W1, L0_ffn_W2, L0_ffn_ln_g, L0_ffn_ln_b, L0_ffn_router_W, L0_ffn_router_b, L0_ffn_raw_U, L0_ffn_raw_V, L0_ffn_gamma, L1_attn_w_q, L1_attn_w_kv, L1_attn_w_out, L1_attn_b_out, L1_attn_scale, L1_ffn_kernel, L1_ffn_bias, L1_ffn_a, L1_ffn_b, L2_attn_Win, L2_attn_bin, L2_attn_Wx, L2_attn_bx, L2_attn_Wdt, L2_attn_bdt, L2_attn_A_log, L2_attn_Dp, L2_attn_Wout, L2_attn_bout, L2_ffn_Wg, L2_ffn_bg, L2_ffn_W1, L2_ffn_b1, L2_ffn_W2, L2_ffn_b2, L2_ffn_gamma, L2_ffn_beta, L3_attn_Wq, L3_attn_Wk, L3_attn_Wv, L3_attn_Wo, L3_attn_delta, L3_attn_G1, L3_attn_G2, L3_attn_norm_w, L3_ffn_Wqkv, L3_ffn_q_scale, L3_ffn_k_scale, L3_ffn_Wo, L3_ffn_ln_g, L3_ffn_ln_b, L3_ffn_W1, L3_ffn_b1, L3_ffn_W2, L3_ffn_b2):

    def _L0_attn_ref(x, Wq, Wk, Wv, Wo, W_feat):
        import math
        import jax, jax.numpy as jnp
        import numpy as np
        B, T, D_MODEL = (4, 256, 128)
        H, HD = (16, 64)
        NF = 128
        EPS = 1e-06
        INV_SQRT_NF = 1.0 / math.sqrt(NF)

        def make_orf(key, head_dim, n_features, dtype=jnp.float32):
            n_blocks = math.ceil(n_features / head_dim)
            keys = jax.random.split(key, n_blocks)
            blocks = []
            for k in keys:
                g = jax.random.normal(k, (head_dim, head_dim), dtype)
                qm, _ = jnp.linalg.qr(g)
                blocks.append(qm)
            W = jnp.concatenate(blocks, axis=1)[:, :n_features]
            return W * jnp.asarray(math.sqrt(head_dim), dtype)

        def _favor_plus(x, W):
            sq = 0.5 * jnp.sum(x * x, axis=-1, keepdims=True)
            return jnp.exp(x @ W - sq) * INV_SQRT_NF

        def _causal_linear_attention(qp, kp, v):
            Bb, Hh = (qp.shape[0], qp.shape[1])

            def step(carry, qkv):
                S, z = carry
                q_t, k_t, v_t = qkv
                S = S + jnp.einsum('bhd,bhe->bhde', k_t, v_t)
                z = z + k_t
                num = jnp.einsum('bhd,bhde->bhe', q_t, S)
                den = jnp.einsum('bhd,bhd->bh', q_t, z) + EPS
                return ((S, z), num / den[..., None])
            S0 = jnp.zeros((Bb, Hh, NF, HD), qp.dtype)
            z0 = jnp.zeros((Bb, Hh, NF), qp.dtype)
            xs = (jnp.moveaxis(qp, 2, 0), jnp.moveaxis(kp, 2, 0), jnp.moveaxis(v, 2, 0))
            _, ys = jax.lax.scan(step, (S0, z0), xs)
            return jnp.moveaxis(ys, 0, 2)
        Bb, Tt, _ = x.shape

        def heads(W):
            return (x @ W).reshape(Bb, Tt, H, HD).transpose(0, 2, 1, 3)
        q, k, v = (heads(Wq), heads(Wk), heads(Wv))
        qp = _favor_plus(q, W_feat)
        kp = _favor_plus(k, W_feat)
        y = _causal_linear_attention(qp, kp, v)
        y = y.transpose(0, 2, 1, 3).reshape(Bb, Tt, H * HD)
        return y @ Wo

    def _L0_ffn_ref(x, W1, W2, ln_g, ln_b, router_W, router_b, raw_U, raw_V, gamma):
        import jax, jax.numpy as jnp
        import numpy as np
        TAU = 10.0
        EPS = 1e-06
        TOP_K = 8

        def _layernorm(x, g, b):
            mu = jnp.mean(x, axis=-1, keepdims=True)
            var = jnp.var(x, axis=-1, keepdims=True)
            return (x - mu) * jax.lax.rsqrt(var + 1e-05) * g + b

        def _unit_rows(W):
            n = jnp.linalg.norm(W, axis=1, keepdims=True)
            return W / jnp.maximum(n, EPS)
        B, S, D = x.shape
        x_flat = x.reshape(-1, D)
        r_raw = _layernorm(x_flat, ln_g, ln_b) @ router_W.T + router_b
        r = jnp.clip(r_raw, -TAU, TAU)
        alpha = jax.nn.softplus(r)
        phi, idx = jax.lax.top_k(alpha, TOP_K)
        S_sum = jnp.sum(phi, axis=-1, keepdims=True)
        Z = phi / (S_sum + EPS) * jnp.tanh(S_sum)
        U_sel = _unit_rows(raw_U)[idx]
        V_sel = _unit_rows(raw_V)[idx]
        h_lat = jnp.einsum('nd,nkd->nk', x_flat, U_sel)
        dyn = jnp.einsum('nk,nkd->nd', h_lat * Z, V_sel).reshape(B, S, D) * gamma
        static = (jax.nn.gelu(x_flat @ W1.T, approximate=False) @ W2.T).reshape(B, S, D)
        return static + dyn

    def _L1_attn_ref(x, w_q, w_kv, w_out, b_out, scale):
        import math
        import jax, jax.numpy as jnp
        import numpy as np
        B, S, D, H, DH = (2, 256, 128, 16, 64)
        INNER = H * DH

        def _l2norm(t):
            n = jnp.linalg.norm(t, axis=-1, keepdims=True)
            return t / jnp.maximum(n, 1e-12)
        b, s, _ = x.shape
        h = scale.shape[1]
        q = (x @ w_q).reshape(b, s, h, -1).transpose(0, 2, 1, 3)
        kv = x @ w_kv
        k, v = jnp.split(kv, 2, axis=-1)
        k = k.reshape(b, s, h, -1).transpose(0, 2, 1, 3)
        v = v.reshape(b, s, h, -1).transpose(0, 2, 1, 3)
        q = _l2norm(q) * jnp.exp(scale)
        k = _l2norm(k)
        sim = jnp.einsum('bhid,bhjd->bhij', q, k)
        attn = jax.nn.softmax(sim, axis=-1)
        out = jnp.einsum('bhij,bhjd->bhid', attn, v)
        out = out.transpose(0, 2, 1, 3).reshape(b, s, h * out.shape[-1])
        return out @ w_out + b_out

    def _L1_ffn_ref(x, kernel, bias, a, b):
        import jax, jax.numpy as jnp
        import numpy as np
        INT4_QMAX = 7.0

        def simulate_quantize_int4(w):
            scale = jnp.max(jnp.abs(w)) / INT4_QMAX
            q = jnp.clip(jnp.round(w / scale), -8.0, 7.0)
            return q * scale
        w = simulate_quantize_int4(kernel)
        y = jnp.einsum('bsd,df->bsf', x, w) + bias
        lora = jnp.einsum('bsr,rf->bsf', jnp.einsum('bsd,dr->bsr', x, a), b)
        return y + lora

    def _L2_attn_ref(x, Win, bin, Wx, bx, Wdt, bdt, A_log, Dp, Wout, bout):
        import jax, jax.numpy as jnp
        import numpy as np
        D_MODEL, D_STATE, EXPAND = (128, 16, 2)
        D_INNER = D_MODEL * EXPAND
        DT_RANK = int(np.ceil(D_MODEL / 16))
        BATCH, SEQ = (2, 256)

        def _ssm_scan(xs, A, Bs, Cs, delta):
            batch, _, d_inner = xs.shape
            n = A.shape[1]

            def step(h, inp):
                x_t, d_t, B_t, C_t = inp
                dA = jnp.exp(d_t[:, :, None] * A)
                h = dA * h + (d_t * x_t)[:, :, None] * B_t[:, None, :]
                y = jnp.einsum('bdn,bn->bd', h, C_t)
                return (h, y)
            h0 = jnp.zeros((batch, d_inner, n), jnp.float32)
            inps = (xs.transpose(1, 0, 2), delta.transpose(1, 0, 2), Bs.transpose(1, 0, 2), Cs.transpose(1, 0, 2))
            _, ys = jax.lax.scan(step, h0, inps)
            return ys.transpose(1, 0, 2)

        def _reference_tuple_inner(x, Win, bin, Wx, bx, Wdt, bdt, A_log, Dp, Wout, bout):
            xz = x @ Win + bin
            xs, z = jnp.split(xz, 2, axis=-1)
            xs = jax.nn.silu(xs)
            xp = xs @ Wx + bx
            dp = xp[..., :DT_RANK]
            Bs = xp[..., DT_RANK:DT_RANK + D_STATE]
            Cs = xp[..., DT_RANK + D_STATE:]
            delta = jax.nn.softplus(dp @ Wdt + bdt)
            A = -jnp.exp(A_log.astype(jnp.float32))
            hidden = _ssm_scan(xs, A, Bs, Cs, delta)
            y = (hidden + xs * Dp) * jax.nn.silu(z)
            out = y @ Wout + bout
            return (out, hidden)
        return _reference_tuple_inner(x, Win, bin, Wx, bx, Wdt, bdt, A_log, Dp, Wout, bout)[0]

    def _L2_ffn_ref(x, Wg, bg, W1, b1, W2, b2, gamma, beta):
        import jax, jax.numpy as jnp
        import numpy as np
        B, S, D = (2, 256, 128)
        E, K, DFF = (8, 2, 4 * 128)
        EPS_GATE = 1e-08
        EPS_LN = 1e-05
        b, s, d = x.shape
        xf = x.reshape(-1, d)
        T = xf.shape[0]
        num_experts = Wg.shape[1]
        logits = xf @ Wg + bg
        w = jax.nn.softmax(logits, axis=-1)
        top_w, top_idx = jax.lax.top_k(w, K)
        top_w = top_w / (top_w.sum(axis=-1, keepdims=True) + EPS_GATE)
        cw = jnp.zeros((T, num_experts), xf.dtype).at[jnp.arange(T)[:, None], top_idx].add(top_w)
        out = jnp.zeros_like(xf)
        for e in range(num_experts):
            h = jax.nn.gelu(xf @ W1[e] + b1[e], approximate=False)
            y = h @ W2[e] + b2[e]
            out = out + cw[:, e:e + 1] * y
        mu = out.mean(axis=-1, keepdims=True)
        var = out.var(axis=-1, keepdims=True)
        out = (out - mu) / jnp.sqrt(var + EPS_LN) * gamma + beta
        return out.reshape(b, s, d)

    def _L3_attn_ref(x, Wq, Wk, Wv, Wo, delta, G1, G2, norm_w):
        import jax, jax.numpy as jnp
        import numpy as np
        E = 128
        D = 64
        H = E // D
        EPS = 1e-05
        B, T, _ = x.shape
        q = jax.nn.silu(x @ Wq)
        v = x @ Wv
        log_f = jax.nn.log_sigmoid(x @ Wk + delta)
        k = -jnp.expm1(log_f)

        def to_tbhd(a):
            return a.reshape(B, T, H, D).transpose(1, 0, 2, 3)
        qh, kh, vh, gh = map(to_tbhd, (q, k, v, log_f))
        S0 = jnp.zeros((B, H, D, D), x.dtype)

        def step(S, inp):
            q_t, k_t, v_t, g_t = inp
            S = S * jnp.exp(g_t)[..., None] + k_t[..., None] * v_t[..., None, :]
            o_t = jnp.einsum('bhk,bhkv->bhv', q_t, S)
            return (S, o_t)
        _, o = jax.lax.scan(step, S0, (qh, kh, vh, gh))
        o = o.transpose(1, 0, 2, 3).reshape(B, T, E)
        gate = x @ G1 @ G2
        o = o * jax.nn.sigmoid(gate)
        og = o.reshape(B, T, H, D)
        og = og * jax.lax.rsqrt(jnp.mean(og * og, axis=-1, keepdims=True) + EPS)
        o = og.reshape(B, T, E) * norm_w
        return o @ Wo

    def _L3_ffn_ref(x, Wqkv, q_scale, k_scale, Wo, ln_g, ln_b, W1, b1, W2, b2):
        import jax, jax.numpy as jnp
        import numpy as np
        DIM = 128
        DEPTH = 6
        HEADS = 16
        DIM_HEAD = 64
        WINDOW = 32
        INNER = HEADS * DIM_HEAD
        DIM_INNER = int(DIM * 4 * 2 / 3)
        QK_SCALE = 8.0

        def shift_tokens(t):
            a, s = jnp.split(t, 2, -1)
            s = jnp.pad(s, ((0, 0), (1, 0), (0, 0)))[:, :-1]
            return jnp.concatenate([a, s], -1)

        def l2norm(t):
            return t / jnp.maximum(jnp.linalg.norm(t, axis=-1, keepdims=True), 1e-12)

        def rotate_half(x):
            x1, x2 = jnp.split(x, 2, -1)
            return jnp.concatenate([-x2, x1], -1)

        def rotary_tables(n):
            half = jnp.arange(0, DIM_HEAD, 2, dtype=jnp.float32)
            inv_freq = 1.0 / 10000.0 ** (half / DIM_HEAD)
            t = jnp.arange(n, dtype=jnp.float32)
            freqs = t[:, None] * inv_freq[None, :]
            freqs = jnp.concatenate([freqs, freqs], -1)
            base_scale = (half + 0.4 * DIM_HEAD) / (1.4 * DIM_HEAD)
            power = (t - n // 2) / (WINDOW // 2)
            scale = base_scale[None, :] ** power[:, None]
            scale = jnp.concatenate([scale, scale], -1)
            return (freqs, scale)

        def local_attention(q, k, v):
            b, h, n, d = q.shape
            w = WINDOW
            nw = n // w
            bq = q.reshape(b, h, nw, w, d)
            bk = k.reshape(b, h, nw, w, d)
            bv = v.reshape(b, h, nw, w, d)

            def look(t):
                p = jnp.pad(t, ((0, 0), (0, 0), (1, 0), (0, 0), (0, 0)))
                return jnp.concatenate([p[:, :, :nw], p[:, :, 1:]], axis=3)
            bk2, bv2 = (look(bk), look(bv))
            seq = jnp.arange(n).reshape(nw, w)
            seq_p = jnp.pad(seq, ((1, 0), (0, 0)), constant_values=-1)
            jt = jnp.concatenate([seq_p[:nw], seq_p[1:]], axis=1)
            it = seq[:, :, None]
            jb = jt[:, None, :]
            mask = (it < jb) | (it > jb + w) | (jb == -1)
            sim = jnp.einsum('bhwie,bhwje->bhwij', bq, bk2) * QK_SCALE
            sim = jnp.where(mask, -jnp.finfo(sim.dtype).max, sim)
            attn = jax.nn.softmax(sim, -1)
            out = jnp.einsum('bhwij,bhwje->bhwie', attn, bv2)
            return out.reshape(b, h, n, d)

        def attn_layer(x, Wqkv, qs, ksc, Wo):
            b, n, _ = x.shape
            qkv = x @ Wqkv
            q, k, v = jnp.split(qkv, 3, -1)
            sh = lambda t: t.reshape(b, n, HEADS, DIM_HEAD).transpose(0, 2, 1, 3)
            q, k, v = (sh(q), sh(k), sh(v))
            q = l2norm(q) * qs
            k = l2norm(k) * ksc
            freqs, scale = rotary_tables(n)
            cos, sin = (jnp.cos(freqs), jnp.sin(freqs))
            q = q * cos * scale + rotate_half(q) * sin * scale
            inv = 1.0 / scale
            k = k * cos * inv + rotate_half(k) * sin * inv
            out = local_attention(q, k, v)
            out = out.transpose(0, 2, 1, 3).reshape(b, n, INNER)
            return out @ Wo

        def ffn_layer(x, g, bln, W1, b1, W2, b2):
            mu = x.mean(-1, keepdims=True)
            var = ((x - mu) ** 2).mean(-1, keepdims=True)
            xn = (x - mu) / jnp.sqrt(var + 1e-05) * g + bln
            hg = xn @ W1 + b1
            a, gate = jnp.split(hg, 2, -1)
            return a * jax.nn.gelu(gate, approximate=False) @ W2 + b2
        for i in range(DEPTH):
            x = attn_layer(shift_tokens(x), Wqkv[i], q_scale[i], k_scale[i], Wo[i]) + x
            x = ffn_layer(shift_tokens(x), ln_g[i], ln_b[i], W1[i], b1[i], W2[i], b2[i]) + x
        return x
    x = L0_attn_x
    x = x + _L0_attn_ref(_layernorm(x, axis=-1), L0_attn_Wq, L0_attn_Wk, L0_attn_Wv, L0_attn_Wo, L0_attn_W_feat)
    x = x + _L0_ffn_ref(_layernorm(x, axis=-1), L0_ffn_W1, L0_ffn_W2, L0_ffn_ln_g, L0_ffn_ln_b, L0_ffn_router_W, L0_ffn_router_b, L0_ffn_raw_U, L0_ffn_raw_V, L0_ffn_gamma)
    x = x + _L1_attn_ref(_layernorm(x, axis=-1), L1_attn_w_q, L1_attn_w_kv, L1_attn_w_out, L1_attn_b_out, L1_attn_scale)
    x = x + _L1_ffn_ref(_layernorm(x, axis=-1), L1_ffn_kernel, L1_ffn_bias, L1_ffn_a, L1_ffn_b)
    x = x + _L2_attn_ref(_layernorm(x, axis=-1), L2_attn_Win, L2_attn_bin, L2_attn_Wx, L2_attn_bx, L2_attn_Wdt, L2_attn_bdt, L2_attn_A_log, L2_attn_Dp, L2_attn_Wout, L2_attn_bout)
    x = x + _L2_ffn_ref(_layernorm(x, axis=-1), L2_ffn_Wg, L2_ffn_bg, L2_ffn_W1, L2_ffn_b1, L2_ffn_W2, L2_ffn_b2, L2_ffn_gamma, L2_ffn_beta)
    x = x + _L3_attn_ref(_layernorm(x, axis=-1), L3_attn_Wq, L3_attn_Wk, L3_attn_Wv, L3_attn_Wo, L3_attn_delta, L3_attn_G1, L3_attn_G2, L3_attn_norm_w)
    x = x + _L3_ffn_ref(_layernorm(x, axis=-1), L3_ffn_Wqkv, L3_ffn_q_scale, L3_ffn_k_scale, L3_ffn_Wo, L3_ffn_ln_g, L3_ffn_ln_b, L3_ffn_W1, L3_ffn_b1, L3_ffn_W2, L3_ffn_b2)
    return x

_drawn_inputs = setup_inputs


def setup_inputs(seed=0):
    import zlib

    import numpy as np

    out = dict(_drawn_inputs(seed))
    spreads = {'L0_ffn_ln_g': (1.0, 0.2),
     'L0_ffn_ln_b': (0.0, 0.1),
     'L0_ffn_router_b': (0.0, 0.1),
     'L0_ffn_gamma': (0.10000000149011612, 0.2),
     'L1_attn_b_out': (0.0, 0.1),
     'L1_attn_scale': (-2.772235631942749, 0.2),
     'L2_ffn_bg': (0.0, 0.1),
     'L2_ffn_b1': (0.0, 0.1),
     'L2_ffn_b2': (0.0, 0.1),
     'L2_ffn_gamma': (1.0, 0.2),
     'L2_ffn_beta': (0.0, 0.1),
     'L3_attn_delta': (4.595119953155518, 0.2),
     'L3_attn_norm_w': (1.0, 0.2),
     'L3_ffn_q_scale': (1.0, 0.2),
     'L3_ffn_k_scale': (1.0, 0.2),
     'L3_ffn_ln_g': (1.0, 0.2),
     'L3_ffn_ln_b': (0.0, 0.1),
     'L3_ffn_b1': (0.0, 0.1),
     'L3_ffn_b2': (0.0, 0.1)}
    factors = {}
    for name, (base, spread) in spreads.items():
        noise = np.random.default_rng([zlib.crc32(name.encode()), seed]).standard_normal(out[name].shape)
        drawn = base * np.exp(spread * noise) if base else spread * noise
        out[name] = jnp.asarray(drawn.astype(out[name].dtype))
    for name, factor in factors.items():
        out[name] = (out[name] * factor).astype(out[name].dtype)
    return out
```

```python
from contextlib import ExitStack

import numpy as np
import concourse.bass as bass
from concourse import mybir

ALU = mybir.AluOpType
ACT = mybir.ActivationFunctionType
AX_X = mybir.AxisListType.X
F32 = mybir.dt.float32
U32 = mybir.dt.uint32

P = 128
BATCH, SEQ, D = 16, 256, 128
TILES = BATCH * SEQ // P
GT = 4
GN = GT * P
GROUPS = TILES // GT
GB = GN // SEQ
ST = SEQ // P
H, HD = 16, 64
PAIRS = H // 2
INNER = H * HD
NF = 128
LN_EPS = 1e-5
DEPTH, WINDOW = 6, 32
MLP = D * 4 * 2 // 3
MLP_CHUNKS = [(lo, min(P, MLP - lo)) for lo in range(0, MLP, P)]
EXP_LN = "natural_log_exp_and_others"
KEYS0, CAUSAL = SEQ, SEQ + P


def signals(nc, ctx, names):
    return [ctx.enter_context(nc.semaphore(n)) for n in names.split()]


def restart(nc, sems):
    numbers = sorted(s.num for s in sems)
    starts = [n for n in numbers if n - 1 not in numbers]
    ends = [n + 1 for n in numbers if n + 1 not in numbers]
    for a, b in zip(starts, ends):
        nc.all_engine_barrier(sems_to_clear=range(a, b))


def spread(a, n):
    return a.unsqueeze(-1).broadcast_to([*a.shape, n])


class LayerNorm:

    def __init__(self, nc, ctx, consts, bank, name):
        sb = lambda n, s: ctx.enter_context(nc.sbuf_tensor(n.replace("ln", name, 1), s, F32))
        self.ident, self.bank = consts["ident"], bank
        self.stats, self.moments = sb("ln_stats_t", [P, GT, 6]), sb("ln_moments_t", [P, GT, 2])
        self.var, self.log, self.rstd = sb("ln_var_t", [P, GT]), sb("ln_log_t", [P, GT]), sb("ln_rstd_t", [P, GT])
        self.xn = sb("ln_xn", [P, GT, D])
        self.xnT = sb("ln_xnT", [P, GN])
        self.sems = signals(nc, ctx, "ln_stats ln_moments ln_var ln_log ln_rstd ln_normed ln_turned ln_ready".replace("ln_", name + "_"))
        (self.stats_done, self.moments_done, self.var_done, self.log_done, self.rstd_done, self.normed,
         self.turned, self.ready) = self.sems

    def vector(self, dve, x):
        for t in range(GT):
            dve.bn_stats(self.stats[:, t, :], x[:, t, :]).then_inc(self.stats_done, 1)
        dve.wait_ge(self.stats_done, GT)
        for t in range(GT):
            dve.bn_aggr(self.moments[:, t, :], self.stats[:, t, :]).then_inc(self.moments_done, 1)
        dve.wait_ge(self.moments_done, GT)
        dve.tensor_scalar(self.var[:], self.moments[:, :, 1], LN_EPS, None, ALU.add).then_inc(self.var_done, 1)
        dve.wait_ge(self.rstd_done, 1)
        for t in range(GT):
            dve.tensor_scalar(self.xn[:, t, :], x[:, t, :], self.moments[:, t, 0:1], self.rstd[:, t:t + 1],
                              ALU.subtract, ALU.mult).then_inc(self.normed, 1)

    def scalar(self, act, copy=True):
        act.wait_ge(self.var_done, 1)
        act.activation(self.log[:], self.var[:], ACT.Ln).then_inc(self.log_done, 1)
        act.wait_ge(self.log_done, 1)
        act.activation(self.rstd[:], self.log[:], ACT.Exp, scale=-0.5).then_inc(self.rstd_done, 1)
        if copy:
            act.wait_ge(self.turned, GT)
            act.copy(self.xnT[:], self.bank).then_inc(self.ready, 1)

    def tensor(self, pe):
        for t in range(GT):
            pe.wait_ge(self.normed, t + 1)
            pe.transpose(self.bank[:, t * P:(t + 1) * P], self.xn[:, t, :], self.ident).then_inc(self.turned, 1)


def favor_attention(nc, x, banks, consts, w):
    EPS = 1e-6 * NF
    with ExitStack() as ctx:
        sb = lambda n, s: ctx.enter_context(nc.sbuf_tensor("favor_" + n, s, F32))
        ln = LayerNorm(nc, ctx, consts, banks[:, 7, :], "favor_ln")
        qs, ks = sb("qs", [P, 2, GN]), sb("ks", [P, 2, GN])
        qf, kf = sb("qf", [P, 2, GN]), sb("kf", [P, 2, GN])
        scores = sb("scores", [P, 2, GB, CAUSAL])
        v1 = sb("v1", [P, GT, H, HD + 1])
        den, rden = sb("den", [P, 2, GT]), sb("rden", [P, 2, GT])
        y, yT = sb("y", [P, 2, GT, D]), sb("yT", [P, PAIRS, GN])
        sems = signals(nc, ctx, "projected squared copied featured exped scored masked summed den_ready "
                                "rden_ready head_done v_projected v_copied y_turned y_copied out_ready added")
        (projected, squared, copied, featured, exped, scored, masked, summed, den_ready, rden_ready, head_done,
         v_projected, v_copied, y_turned, y_copied, out_ready, added) = sems
        sems = ln.sems + sems

        with nc.Block() as block:
            @block.sync
            def _(sp):
                sp.wait_ge(w["loaded"], w["total"])

            @block.vector
            def _(dve):
                dve.memset(v1[:, :, :, HD:HD + 1], 1.0)

            @block.scalar
            def _(act):
                act.preload_act_table_set(EXP_LN)

        with nc.Fori(0, GROUPS) as g:
            xg = x[:, bass.ds(g * GT, GT), :]
            with nc.Block() as block:
                @block.tensor
                def _(pe):
                    ln.tensor(pe)
                    pe.wait_ge(ln.ready, 1)
                    for n in range(2 * GT):
                        if n >= 2:
                            pe.wait_ge(v_copied, n - 1)
                        pe.matmul(banks[:, 4 + n % 2, :], ln.xnT[:, (n // 2) * P:(n // 2 + 1) * P],
                                  w["Wv"][:, (n % 2) * 512:(n % 2 + 1) * 512], start=True, stop=True)\
                            .then_inc(v_projected, 1)

                    def project(h):
                        for n, name in enumerate(("Wq2", "Wk2")):
                            if h:
                                pe.wait_ge(squared, 2 * (h - 1) + n + 1)
                                pe.wait_ge(copied, 2 * (h - 1) + n + 1)
                            pe.matmul(banks[:, n, :], w[name][:, h, :], ln.xnT[:], start=True, stop=True)\
                                .then_inc(projected, 1)

                    def features(h):
                        for n, s in enumerate((qs, ks)):
                            pe.wait_ge(squared, 2 * h + n + 1)
                            pe.wait_ge(copied, 2 * h + n + 1)
                            if h:
                                pe.wait_ge(exped, 2 * (h - 1) + n + 1)
                            pe.matmul(banks[:, 2 + n, :], w["Wfeat"][:], s[:, h % 2, :], start=True, stop=True)\
                                .then_inc(featured, 1)

                    def score(h):
                        pe.wait_ge(exped, 2 * h + 2)
                        if h == 0:
                            pe.wait_ge(v_copied, 2 * GT)
                        for b in range(GB):
                            if h:
                                pe.wait_ge(masked, GB * (h - 1) + b + 1)
                            c = b * SEQ
                            pe.matmul(banks[:, 4 + b, 0:SEQ], kf[:, h % 2, c:c + P], qf[:, h % 2, c:c + SEQ],
                                      start=True, stop=True)
                            pe.matmul(banks[:, 4 + b, SEQ:CAUSAL], kf[:, h % 2, c + P:c + SEQ],
                                      qf[:, h % 2, c + P:c + SEQ], start=True, stop=True).then_inc(scored, 1)

                    def values(h):
                        pe.wait_ge(masked, GB * (h + 1))
                        if h:
                            pe.wait_ge(head_done, h)
                        for b in range(GB):
                            for i in range(ST):
                                out = banks[:, 6, (b * ST + i) * (HD + 1):(b * ST + i + 1) * (HD + 1)]
                                for j in range(i + 1):
                                    c = (i * P if j == 0 else SEQ)
                                    last = pe.matmul(out, scores[:, h % 2, b, c:c + P], v1[:, b * ST + j, h, :],
                                                     start=(j == 0), stop=(j == i))
                        last.then_inc(summed, 1)

                    def turn(j):
                        pe.wait_ge(head_done, 2 * j + 2)
                        if j:
                            pe.wait_ge(y_copied, j)
                        for t in range(GT):
                            last = pe.transpose(banks[:, 7, t * P:(t + 1) * P], y[:, j % 2, t, :],
                                                consts["ident"])
                        last.then_inc(y_turned, 1)

                    for i in range(H + 5):
                        if i < H:
                            project(i)
                        if 1 <= i <= H:
                            features(i - 1)
                        if 2 <= i <= H + 1:
                            score(i - 2)
                        if 3 <= i <= H + 2:
                            values(i - 3)
                        if i >= 5 and i % 2:
                            turn((i - 5) // 2)
                    pe.wait_ge(y_copied, PAIRS)
                    for t in range(GT):
                        for j in range(PAIRS):
                            last = pe.matmul(banks[:, 0, t * P:(t + 1) * P], yT[:, j, t * P:(t + 1) * P],
                                             w["Wo"][:, j, :], start=(j == 0), stop=(j == PAIRS - 1))
                    last.then_inc(out_ready, 1)

                @block.scalar
                def _(act):
                    ln.scalar(act)
                    for n in range(2 * GT):
                        act.wait_ge(v_projected, n + 1)
                        act.copy(v1[:, n // 2, (n % 2) * PAIRS:(n % 2 + 1) * PAIRS, 0:HD],
                                 banks[:, 4 + n % 2, :].rearrange("p (h d) -> p h d", d=HD)).then_inc(v_copied, 1)

                    def square(h):
                        for n, s in enumerate((qs, ks)):
                            act.wait_ge(projected, 2 * h + n + 1)
                            if h >= 2:
                                act.wait_ge(featured, 2 * (h - 2) + n + 1)
                            act.activation(s[HD:P, h % 2, :], banks[HD:P, n, :], ACT.Square).then_inc(squared, 1)

                    def exp(h):
                        for n, f in enumerate((qf, kf)):
                            act.wait_ge(featured, 2 * h + n + 1)
                            if h >= 2:
                                act.wait_ge(scored, GB * (h - 1))
                            act.activation(f[:, h % 2, :], banks[:, 2 + n, :], ACT.Exp).then_inc(exped, 1)

                    def y_copy(j):
                        act.wait_ge(y_turned, j + 1)
                        act.copy(yT[:, j, :], banks[:, 7, :]).then_inc(y_copied, 1)

                    for i in range(H + 5):
                        if i < H:
                            square(i)
                        if 1 <= i <= H:
                            exp(i - 1)
                        if i >= 5 and i % 2:
                            y_copy((i - 5) // 2)

                @block.vector
                def _(dve):
                    ln.vector(dve, xg)

                    def copy(h):
                        for n, s in enumerate((qs, ks)):
                            dve.wait_ge(projected, 2 * h + n + 1)
                            if h >= 2:
                                dve.wait_ge(featured, 2 * (h - 2) + n + 1)
                            dve.tensor_copy(s[0:HD, h % 2, :], banks[0:HD, n, :]).then_inc(copied, 1)

                    def mask(h):
                        if h >= 2:
                            dve.wait_ge(summed, h - 1)
                        for b in range(GB):
                            dve.wait_ge(scored, GB * h + b + 1)
                            dve.tensor_tensor(scores[:, h % 2, b, :], banks[:, 4 + b, 0:CAUSAL], consts["causal"],
                                              ALU.mult).then_inc(masked, 1)

                    def normalize(h):
                        dve.wait_ge(summed, h + 1)
                        out = banks[:, 6, 0:GT * (HD + 1)].rearrange("p (t e) -> p t e", e=HD + 1)
                        dve.tensor_scalar(den[:, h % 2, :], out[:, :, HD], EPS, None, ALU.add).then_inc(den_ready, 1)
                        dve.wait_ge(den_ready, h + 1)
                        dve.reciprocal(rden[:, h % 2, :], den[:, h % 2, :]).then_inc(rden_ready, 1)
                        dve.wait_ge(rden_ready, h + 1)
                        if h >= 4:
                            dve.wait_ge(y_turned, h // 2 - 1)
                        dve.tensor_tensor(y[:, h // 2 % 2, :, h % 2 * HD:(h % 2 + 1) * HD], out[:, :, 0:HD],
                                          spread(rden[:, h % 2, :], HD), ALU.mult)\
                            .then_inc(head_done, 1)

                    for i in range(H + 4):
                        if i < H:
                            copy(i)
                        if 2 <= i <= H + 1:
                            mask(i - 2)
                        if 3 <= i <= H + 2:
                            normalize(i - 3)
                    dve.wait_ge(out_ready, 1)
                    dve.tensor_tensor(xg, xg, banks[:, 0, :].rearrange("p (t d) -> p t d", d=D), ALU.add)\
                        .then_inc(added, 1)
            restart(nc, sems)

def router_ffn(nc, x, banks, consts, w):
    DFF, NB, TOP, TAU, EPS = 512, 64, 8, 10.0, 1e-6
    CH = DFF // P
    with ExitStack() as ctx:
        sb = lambda n, s: ctx.enter_context(nc.sbuf_tensor("router_" + n, s, F32))
        ln = LayerNorm(nc, ctx, consts, banks[:, 2, :], "router_ln")
        ln2 = LayerNorm(nc, ctx, consts, banks[:, 3, :], "router_ln2")
        unT, vg = sb("unT", [P, NB]), sb("vg", [NB, D])
        rows, sq, ss, root = sb("unit_rows", [NB, 2, D]), sb("unit_sq", [NB, 2, D]), sb("unit_ss", [NB, 2]), sb("unit_root", [NB, 2])
        hT = sb("hT", [P, CH, GN])
        r, alpha, left = sb("r", [P, GT, NB]), sb("alpha", [P, GT, NB]), sb("left", [P, GT, NB])
        top, total, tanh, rtotal = sb("top", [P, GT, TOP]), sb("total", [P, GT]), sb("tanh", [P, GT]), sb("rtotal", [P, GT])
        phi, coef, picked, pickedT = sb("phi", [P, GT, NB]), sb("coef", [P, GT]), sb("picked", [P, GT, NB]), sb("pickedT", [NB, GN])
        steps, turned, read = signals(nc, ctx, "unit_steps unit_turned unit_read")
        sems = signals(nc, ctx, "widened gelu_done logits clipped exped alpha_ready top_ready left_ready phi_ready "
                                "total_ready tanh_ready eps_added coef_part coef_ready latent picked_part picked_ready "
                                "picked_turned picked_copied out_ready added")
        (widened, gelu_done, logits, clipped, exped, alpha_ready, top_ready, left_ready, phi_ready, total_ready,
         tanh_ready, eps_added, coef_part, coef_ready, latent, picked_part, picked_ready, picked_turned,
         picked_copied, out_ready, added) = sems
        sems = ln.sems + ln2.sems + [steps, turned, read] + sems

        with nc.Block() as block:
            @block.sync
            def _(sp):
                sp.wait_ge(w["loaded"], w["total"])
        with nc.Block() as block:
            @block.scalar
            def _(act):
                act.preload_act_table_set(EXP_LN)
                for n, name in enumerate(("U", "V")):
                    act.activation(sq[:, n, :], w[name][:], ACT.Square).then_inc(steps, 1)
                act.wait_ge(steps, 4)
                act.activation(root[:], ss[:], ACT.Ln).then_inc(steps, 1)
                act.wait_ge(steps, 5)
                act.activation(ss[:], root[:], ACT.Exp, scale=-0.5).then_inc(steps, 1)

            @block.vector
            def _(dve):
                dve.wait_ge(steps, 2)
                dve.tensor_reduce(ss[:], sq[:], AX_X, ALU.add).then_inc(steps, 1)
                dve.wait_ge(steps, 3)
                dve.tensor_scalar(ss[:], ss[:], EPS * EPS, None, ALU.max).then_inc(steps, 1)
                dve.wait_ge(steps, 6)
                for n, name in enumerate(("U", "V")):
                    dve.tensor_scalar(rows[:, n, :], w[name][:], ss[:, n:n + 1], None, ALU.mult).then_inc(steps, 1)
                dve.wait_ge(steps, 8)
                dve.tensor_tensor(vg[:], rows[:, 1, :], w["gamma"][:], ALU.mult).then_inc(read, 1)
                dve.wait_ge(turned, 1)
                dve.tensor_copy(unT[:], banks[:, 0, 0:NB]).then_inc(read, 1)

            @block.tensor
            def _(pe):
                pe.wait_ge(steps, 7)
                pe.transpose(banks[:, 0, 0:NB], rows[:, 0, :], consts["ident"][0:NB, 0:NB]).then_inc(turned, 1)
        restart(nc, sems)

        with nc.Fori(0, GROUPS) as g:
            xg = x[:, bass.ds(g * GT, GT), :]
            with nc.Block() as block:
                @block.tensor
                def _(pe):
                    ln.tensor(pe)
                    pe.wait_ge(ln.ready, 1)
                    for t in range(GT):
                        last = pe.matmul(banks[:, 5, t * NB:(t + 1) * NB], ln.xnT[:, t * P:(t + 1) * P], unT[:],
                                         start=True, stop=True)
                    last.then_inc(latent, 1)
                    for c in range(2):
                        pe.matmul(banks[:, c, :], w["W1T"][:, c * P:(c + 1) * P], ln.xnT[:], start=True, stop=True)\
                            .then_inc(widened, 1)
                    ln2.tensor(pe)
                    pe.wait_ge(ln2.ready, 1)
                    for t in range(GT):
                        o = banks[:, 4, t * NB:(t + 1) * NB]
                        pe.matmul(o, ln2.xnT[:, t * P:(t + 1) * P], w["RT"][:], start=True, stop=False)
                        last = pe.matmul(o, consts["ones"][0:1, 0:P], w["rb"][:], start=False, stop=True)
                    last.then_inc(logits, 1)
                    for c in range(2, CH):
                        pe.wait_ge(gelu_done, c - 1)
                        pe.matmul(banks[:, c % 2, :], w["W1T"][:, c * P:(c + 1) * P], ln.xnT[:], start=True, stop=True)\
                            .then_inc(widened, 1)
                    for t in range(GT):
                        pe.wait_ge(picked_ready, 1)
                        last = pe.transpose(banks[0:NB, 6, t * P:(t + 1) * P], picked[:, t, :], consts["ident"])
                    last.then_inc(picked_turned, 1)
                    pe.wait_ge(gelu_done, CH)
                    pe.wait_ge(picked_copied, 1)
                    for t in range(GT):
                        o = banks[:, 7, t * P:(t + 1) * P]
                        for c in range(CH):
                            pe.matmul(o, hT[:, c, t * P:(t + 1) * P], w["W2T"][:, c, :], start=(c == 0), stop=False)
                        last = pe.matmul(o, pickedT[:, t * P:(t + 1) * P], vg[:], start=False, stop=True)
                    last.then_inc(out_ready, 1)

                @block.scalar
                def _(act):
                    act.preload_act_table_set(EXP_LN)
                    ln.scalar(act)
                    ln2.scalar(act, copy=False)
                    act.wait_ge(ln2.turned, GT)
                    act.activation(ln2.xnT[:], banks[:, 3, :], ACT.Identity, bias=w["ln_b"][:], scale=w["ln_g"][:])\
                        .then_inc(ln2.ready, 1)
                    act.wait_ge(clipped, 1)
                    act.activation(r[:], r[:], ACT.Exp).then_inc(exped, 1)
                    act.wait_ge(exped, 1)
                    act.activation(alpha[:], r[:], ACT.Ln, bias=1.0).then_inc(alpha_ready, 1)
                    for c in range(CH):
                        act.wait_ge(widened, c + 1)
                        act.activation(hT[:, c, :], banks[:, c % 2, :], ACT.Gelu).then_inc(gelu_done, 1)
                    act.wait_ge(total_ready, 1)
                    act.activation(tanh[:], total[:], ACT.Tanh).then_inc(tanh_ready, 1)
                    act.wait_ge(picked_turned, 1)
                    act.copy(pickedT[:], banks[0:NB, 6, :]).then_inc(picked_copied, 1)

                @block.vector
                def _(dve):
                    ln.vector(dve, xg)
                    dve.wait_ge(ln.normed, GT)
                    ln2.vector(dve, ln.xn)
                    dve.wait_ge(logits, 1)
                    dve.tensor_scalar(r[:], banks[:, 4, 0:GT * NB].rearrange("p (t n) -> p t n", n=NB), -TAU, TAU,
                                      ALU.max, ALU.min).then_inc(clipped, 1)
                    dve.wait_ge(alpha_ready, 1)
                    for t in range(GT):
                        dve.max(top[:, t, :], alpha[:, t, :]).then_inc(top_ready, 1)
                    dve.wait_ge(top_ready, GT)
                    for t in range(GT):
                        dve.match_replace(left[:, t, :], top[:, t, :], alpha[:, t, :], -1.0).then_inc(left_ready, 1)
                    dve.tensor_reduce(total[:], top[:], AX_X, ALU.add).then_inc(total_ready, 1)
                    dve.wait_ge(left_ready, GT)
                    dve.scalar_tensor_tensor(phi[:], left[:], 0.0, alpha[:], ALU.is_lt, ALU.mult).then_inc(phi_ready, 1)
                    dve.wait_ge(total_ready, 1)
                    dve.tensor_scalar(rtotal[:], total[:], EPS, None, ALU.add).then_inc(eps_added, 1)
                    dve.wait_ge(eps_added, 1)
                    dve.reciprocal(coef[:], rtotal[:]).then_inc(coef_part, 1)
                    dve.wait_ge(coef_part, 1)
                    dve.wait_ge(tanh_ready, 1)
                    dve.tensor_tensor(coef[:], coef[:], tanh[:], ALU.mult).then_inc(coef_ready, 1)
                    dve.wait_ge(phi_ready, 1)
                    dve.wait_ge(latent, 1)
                    dve.tensor_tensor(picked[:], phi[:], banks[:, 5, 0:GT * NB].rearrange("p (t n) -> p t n", n=NB),
                                      ALU.mult).then_inc(picked_part, 1)
                    dve.wait_ge(coef_ready, 1)
                    dve.wait_ge(picked_part, 1)
                    dve.tensor_tensor(picked[:], picked[:], spread(coef[:], NB), ALU.mult).then_inc(picked_ready, 1)
                    dve.wait_ge(out_ready, 1)
                    dve.tensor_tensor(xg, xg, banks[:, 7, :].rearrange("p (t d) -> p t d", d=D), ALU.add)\
                        .then_inc(added, 1)
            restart(nc, sems)


def cosine_attention(nc, x, banks, consts, w):
    HALF = INNER // 2
    UP = 2.0 ** 32
    with ExitStack() as ctx:
        sb = lambda n, s: ctx.enter_context(nc.sbuf_tensor("cosine_" + n, s, F32))
        ln = LayerNorm(nc, ctx, consts, banks[:, 7, :], "cosine_ln")
        peak, npeak = sb("peak", [P, H]), sb("npeak", [P, H])
        raw = sb("raw", [P, 2, GT, INNER])
        sq = sb("sq", [P, 2, HALF])
        ss, lg, inv = sb("ss", [P, 2, GT, H]), sb("lg", [P, 2, GT, H]), sb("inv", [P, 2, GT, H])
        turned_qk = sb("turned_qk", [P, 2, 2, GN])
        probs = sb("probs", [P, 2, GB, ST * SEQ])
        v1 = sb("v1", [P, GT, H, HD + 1])
        rden = sb("rden", [P, 2, GT])
        y = sb("y", [P, 2, GT, D])
        yT = lambda j: raw[:, 0, :, j * P:(j + 1) * P]
        sems = signals(nc, ctx, "projected squared copied reduced clamped logged rooted scaled unit_v unit_g qk_turned "
                                "qk_copied scored exped summed rden_ready head_done v_copied y_turned y_copied "
                                "out_ready added peak_ready npeak_ready")
        (projected, squared, copied, reduced, clamped, logged, rooted, scaled, unit_v, unit_g, qk_turned, qk_copied,
         scored, exped, summed, rden_ready, head_done, v_copied, y_turned, y_copied, out_ready, added, peak_ready,
         npeak_ready) = sems
        sems = ln.sems + sems
        QK = 4 * GT
        POOL_UNITS = 2

        with nc.Block() as block:
            @block.sync
            def _(sp):
                sp.wait_ge(w["loaded"], w["total"])
        with nc.Block() as block:
            @block.scalar
            def _(act):
                act.preload_act_table_set(EXP_LN)
                act.activation(peak[:], w["scale"][:], ACT.Exp).then_inc(peak_ready, 1)

            @block.vector
            def _(dve):
                dve.memset(v1[:, :, :, HD:HD + 1], 1.0)
                dve.wait_ge(peak_ready, 1)
                dve.tensor_scalar(npeak[:], peak[:], -1.0, None, ALU.mult).then_inc(npeak_ready, 1)
        restart(nc, sems)

        with nc.Fori(0, GROUPS) as g:
            xg = x[:, bass.ds(g * GT, GT), :]
            with nc.Block() as block:
                @block.tensor
                def _(pe):
                    ln.tensor(pe)
                    pe.wait_ge(ln.ready, 1)
                    for n in range(QK + 2 * GT):
                        if 4 <= n < QK + 4:
                            pe.wait_ge(copied, n - 3)
                        elif n >= QK + 4:
                            pe.wait_ge(v_copied, n - QK - 3)
                        t, m, half = (n // 4, n // 2 % 2, n % 2) if n < QK else ((n - QK) // 2, 2, n % 2)
                        c = m * INNER + half * HALF
                        pe.matmul(banks[:, n % 4, :], ln.xnT[:, t * P:(t + 1) * P], w["Wqkv"][:, c:c + HALF],
                                  start=True, stop=True).then_inc(projected, 1)

                    def turn_qk(j):
                        if j:
                            pe.wait_ge(qk_copied, 2 * j)
                        for m in range(2):
                            for t in range(GT):
                                if j == 0:
                                    u = m * GT + t
                                    if u < POOL_UNITS:
                                        pe.wait_ge(unit_g, u + 1)
                                    else:
                                        pe.wait_ge(unit_v, u - POOL_UNITS + 1)
                                last = pe.transpose(banks[:, 4 + m, t * P:(t + 1) * P],
                                                    raw[:, m, t, j * P:(j + 1) * P], consts["ident"])
                            last.then_inc(qk_turned, 1)

                    def score(h):
                        pe.wait_ge(qk_copied, 2 * (h // 2) + 2)
                        if h == 0:
                            pe.wait_ge(v_copied, 2 * GT)
                        if h >= 2:
                            pe.wait_ge(exped, GB * (h - 1))
                        lo = HD * (h % 2)
                        q, k = (turned_qk[lo:lo + HD, h // 2 % 2, m, :] for m in range(2))
                        for b in range(GB):
                            for s in range(ST):
                                c = b * SEQ
                                last = pe.matmul(banks[:, 2 * (h % 2) + b, s * SEQ:(s + 1) * SEQ],
                                                 k[:, c + s * P:c + (s + 1) * P], q[:, c:c + SEQ], start=True, stop=True)
                            last.then_inc(scored, 1)

                    def values(h):
                        pe.wait_ge(exped, GB * (h + 1))
                        if h:
                            pe.wait_ge(head_done, h)
                        for b in range(GB):
                            for i in range(ST):
                                o = banks[:, 6, (b * ST + i) * (HD + 1):(b * ST + i + 1) * (HD + 1)]
                                for s in range(ST):
                                    c = s * SEQ + i * P
                                    last = pe.matmul(o, probs[:, h % 2, b, c:c + P], v1[:, b * ST + s, h, :],
                                                     start=(s == 0), stop=(s == ST - 1))
                        last.then_inc(summed, 1)

                    def turn_y(j):
                        pe.wait_ge(head_done, 2 * j + 2)
                        if j:
                            pe.wait_ge(y_copied, j)
                        for t in range(GT):
                            last = pe.transpose(banks[:, 7, t * P:(t + 1) * P], y[:, j % 2, t, :],
                                                consts["ident"])
                        last.then_inc(y_turned, 1)

                    for i in range(H + 4):
                        if i % 2 == 0 and i < H:
                            turn_qk(i // 2)
                        if 1 <= i <= H:
                            score(i - 1)
                        if 2 <= i <= H + 1:
                            values(i - 2)
                        if i >= 4 and i % 2 == 0:
                            turn_y((i - 4) // 2)
                    pe.wait_ge(y_copied, PAIRS)
                    for t in range(GT):
                        o = banks[:, 4, t * P:(t + 1) * P]
                        for j in range(PAIRS):
                            pe.matmul(o, yT(j)[:, t, :], w["Wo"][:, j, :], start=(j == 0), stop=False)
                        last = pe.matmul(o, consts["ones"][0:1, 0:P], w["bo"][:], start=False, stop=True)
                    last.then_inc(out_ready, 1)

                @block.scalar
                def _(act):
                    ln.scalar(act)
                    for n in range(QK):
                        act.wait_ge(copied, n + 1)
                        if n >= 2:
                            act.wait_ge(reduced, n - 1)
                        t, m, half = n // 4, n // 2 % 2, n % 2
                        act.activation(sq[:, n % 2, :], raw[:, m, t, half * HALF:(half + 1) * HALF], ACT.Square)\
                            .then_inc(squared, 1)
                    for n in range(2 * GT):
                        act.wait_ge(projected, QK + n + 1)
                        act.copy(v1[:, n // 2, (n % 2) * PAIRS:(n % 2 + 1) * PAIRS, 0:HD],
                                 banks[:, n % 4, :].rearrange("p (h d) -> p h d", d=HD)).then_inc(v_copied, 1)
                        if n == 3:
                            act.wait_ge(clamped, 1)
                            act.activation(lg[:], ss[:], ACT.Ln).then_inc(logged, 1)
                            act.wait_ge(logged, 1)
                            act.activation(inv[:], lg[:], ACT.Exp, scale=-0.5).then_inc(rooted, 1)

                    def copy_qk(j):
                        for m in range(2):
                            act.wait_ge(qk_turned, 2 * j + m + 1)
                            if j >= 2:
                                act.wait_ge(scored, 2 * GB * (j - 1))
                            act.copy(turned_qk[:, j % 2, m, :], banks[:, 4 + m, :]).then_inc(qk_copied, 1)

                    def exp(h):
                        for b in range(GB):
                            act.wait_ge(scored, GB * h + b + 1)
                            if h >= 2:
                                act.wait_ge(summed, h - 1)
                            act.activation(probs[:, h % 2, b, :], banks[:, 2 * (h % 2) + b, :], ACT.Exp,
                                           bias=npeak[:, h:h + 1], scale=peak[:, h:h + 1]).then_inc(exped, 1)

                    for i in range(H + 1):
                        if i % 2 == 0 and i < H:
                            copy_qk(i // 2)
                        if i >= 1:
                            exp(i - 1)

                @block.gpsimd
                def _(pool):
                    pool.wait_ge(scaled, 1)
                    pool.wait_ge(copied, QK)
                    for u in range(POOL_UNITS):
                        a = raw[:, u // GT, u % GT, :].rearrange("p (h d) -> p h d", d=HD)
                        pool.tensor_tensor(a, a, spread(inv[:, u // GT, u % GT, :], HD), ALU.mult).then_inc(unit_g, 1)

                @block.vector
                def _(dve):
                    ln.vector(dve, xg)

                    def reduce(n):
                        t, m, half = n // 4, n // 2 % 2, n % 2
                        dve.wait_ge(squared, n + 1)
                        dve.tensor_reduce(ss[:, m, t, half * PAIRS:(half + 1) * PAIRS],
                                          sq[:, n % 2, :].rearrange("p (h d) -> p h d", d=HD), AX_X, ALU.add)\
                            .then_inc(reduced, 1)

                    for n in range(QK):
                        t, m, half = n // 4, n // 2 % 2, n % 2
                        dve.wait_ge(projected, n + 1)
                        dve.tensor_copy(raw[:, m, t, half * HALF:(half + 1) * HALF], banks[:, n % 4, :]).then_inc(copied, 1)
                        if n:
                            reduce(n - 1)
                    reduce(QK - 1)
                    dve.wait_ge(reduced, QK)
                    dve.tensor_scalar(ss[:], ss[:], 1e-24, UP, ALU.max, ALU.mult).then_inc(clamped, 1)
                    dve.wait_ge(rooted, 1)
                    dve.tensor_scalar(inv[:], inv[:], UP ** 0.5, None, ALU.mult).then_inc(scaled, 1)
                    dve.wait_ge(scaled, 1)
                    dve.wait_ge(copied, QK)
                    for u in range(POOL_UNITS, 2 * GT):
                        a = raw[:, u // GT, u % GT, :].rearrange("p (h d) -> p h d", d=HD)
                        dve.tensor_tensor(a, a, spread(inv[:, u // GT, u % GT, :], HD), ALU.mult).then_inc(unit_v, 1)
                    for h in range(H):
                        dve.wait_ge(summed, h + 1)
                        o = banks[:, 6, 0:GT * (HD + 1)].rearrange("p (t e) -> p t e", e=HD + 1)
                        dve.reciprocal(rden[:, h % 2, :], o[:, :, HD]).then_inc(rden_ready, 1)
                        dve.wait_ge(rden_ready, h + 1)
                        if h >= 4:
                            dve.wait_ge(y_turned, h // 2 - 1)
                        dve.tensor_tensor(y[:, h // 2 % 2, :, h % 2 * HD:(h % 2 + 1) * HD], o[:, :, 0:HD], spread(rden[:, h % 2, :], HD),
                                          ALU.mult).then_inc(head_done, 1)
                        if h % 2:
                            j = h // 2
                            dve.wait_ge(y_turned, j + 1)
                            dve.tensor_copy(yT(j), banks[:, 7, :].rearrange("p (t d) -> p t d", d=D)).then_inc(y_copied, 1)
                    dve.wait_ge(out_ready, 1)
                    dve.tensor_tensor(xg, xg, banks[:, 4, :].rearrange("p (t d) -> p t d", d=D), ALU.add)\
                        .then_inc(added, 1)
            restart(nc, sems)


def int4_linear(nc, x, banks, consts, w):
    RANK, QMAX = 16, 7.0
    ROUND = 1.5 * 2.0 ** 23
    with ExitStack() as ctx:
        sb = lambda n, s: ctx.enter_context(nc.sbuf_tensor("int4_" + n, s, F32))
        ln = LayerNorm(nc, ctx, consts, banks[:, 2, :], "int4_ln")
        rowmax, allmax, step, rstep = sb("rowmax", [P, 1]), sb("allmax", [P, 1]), sb("step", [P, 1]), sb("rstep", [P, 1])
        wq, low = sb("wq", [P, D]), sb("low", [RANK, GN])
        quant, quant_max = signals(nc, ctx, "quant_steps quant_max")
        sems = signals(nc, ctx, "low_ready low_copied out_ready added")
        low_ready, low_copied, out_ready, added = sems
        sems = ln.sems + [quant, quant_max] + sems

        with nc.Block() as block:
            @block.sync
            def _(sp):
                sp.wait_ge(w["loaded"], w["total"])
        with nc.Block() as block:
            @block.vector
            def _(dve):
                dve.tensor_reduce(rowmax[:], w["kernel"][:], AX_X, ALU.max, apply_absolute_value=True).then_inc(quant, 1)
                dve.wait_ge(quant_max, 1)
                dve.tensor_scalar(step[:], allmax[:], 1.0 / QMAX, None, ALU.mult).then_inc(quant, 1)
                dve.wait_ge(quant, 2)
                dve.reciprocal(rstep[:], step[:]).then_inc(quant, 1)
                dve.wait_ge(quant, 3)
                dve.tensor_scalar(wq[:], w["kernel"][:], rstep[:], None, ALU.mult).then_inc(quant, 1)
                dve.wait_ge(quant, 4)
                dve.tensor_scalar(wq[:], wq[:], ROUND, None, ALU.add).then_inc(quant, 1)
                dve.wait_ge(quant, 5)
                dve.tensor_scalar(wq[:], wq[:], -ROUND, None, ALU.add).then_inc(quant, 1)
                dve.wait_ge(quant, 6)
                dve.tensor_scalar(wq[:], wq[:], -8.0, 7.0, ALU.max, ALU.min).then_inc(quant, 1)
                dve.wait_ge(quant, 7)
                dve.tensor_scalar(wq[:], wq[:], step[:], None, ALU.mult).then_inc(quant, 1)

            @block.gpsimd
            def _(pool):
                pool.wait_ge(quant, 1)
                pool.partition_all_reduce(allmax[:], rowmax[:], P, bass.bass_isa.ReduceOp.max).then_inc(quant_max, 1)

            @block.scalar
            def _(act):
                act.preload_act_table_set(EXP_LN)
        restart(nc, sems)

        with nc.Fori(0, GROUPS) as g:
            xg = x[:, bass.ds(g * GT, GT), :]
            with nc.Block() as block:
                @block.tensor
                def _(pe):
                    ln.tensor(pe)
                    pe.wait_ge(ln.ready, 1)
                    pe.matmul(banks[0:RANK, 0, :], w["a"][:], ln.xnT[:], start=True, stop=True).then_inc(low_ready, 1)
                    pe.wait_ge(low_copied, 1)
                    for t in range(GT):
                        o, c = banks[:, 1, t * P:(t + 1) * P], slice(t * P, (t + 1) * P)
                        pe.matmul(o, ln.xnT[:, c], wq[:], start=True, stop=False)
                        pe.matmul(o, low[:, c], w["b"][:], start=False, stop=False)
                        last = pe.matmul(o, consts["ones"][0:1, 0:P], w["bias"][:], start=False, stop=True)
                    last.then_inc(out_ready, 1)

                @block.scalar
                def _(act):
                    ln.scalar(act)
                    act.wait_ge(low_ready, 1)
                    act.copy(low[:], banks[0:RANK, 0, :]).then_inc(low_copied, 1)

                @block.vector
                def _(dve):
                    ln.vector(dve, xg)
                    dve.wait_ge(out_ready, 1)
                    dve.tensor_tensor(xg, xg, banks[:, 1, :].rearrange("p (t d) -> p t d", d=D), ALU.add)\
                        .then_inc(added, 1)
            restart(nc, sems)


def state_space(nc, x, banks, consts, w):
    INNER_D, NS, RANK = 256, 16, 8
    CH = INNER_D // P
    with ExitStack() as ctx:
        sb = lambda n, s: ctx.enter_context(nc.sbuf_tensor("mamba_" + n, s, F32))
        ln = LayerNorm(nc, ctx, consts, banks[:, 7, :], "mamba_ln")
        a_neg = sb("a_neg", [P, CH, NS])
        xs, gate = sb("xs", [P, CH, GN]), sb("gate", [P, CH, GN])
        dp, bs, cs = sb("dp", [RANK, GN]), sb("bs", [NS, GN]), sb("cs", [NS, GN])
        v, mag, delta, dx = (sb(n, [P, CH, GN]) for n in ("dt_in", "dt_mag", "delta", "dx"))
        decay, drive, state, seen = (sb(n, [P, 2, CH, GN]) for n in ("decay", "drive", "state", "seen"))
        c_wide = sb("c_wide", [P, 2, GN])
        yT = sb("yT", [P, CH, GN])
        prep = signals(nc, ctx, "prep")[0]
        sems = signals(nc, ctx, "widened xs_ready gate_ready lowered low_biased dt_ready dt_biased mag_ready mag_exp "
                                "mag_log delta_ready dx_ready b_spread c_spread c_copied decayed driven scanned "
                                "read_out gathered skip_added gated out_ready added")
        (widened, xs_ready, gate_ready, lowered, low_biased, dt_ready, dt_biased, mag_ready, mag_exp, mag_log,
         delta_ready, dx_ready, b_spread, c_spread, c_copied, decayed, driven, scanned, read_out, gathered, skip_added,
         gated, out_ready, added) = sems
        sems = ln.sems + [prep] + sems

        with nc.Block() as block:
            @block.sync
            def _(sp):
                sp.wait_ge(w["loaded"], w["total"])
        with nc.Block() as block:
            @block.scalar
            def _(act):
                act.preload_act_table_set(EXP_LN)
                act.activation(a_neg[:], w["A_log"][:], ACT.Exp).then_inc(prep, 1)

            @block.vector
            def _(dve):
                dve.wait_ge(prep, 1)
                dve.tensor_scalar(a_neg[:], a_neg[:], -1.0, None, ALU.mult).then_inc(prep, 1)
                for r in range(2):
                    for c in range(CH):
                        for b in range(GB):
                            dve.memset(decay[:, r, c, b * SEQ:b * SEQ + 1], 0.0)
        restart(nc, sems)

        with nc.Fori(0, GROUPS) as g:
            xg = x[:, bass.ds(g * GT, GT), :]
            with nc.Block() as block:
                @block.tensor
                def _(pe):
                    ln.tensor(pe)
                    pe.wait_ge(ln.ready, 1)
                    for c in range(2 * CH):
                        pe.matmul(banks[:, c, :], w["Win"][:, c * P:(c + 1) * P], ln.xnT[:], start=True, stop=True)\
                            .then_inc(widened, 1)
                    pe.wait_ge(xs_ready, CH)
                    for n, (lo, m) in enumerate(((0, RANK), (RANK, NS), (RANK + NS, NS))):
                        for c in range(CH):
                            last = pe.matmul(banks[0:m, 4 + n, :], w["Wx"][:, c, lo:lo + m], xs[:, c, :],
                                             start=(c == 0), stop=(c == CH - 1))
                        last.then_inc(lowered, 1)
                    pe.wait_ge(low_biased, 1)
                    for c in range(CH):
                        pe.matmul(banks[:, c, :], w["Wdt"][:, c * P:(c + 1) * P], dp[:], start=True, stop=True)\
                            .then_inc(dt_ready, 1)
                    pe.wait_ge(low_biased, 3)
                    pe.wait_ge(gate_ready, CH)

                    def gather(n):
                        pe.wait_ge(read_out, n + 1)
                        for c in range(CH):
                            last = pe.matmul(banks[:, 6 + c, :], consts["ident"], seen[:, n % 2, c, :],
                                             start=(n == 0), stop=(n == NS - 1))
                        last.then_inc(gathered, 1)

                    for n in range(NS):
                        pick = consts["pick"][:, n * P:(n + 1) * P]
                        if n >= 2:
                            pe.wait_ge(driven, n - 1)
                        pe.matmul(banks[:, 2 + n % 2, :], pick, bs[:], start=True, stop=True).then_inc(b_spread, 1)
                        if n >= 2:
                            pe.wait_ge(c_copied, n - 1)
                        pe.matmul(banks[:, 4 + n % 2, :], pick, cs[:], start=True, stop=True).then_inc(c_spread, 1)
                        if n:
                            gather(n - 1)
                    gather(NS - 1)
                    pe.wait_ge(gated, CH)
                    for t in range(GT):
                        o = banks[:, 0, t * P:(t + 1) * P]
                        for c in range(CH):
                            pe.matmul(o, yT[:, c, t * P:(t + 1) * P], w["Wout"][:, c, :], start=(c == 0), stop=False)
                        last = pe.matmul(o, consts["ones"][0:1, 0:P], w["bout"][:], start=False, stop=True)
                    last.then_inc(out_ready, 1)

                @block.scalar
                def _(act):
                    act.preload_act_table_set(EXP_LN)
                    ln.scalar(act)
                    for c in range(CH):
                        act.wait_ge(widened, c + 1)
                        act.activation(xs[:, c, :], banks[:, c, :], ACT.Silu, bias=w["bin"][:, c:c + 1]).then_inc(xs_ready, 1)
                    for c in range(CH):
                        act.wait_ge(widened, CH + c + 1)
                        act.activation(gate[:, c, :], banks[:, CH + c, :], ACT.Silu, bias=w["bin"][:, CH + c:CH + c + 1])\
                            .then_inc(gate_ready, 1)
                    act.preload_act_table_set(EXP_LN)
                    act.wait_ge(dt_biased, CH)
                    act.activation(mag[:], v[:], ACT.Abs).then_inc(mag_ready, 1)
                    act.wait_ge(mag_ready, 1)
                    act.activation(mag[:], mag[:], ACT.Exp, scale=-1.0).then_inc(mag_exp, 1)
                    act.wait_ge(mag_exp, 1)
                    act.activation(mag[:], mag[:], ACT.Ln, bias=1.0).then_inc(mag_log, 1)
                    act.wait_ge(delta_ready, 1)
                    for n in range(NS):
                        if n >= 2:
                            act.wait_ge(scanned, CH * (n - 1))
                        for c in range(CH):
                            into = decay[:, n % 2, c, :].rearrange("p (b s) -> p b s", s=SEQ)[:, :, 1:]
                            act.activation(into, delta[:, c, :].rearrange("p (b s) -> p b s", s=SEQ)[:, :, 1:], ACT.Exp,
                                           scale=a_neg[:, c, n:n + 1]).then_inc(decayed, 1)
                        act.wait_ge(c_spread, n + 1)
                        if n >= 2:
                            act.wait_ge(read_out, n - 1)
                        act.copy(c_wide[:, n % 2, :], banks[:, 4 + n % 2, :]).then_inc(c_copied, 1)

                @block.gpsimd
                def _(pool):
                    for n in range(NS):
                        pool.wait_ge(scanned, CH * (n + 1))
                        pool.wait_ge(c_copied, n + 1)
                        if n >= 2:
                            pool.wait_ge(gathered, n - 1)
                        pool.tensor_tensor(seen[:, n % 2, :, :], state[:, n % 2, :, :],
                                           c_wide[:, n % 2:n % 2 + 1, :].broadcast_to([P, CH, GN]), ALU.mult)\
                            .then_inc(read_out, 1)

                @block.vector
                def _(dve):
                    ln.vector(dve, xg)
                    for n, (into, bias) in enumerate(((dp, "bdp"), (bs, "bB"), (cs, "bC"))):
                        dve.wait_ge(lowered, n + 1)
                        m = into.shape[0]
                        dve.tensor_scalar(into[:], banks[0:m, 4 + n, :], w[bias][:], None, ALU.add).then_inc(low_biased, 1)
                    for c in range(CH):
                        dve.wait_ge(dt_ready, c + 1)
                        dve.tensor_scalar(v[:, c, :], banks[:, c, :], w["bdt"][:, c:c + 1], None, ALU.add).then_inc(dt_biased, 1)
                    dve.wait_ge(dt_biased, CH)
                    dve.wait_ge(mag_log, 1)
                    dve.scalar_tensor_tensor(delta[:], v[:], 0.0, mag[:], ALU.max, ALU.add).then_inc(delta_ready, 1)
                    dve.wait_ge(delta_ready, 1)
                    dve.wait_ge(xs_ready, CH)
                    dve.tensor_tensor(dx[:], delta[:], xs[:], ALU.mult).then_inc(dx_ready, 1)
                    dve.wait_ge(dx_ready, 1)
                    for n in range(NS):
                        if n >= 2:
                            dve.wait_ge(scanned, CH * (n - 1))
                        dve.wait_ge(b_spread, n + 1)
                        dve.tensor_tensor(drive[:, n % 2, :, :], dx[:],
                                          banks[:, 2 + n % 2:3 + n % 2, :].broadcast_to([P, CH, GN]), ALU.mult)\
                            .then_inc(driven, 1)
                        dve.wait_ge(driven, n + 1)
                        if n >= 2:
                            dve.wait_ge(read_out, n - 1)
                        for c in range(CH):
                            dve.wait_ge(decayed, CH * n + c + 1)
                            dve.tensor_tensor_scan(state[:, n % 2, c, :], decay[:, n % 2, c, :], drive[:, n % 2, c, :],
                                                   0.0, ALU.mult, ALU.add).then_inc(scanned, 1)
                    dve.wait_ge(gathered, NS)
                    for c in range(CH):
                        dve.scalar_tensor_tensor(yT[:, c, :], xs[:, c, :], w["Dp"][:, c:c + 1], banks[:, 6 + c, :],
                                                 ALU.mult, ALU.add).then_inc(skip_added, 1)
                        dve.wait_ge(skip_added, c + 1)
                        dve.tensor_tensor(yT[:, c, :], yT[:, c, :], gate[:, c, :], ALU.mult).then_inc(gated, 1)
                    dve.wait_ge(out_ready, 1)
                    dve.tensor_tensor(xg, xg, banks[:, 0, :].rearrange("p (t d) -> p t d", d=D), ALU.add)\
                        .then_inc(added, 1)
            restart(nc, sems)


def expert_ffn(nc, x, banks, consts, w):
    E, TOP, DFF, EPS = 8, 2, 512, 1e-8
    CH = DFF // P
    with ExitStack() as ctx:
        sb = lambda n, s, d=F32: ctx.enter_context(nc.sbuf_tensor("experts_" + n, s, d))
        ln = LayerNorm(nc, ctx, consts, banks[:, 7, :], "experts_ln")
        ln2 = LayerNorm(nc, ctx, consts, banks[:, 7, :], "experts_ln2")
        hT = sb("hT", [P, 2, CH, GN])
        peak, z, mass, rmass, prob = sb("peak", [P, GT]), sb("z", [P, GT, E]), sb("mass", [P, GT]), sb("rmass", [P, GT]), sb("prob", [P, GT, E])
        top, place, placef = sb("top", [P, GT, 8]), sb("place", [P, GT, 8], U32), sb("placef", [P, GT, 8])
        pair, rpair, share = sb("pair", [P, GT]), sb("rpair", [P, GT]), sb("share", [P, GT, TOP])
        part, weight, weightT = sb("part", [P, TOP, GT, E]), sb("weight", [P, GT, E]), sb("weightT", [E, GN])
        acc = sb("acc", [P, GT, D])
        sems = signals(nc, ctx, "logits peak_ready centred exped mass_ready rmass_ready prob_ready top_ready placed "
                                "place_copied pair_sum pair_eps rpair_ready share_ready parted weighted w_turned "
                                "w_copied bias_ready acc_ready widened gelu_done narrowed taken scaled_out shifted added")
        (logits, peak_ready, centred, exped, mass_ready, rmass_ready, prob_ready, top_ready, placed, place_copied,
         pair_sum, pair_eps, rpair_ready, share_ready, parted, weighted, w_turned, w_copied, bias_ready, acc_ready,
         widened, gelu_done, narrowed, taken, scaled_out, shifted, added) = sems
        sems = ln.sems + ln2.sems + sems

        with nc.Block() as block:
            @block.sync
            def _(sp):
                sp.wait_ge(w["loaded"], w["total"])

        with nc.Fori(0, GROUPS) as g:
            xg = x[:, bass.ds(g * GT, GT), :]
            with nc.Block() as block:
                @block.tensor
                def _(pe):
                    ln.tensor(pe)
                    pe.wait_ge(ln.ready, 1)
                    for t in range(GT):
                        o = banks[:, 2, t * E:(t + 1) * E]
                        pe.matmul(o, ln.xnT[:, t * P:(t + 1) * P], w["Wg"][:], start=True, stop=False)
                        last = pe.matmul(o, consts["ones"][0:1, 0:P], w["bg"][:], start=False, stop=True)
                    last.then_inc(logits, 1)

                    def widen(e):
                        for c in range(CH):
                            n = e * CH + c
                            if n >= 2:
                                pe.wait_ge(gelu_done, n - 1)
                            pe.matmul(banks[:, n % 2, :], w["W1"][:, e, c * P:(c + 1) * P], ln.xnT[:], start=True,
                                      stop=True).then_inc(widened, 1)

                    def narrow(e):
                        pe.wait_ge(gelu_done, (e + 1) * CH)
                        if e >= 2:
                            pe.wait_ge(taken, GT * (e - 1))
                        for t in range(GT):
                            for c in range(CH):
                                last = pe.matmul(banks[:, 4 + e % 2, t * P:(t + 1) * P],
                                                 hT[:, e % 2, c, t * P:(t + 1) * P], w["W2"][:, e, c, :],
                                                 start=(c == 0), stop=(c == CH - 1))
                        last.then_inc(narrowed, 1)

                    for i in range(E + 1):
                        if i < E:
                            widen(i)
                        if i == 1:
                            pe.wait_ge(weighted, 1)
                            for t in range(GT):
                                last = pe.transpose(banks[0:E, 3, t * P:(t + 1) * P], weight[:, t, :], consts["ident"])
                            last.then_inc(w_turned, 1)
                            pe.wait_ge(w_copied, 1)
                            for t in range(GT):
                                last = pe.matmul(banks[:, 6, t * P:(t + 1) * P], weightT[:, t * P:(t + 1) * P],
                                                 w["b2"][:], start=True, stop=True)
                            last.then_inc(bias_ready, 1)
                        if i:
                            narrow(i - 1)

                @block.scalar
                def _(act):
                    act.preload_act_table_set(EXP_LN)
                    ln.scalar(act)
                    act.wait_ge(centred, 1)
                    act.activation(z[:], z[:], ACT.Exp).then_inc(exped, 1)
                    for n in range(E * CH):
                        e, c = n // CH, n % CH
                        act.wait_ge(widened, n + 1)
                        if e >= 2:
                            act.wait_ge(narrowed, e - 1)
                        act.activation(hT[:, e % 2, c, :], banks[:, n % 2, :], ACT.Gelu, bias=w["b1"][:, n:n + 1])\
                            .then_inc(gelu_done, 1)
                    act.preload_act_table_set(EXP_LN)
                    ln2.scalar(act, copy=False)

                @block.vector
                def _(dve):
                    ln.vector(dve, xg)
                    dve.wait_ge(logits, 1)
                    lo = banks[:, 2, 0:GT * E].rearrange("p (t e) -> p t e", e=E)
                    dve.tensor_reduce(peak[:], lo, AX_X, ALU.max).then_inc(peak_ready, 1)
                    dve.wait_ge(peak_ready, 1)
                    dve.tensor_tensor(z[:], lo, spread(peak[:], E), ALU.subtract).then_inc(centred, 1)
                    dve.wait_ge(exped, 1)
                    dve.tensor_reduce(mass[:], z[:], AX_X, ALU.add).then_inc(mass_ready, 1)
                    dve.wait_ge(mass_ready, 1)
                    dve.reciprocal(rmass[:], mass[:]).then_inc(rmass_ready, 1)
                    dve.wait_ge(rmass_ready, 1)
                    dve.tensor_tensor(prob[:], z[:], spread(rmass[:], E), ALU.mult).then_inc(prob_ready, 1)
                    dve.wait_ge(prob_ready, 1)
                    for t in range(GT):
                        dve.max(top[:, t, :], prob[:, t, :]).then_inc(top_ready, 1)
                    dve.wait_ge(top_ready, GT)
                    for t in range(GT):
                        dve.max_index(place[:, t, :], top[:, t, :], prob[:, t, :]).then_inc(placed, 1)
                    dve.tensor_reduce(pair[:], top[:, :, 0:TOP], AX_X, ALU.add).then_inc(pair_sum, 1)
                    dve.wait_ge(placed, GT)
                    dve.tensor_copy(placef[:], place[:]).then_inc(place_copied, 1)
                    dve.wait_ge(pair_sum, 1)
                    dve.tensor_scalar(pair[:], pair[:], EPS, None, ALU.add).then_inc(pair_eps, 1)
                    dve.wait_ge(pair_eps, 1)
                    dve.reciprocal(rpair[:], pair[:]).then_inc(rpair_ready, 1)
                    dve.wait_ge(rpair_ready, 1)
                    dve.tensor_tensor(share[:], top[:, :, 0:TOP], spread(rpair[:], TOP), ALU.mult).then_inc(share_ready, 1)
                    dve.wait_ge(share_ready, 1)
                    dve.wait_ge(place_copied, 1)
                    for r in range(TOP):
                        for t in range(GT):
                            dve.tensor_scalar(part[:, r, t, :], consts["count"], placef[:, t, r:r + 1],
                                              share[:, t, r:r + 1], ALU.is_equal, ALU.mult).then_inc(parted, 1)
                    dve.wait_ge(parted, TOP * GT)
                    dve.tensor_tensor(weight[:], part[:, 0, :, :], part[:, 1, :, :], ALU.add).then_inc(weighted, 1)
                    dve.wait_ge(w_turned, 1)
                    dve.tensor_copy(weightT[:], banks[0:E, 3, :]).then_inc(w_copied, 1)
                    dve.wait_ge(bias_ready, 1)
                    dve.tensor_copy(acc[:], banks[:, 6, :].rearrange("p (t d) -> p t d", d=D)).then_inc(acc_ready, 1)
                    dve.wait_ge(acc_ready, 1)
                    for e in range(E):
                        dve.wait_ge(narrowed, e + 1)
                        if e:
                            dve.wait_ge(taken, GT * e)
                        for t in range(GT):
                            dve.scalar_tensor_tensor(acc[:, t, :], banks[:, 4 + e % 2, t * P:(t + 1) * P],
                                                     weight[:, t, e:e + 1], acc[:, t, :], ALU.mult, ALU.add)\
                                .then_inc(taken, 1)
                    dve.wait_ge(taken, GT * E)
                    ln2.vector(dve, acc)
                    dve.wait_ge(ln2.normed, GT)
                    dve.tensor_tensor(acc[:], ln2.xn[:], w["gamma"][:].unsqueeze(1).broadcast_to([P, GT, D]), ALU.mult)\
                        .then_inc(scaled_out, 1)
                    dve.wait_ge(scaled_out, 1)
                    dve.tensor_tensor(acc[:], acc[:], w["beta"][:].unsqueeze(1).broadcast_to([P, GT, D]), ALU.add)\
                        .then_inc(shifted, 1)
                    dve.wait_ge(shifted, 1)
                    dve.tensor_tensor(xg, xg, acc[:], ALU.add).then_inc(added, 1)
            restart(nc, sems)


def gated_recurrence(nc, x, banks, consts, w):
    HEADS, HW, CHUNK, EPS = 2, 64, 64, 1e-5
    NC = GN // CHUNK
    SC = NC // GB
    with ExitStack() as ctx:
        sb = lambda n, s: ctx.enter_context(nc.sbuf_tensor("hgrn_" + n, s, F32))
        ln = LayerNorm(nc, ctx, consts, banks[:, 7, :], "hgrn_ln")
        ndelta = sb("ndelta", [P, 1])
        q, k, z, mag, logf, G = (sb("" + n, [P, GN]) for n in ("q", "k", "z", "mag", "logf", "G"))
        eG, enG = sb("eG", [P, GN]), sb("enG", [P, GN])
        low, sgate = sb("low", [HW, GN]), sb("sgate", [CHUNK, NC, D])
        vals, keys = sb("vals", [CHUNK, NC, D]), sb("keys", [CHUNK, NC, D])
        att = sb("att", [CHUNK, HEADS, NC, CHUNK])
        kv, S = sb("kv", [P, NC, D]), sb("S", [P, NC, D])
        o, osq, ms, lms, rms = sb("o", [CHUNK, NC, D]), sb("osq", [CHUNK, NC, D]), sb("ms", [CHUNK, NC * HEADS]), sb("lms", [CHUNK, NC * HEADS]), sb("rms", [CHUNK, NC * HEADS])
        oT = sb("oT", [P, GN])
        prep = signals(nc, ctx, "prep")[0]
        sems = signals(nc, ctx, "projected q_silu k_sigmoid z_biased low_copied v_ready v_copied gates gate_ready "
                                "mag_ready mag_exp mag_log logf_ready G_ready eG_ready enG_ready q_ready k_ready "
                                "keys_turned keys_copied att_ready att_masked kv_ready kv_scaled S_ready o_ready "
                                "o_gated o_squared ms_ready ms_eps ms_log rms_ready o_normed o_turned oT_ready "
                                "out_ready added")
        (projected, q_silu, k_sigmoid, z_biased, low_copied, v_ready, v_copied, gates, gate_ready, mag_ready, mag_exp,
         mag_log, logf_ready, G_ready, eG_ready, enG_ready, q_ready, k_ready, keys_turned, keys_copied, att_ready,
         att_masked, kv_ready, kv_scaled, S_ready, o_ready, o_gated, o_squared, ms_ready, ms_eps, ms_log, rms_ready,
         o_normed, o_turned, oT_ready, out_ready, added) = sems
        sems = ln.sems + [prep] + sems
        ch = lambda c: slice(c * CHUNK, (c + 1) * CHUNK)
        at = lambda first, c: banks[0:CHUNK, first + c // 4, (c % 4) * D:(c % 4 + 1) * D]
        both = lambda first: banks[0:CHUNK, first:first + 2, :].rearrange("p a (c d) -> p (a c) d", d=D)

        with nc.Block() as block:
            @block.sync
            def _(sp):
                sp.wait_ge(w["loaded"], w["total"])
        with nc.Block() as block:
            @block.vector
            def _(dve):
                dve.tensor_scalar(ndelta[:], w["delta"][:], -1.0, None, ALU.mult)

        with nc.Fori(0, GROUPS) as g:
            xg = x[:, bass.ds(g * GT, GT), :]
            with nc.Block() as block:
                @block.tensor
                def _(pe):
                    ln.tensor(pe)
                    pe.wait_ge(ln.ready, 1)
                    for n, name in enumerate(("Wk", "Wq", "G1")):
                        m = w[name].shape[1]
                        pe.matmul(banks[0:m, n, :], w[name][:], ln.xnT[:], start=True, stop=True).then_inc(projected, 1)
                    for c in range(NC):
                        last = pe.matmul(at(3, c), ln.xnT[:, ch(c)], w["Wv"][:], start=True, stop=True)
                    last.then_inc(v_ready, 1)
                    pe.wait_ge(low_copied, 1)
                    for c in range(NC):
                        last = pe.matmul(at(5, c), low[:, ch(c)], w["G2"][:], start=True, stop=True)
                    last.then_inc(gates, 1)
                    pe.wait_ge(k_ready, 1)
                    pe.wait_ge(q_ready, 1)
                    for c in range(NC):
                        for h in range(HEADS):
                            r = slice(h * HW, (h + 1) * HW)
                            last = pe.matmul(banks[0:CHUNK, 1 + h, ch(c)], k[r, ch(c)], q[r, ch(c)], start=True, stop=True)
                    last.then_inc(att_ready, 1)
                    pe.wait_ge(v_copied, 1)
                    for c in range(NC):
                        last = pe.transpose(at(3, c), k[:, ch(c)], consts["ident"])
                    last.then_inc(keys_turned, 1)
                    pe.wait_ge(keys_copied, 1)
                    for c in range(NC):
                        last = pe.matmul(banks[:, 3 + c // 4, (c % 4) * D:(c % 4 + 1) * D], keys[:, c, :], vals[:, c, :],
                                         start=True, stop=True)
                    last.then_inc(kv_ready, 1)
                    pe.wait_ge(gate_ready, 1)
                    pe.wait_ge(att_masked, HEADS)
                    for i in range(SC):
                        if i:
                            pe.wait_ge(S_ready, GB * i)
                        for b in range(GB):
                            c = b * SC + i
                            if i:
                                pe.matmul(at(5, c), q[:, ch(c)], S[:, c, :], start=True, stop=False)
                            for h in range(HEADS):
                                last = pe.matmul(at(5, c)[:, h * HW:(h + 1) * HW], att[:, h, c, :],
                                                 vals[:, c, h * HW:(h + 1) * HW], start=(i == 0), stop=(i == 0 or h == HEADS - 1))
                    last.then_inc(o_ready, 1)
                    pe.wait_ge(o_normed, 1)
                    for c in range(NC):
                        last = pe.transpose(banks[:, 7, ch(c)], o[:, c, :], consts["ident"][0:CHUNK, 0:CHUNK])
                    last.then_inc(o_turned, 1)
                    pe.wait_ge(oT_ready, 1)
                    for t in range(GT):
                        last = pe.matmul(banks[:, 0, t * P:(t + 1) * P], oT[:, t * P:(t + 1) * P], w["Wo"][:],
                                         start=True, stop=True)
                    last.then_inc(out_ready, 1)

                @block.scalar
                def _(act):
                    act.preload_act_table_set(EXP_LN)
                    ln.scalar(act)
                    act.wait_ge(z_biased, 1)
                    act.activation(mag[:], z[:], ACT.Abs).then_inc(mag_ready, 1)
                    act.wait_ge(mag_ready, 1)
                    act.activation(mag[:], mag[:], ACT.Exp, scale=-1.0).then_inc(mag_exp, 1)
                    act.wait_ge(mag_exp, 1)
                    act.activation(mag[:], mag[:], ACT.Ln, bias=1.0).then_inc(mag_log, 1)
                    act.wait_ge(G_ready, 1)
                    act.activation(eG[:], G[:], ACT.Exp).then_inc(eG_ready, 1)
                    act.activation(enG[:], G[:], ACT.Exp, scale=-1.0).then_inc(enG_ready, 1)
                    act.activation(k[:], z[:], ACT.Sigmoid, scale=-1.0).then_inc(k_sigmoid, 1)
                    act.wait_ge(gates, 1)
                    act.activation(sgate[:], both(5), ACT.Sigmoid).then_inc(gate_ready, 1)
                    act.wait_ge(projected, 2)
                    act.activation(q[:], banks[:, 1, :], ACT.Silu).then_inc(q_silu, 1)
                    act.preload_act_table_set(EXP_LN)
                    act.wait_ge(keys_turned, 1)
                    act.copy(keys[:], both(3)).then_inc(keys_copied, 1)
                    act.wait_ge(o_gated, 1)
                    act.activation(osq[:], o[:], ACT.Square).then_inc(o_squared, 1)
                    act.wait_ge(ms_eps, 1)
                    act.activation(lms[:], ms[:], ACT.Ln).then_inc(ms_log, 1)
                    act.wait_ge(ms_log, 1)
                    act.activation(rms[:], lms[:], ACT.Exp, scale=-0.5).then_inc(rms_ready, 1)
                    act.wait_ge(o_turned, 1)
                    act.activation(oT[:], banks[:, 7, :], ACT.Copy, scale=w["norm_w"][:]).then_inc(oT_ready, 1)

                @block.vector
                def _(dve):
                    ln.vector(dve, xg)
                    dve.wait_ge(projected, 1)
                    dve.tensor_scalar(z[:], banks[:, 0, :], w["delta"][:], None, ALU.add).then_inc(z_biased, 1)
                    dve.wait_ge(projected, 3)
                    dve.tensor_copy(low[:], banks[0:HW, 2, :]).then_inc(low_copied, 1)
                    dve.wait_ge(v_ready, 1)
                    dve.tensor_copy(vals[:], both(3)).then_inc(v_copied, 1)
                    dve.wait_ge(z_biased, 1)
                    dve.wait_ge(mag_log, 1)
                    dve.scalar_tensor_tensor(logf[:], z[:], 0.0, mag[:], ALU.min, ALU.subtract).then_inc(logf_ready, 1)
                    dve.wait_ge(logf_ready, 1)
                    dve.tensor_tensor_scan(G[:], consts["inside"], logf[:], 0.0, ALU.mult, ALU.add).then_inc(G_ready, 1)
                    dve.wait_ge(enG_ready, 1)
                    dve.wait_ge(k_sigmoid, 1)
                    dve.tensor_tensor(k[:], k[:], enG[:], ALU.mult).then_inc(k_ready, 1)
                    dve.wait_ge(eG_ready, 1)
                    dve.wait_ge(q_silu, 1)
                    dve.tensor_tensor(q[:], q[:], eG[:], ALU.mult).then_inc(q_ready, 1)
                    dve.wait_ge(att_ready, 1)
                    for h in range(HEADS):
                        dve.tensor_tensor(att[:, h, :, :], banks[0:CHUNK, 1 + h, :].rearrange("p (c t) -> p c t", t=CHUNK),
                                          consts["causal"][0:CHUNK, 0:CHUNK].unsqueeze(1).broadcast_to([CHUNK, NC, CHUNK]),
                                          ALU.mult).then_inc(att_masked, 1)
                    dve.wait_ge(kv_ready, 1)
                    end = lambda c: eG[:, (c + 1) * CHUNK - 1:(c + 1) * CHUNK]
                    into = lambda c: (S[:, c + 1, :] if c % SC == 0 else kv[:, c, :])
                    for b in range(GB):
                        for i in range(SC - 1):
                            c = b * SC + i
                            dve.scalar_tensor_tensor(into(c), banks[:, 3 + c // 4, (c % 4) * D:(c % 4 + 1) * D], end(c),
                                                     consts["blocks"], ALU.mult, ALU.mult).then_inc(kv_scaled, 1)
                    dve.wait_ge(kv_scaled, GB * (SC - 1))
                    dve.engine_nop().then_inc(S_ready, GB)
                    for i in range(1, SC - 1):
                        if i > 1:
                            dve.wait_ge(S_ready, GB * i)
                        for b in range(GB):
                            c = b * SC + i
                            dve.scalar_tensor_tensor(S[:, c + 1, :], S[:, c, :], end(c), kv[:, c, :], ALU.mult, ALU.add)\
                                .then_inc(S_ready, 1)
                    dve.wait_ge(o_ready, 1)
                    dve.wait_ge(gate_ready, 1)
                    dve.tensor_tensor(o[:], both(5), sgate[:], ALU.mult).then_inc(o_gated, 1)
                    dve.wait_ge(o_squared, 1)
                    dve.tensor_reduce(ms[:], osq[:].rearrange("p c (h d) -> p (c h) d", d=HW), AX_X, ALU.add).then_inc(ms_ready, 1)
                    dve.wait_ge(ms_ready, 1)
                    dve.tensor_scalar(ms[:], ms[:], 1.0 / HW, EPS, ALU.mult, ALU.add).then_inc(ms_eps, 1)
                    dve.wait_ge(rms_ready, 1)
                    oh = o[:].rearrange("p c (h d) -> p (c h) d", d=HW)
                    dve.tensor_tensor(oh, oh, spread(rms[:], HW), ALU.mult).then_inc(o_normed, 1)
                    dve.wait_ge(out_ready, 1)
                    dve.tensor_tensor(xg, xg, banks[:, 0, :].rearrange("p (t d) -> p t d", d=D), ALU.add)\
                        .then_inc(added, 1)
            restart(nc, sems)


def shift_tokens(pe, banks, consts, y, shifted):
    half = banks[:, 6, 0:GT * D // 2].rearrange("p (t d) -> p t d", d=D // 2)
    pe.matmul(half, consts["next"], y[:, :, D // 2:], start=True, stop=False)
    last = pe.matmul(half[:, 1::ST, :], consts["carry"], y[:, 0::ST, D // 2:], start=False, stop=True)
    last.then_inc(shifted, 1)


def band_attention(nc, y, banks, consts, w, tables, tmp):
    HALF, SCALE, UP = INNER // 2, 8.0, 2.0 ** 32
    BAND = P + WINDOW
    SCORES = BAND + P
    QK = 4 * GT
    ys, yT_in, raw, sq, swapped = tmp["ys"], tmp["ysT"], tmp["raw"], tmp["sq"], tmp["swapped"]
    ss, lg, inv, rot, turned_qk = tmp["ss"], tmp["lg"], tmp["inv"], tmp["rot"], tmp["turned_qk"]
    logit, probs, v1, rden, o = tmp["logit"], tmp["probs"], tmp["v1"], tmp["rden"], tmp["o"]
    oT = lambda j: rot[:, 0, :, j * P:(j + 1) * P]
    with ExitStack() as ctx:
        sems = signals(nc, ctx, "shifted low_half high_half in_turned in_ready projected copied squared reduced swap_done cosined "
                                "rotated clamped logged rooted scaled unit qk_turned qk_copied scored banded exped "
                                "summed rden_ready head_done v_copied o_turned o_copied out_ready added")
        (shifted, low_half, high_half, in_turned, in_ready, projected, copied, squared, reduced, swap_done, cosined, rotated,
         clamped, logged, rooted, scaled, unit, qk_turned, qk_copied, scored, banded, exped, summed, rden_ready, head_done,
         v_copied, o_turned, o_copied, out_ready, added) = sems
        where = lambda n: (n // 4, n // 2 % 2, n % 2)
        heads = lambda a: a.rearrange("p (h d) -> p h d", d=HD)

        with nc.Fori(0, GROUPS) as g:
            yg = y[:, bass.ds(g * GT, GT), :]
            with nc.Block() as block:
                @block.tensor
                def _(pe):
                    shift_tokens(pe, banks, consts, yg, shifted)
                    pe.wait_ge(low_half, 1)
                    pe.wait_ge(high_half, 1)
                    for t in range(GT):
                        last = pe.transpose(banks[:, 7, t * P:(t + 1) * P], ys[:, t, :], consts["ident"])
                    last.then_inc(in_turned, 1)
                    pe.wait_ge(in_ready, 1)
                    for n in range(QK + 2 * GT):
                        if 4 <= n < QK + 4:
                            pe.wait_ge(copied, n - 3)
                        elif n >= QK + 4:
                            pe.wait_ge(v_copied, n - QK - 3)
                        t, m, half = where(n) if n < QK else ((n - QK) // 2, 2, n % 2)
                        c = m * INNER + half * HALF
                        pe.matmul(banks[:, n % 4, :], yT_in[:, t * P:(t + 1) * P], w["Wqkv"][:, c:c + HALF],
                                  start=True, stop=True).then_inc(projected, 1)

                    def turn_qk(j):
                        pe.wait_ge(unit, QK)
                        if j:
                            pe.wait_ge(qk_copied, 2 * j)
                        for m in range(2):
                            for t in range(GT):
                                last = pe.transpose(banks[:, 4 + m, t * P:(t + 1) * P],
                                                    rot[:, m, t, j * P:(j + 1) * P], consts["ident"])
                            last.then_inc(qk_turned, 1)

                    def score(h):
                        pe.wait_ge(qk_copied, 2 * (h // 2) + 2)
                        if h == 0:
                            pe.wait_ge(v_copied, 2 * GT)
                        if h >= 2:
                            pe.wait_ge(banded, h - 1)
                        lo = HD * (h % 2)
                        q, k = (turned_qk[lo:lo + HD, h // 2 % 2, m, :] for m in range(2))
                        for b in range(GB):
                            c = b * SEQ
                            pe.matmul(banks[:, 2 * (h % 2) + b, 0:BAND], k[:, c:c + P], q[:, c:c + BAND],
                                      start=True, stop=True)
                            last = pe.matmul(banks[:, 2 * (h % 2) + b, BAND:SCORES], k[:, c + P:c + SEQ],
                                             q[:, c + P:c + SEQ], start=True, stop=True)
                        last.then_inc(scored, 1)

                    def values(h):
                        pe.wait_ge(exped, 2 * (h + 1))
                        if h:
                            pe.wait_ge(head_done, h)
                        for b in range(GB):
                            for i in range(ST):
                                out = banks[:, 6, (b * ST + i) * (HD + 1):(b * ST + i + 1) * (HD + 1)]
                                for j in range(i + 1):
                                    c = (i * P if j == 0 else SEQ)
                                    last = pe.matmul(out, probs[:, h % 2, b, c:c + P], v1[:, b * ST + j, h, :],
                                                     start=(j == 0), stop=(j == i))
                        last.then_inc(summed, 1)

                    def turn_o(j):
                        pe.wait_ge(head_done, 2 * j + 2)
                        if j:
                            pe.wait_ge(o_copied, j)
                        for t in range(GT):
                            last = pe.transpose(banks[:, 7, t * P:(t + 1) * P], o[:, j % 2, t, :],
                                                consts["ident"])
                        last.then_inc(o_turned, 1)

                    for i in range(H + 5):
                        if i % 2 == 0 and i < H:
                            turn_qk(i // 2)
                        if 1 <= i <= H:
                            score(i - 1)
                        if 3 <= i <= H + 2:
                            values(i - 3)
                        if i >= 5 and i % 2:
                            turn_o((i - 5) // 2)
                    pe.wait_ge(o_copied, PAIRS)
                    for t in range(GT):
                        for j in range(PAIRS):
                            last = pe.matmul(banks[:, 4, t * P:(t + 1) * P], oT(j)[:, t, :],
                                             w["Wo"][:, j, :], start=(j == 0), stop=(j == PAIRS - 1))
                    last.then_inc(out_ready, 1)

                @block.scalar
                def _(act):
                    act.copy(ys[:, :, 0:D // 2], yg[:, :, 0:D // 2]).then_inc(low_half, 1)
                    act.wait_ge(in_turned, 1)
                    act.copy(yT_in[:], banks[:, 7, :]).then_inc(in_ready, 1)

                    def square(n):
                        act.wait_ge(copied, n + 1)
                        if n >= 2:
                            act.wait_ge(reduced, n - 1)
                        act.activation(sq[:, n % 2, :], raw[:, n % 4, :], ACT.Square).then_inc(squared, 1)

                    for n in range(QK):
                        act.wait_ge(projected, n + 1)
                        if n >= 4:
                            act.wait_ge(cosined, n - 3)
                            act.wait_ge(swap_done, 2 * (n - 3))
                            act.wait_ge(squared, n - 3)
                        act.copy(raw[:, n % 4, :], banks[:, n % 4, :]).then_inc(copied, 1)
                        square(n)
                    for n in range(2 * GT):
                        act.wait_ge(projected, QK + n + 1)
                        act.copy(v1[:, n // 2, (n % 2) * PAIRS:(n % 2 + 1) * PAIRS, 0:HD], heads(banks[:, n % 4, :]))\
                            .then_inc(v_copied, 1)
                    act.wait_ge(clamped, 1)
                    act.activation(lg[:], ss[:], ACT.Ln).then_inc(logged, 1)
                    act.wait_ge(logged, 1)
                    act.activation(inv[:], lg[:], ACT.Exp, scale=-0.5).then_inc(rooted, 1)

                    def copy_qk(j):
                        for m in range(2):
                            act.wait_ge(qk_turned, 2 * j + m + 1)
                            if j >= 2:
                                act.wait_ge(scored, 2 * (j - 1))
                            act.copy(turned_qk[:, j % 2, m, :], banks[:, 4 + m, :]).then_inc(qk_copied, 1)

                    def exp(h):
                        act.wait_ge(banded, h + 1)
                        if h >= 2:
                            act.wait_ge(summed, h - 1)
                        for lo, hi, into in ((0, BAND, 0), (BAND, SCORES, SEQ)):
                            act.activation(probs[:, h % 2, :, into:into + hi - lo], logit[:, h % 2, :, lo:hi], ACT.Exp,
                                           bias=tables["npeak"][:], scale=SCALE).then_inc(exped, 1)

                    def copy_o(j):
                        act.wait_ge(o_turned, j + 1)
                        act.copy(oT(j), banks[:, 7, :].rearrange("p (t d) -> p t d", d=D)).then_inc(o_copied, 1)

                    for i in range(H + 5):
                        if i % 2 == 0 and i < H:
                            copy_qk(i // 2)
                        if 2 <= i <= H + 1:
                            exp(i - 2)
                        if i >= 5 and i % 2:
                            copy_o((i - 5) // 2)

                @block.gpsimd
                def _(pool):
                    for n in range(QK):
                        t, m, half = where(n)
                        pool.wait_ge(copied, n + 1)
                        if n >= 2:
                            pool.wait_ge(rotated, n - 1)
                        for r in range(2):
                            lo, other = slice(32 * r, 32 * r + 32), slice(32 - 32 * r, 64 - 32 * r)
                            pool.tensor_tensor(heads(swapped[:, n % 2, :])[:, :, lo], heads(raw[:, n % 4, :])[:, :, other],
                                               tables["all"][:, 2 * m + 1, t % ST, lo].unsqueeze(1)
                                               .broadcast_to([P, PAIRS, 32]), ALU.mult).then_inc(swap_done, 1)

                @block.vector
                def _(dve):
                    dve.wait_ge(shifted, 1)
                    dve.tensor_copy(ys[:, :, D // 2:], banks[:, 6, 0:GT * D // 2].rearrange("p (t d) -> p t d", d=D // 2))\
                        .then_inc(high_half, 1)
                    part = lambda n: heads(rot[:, where(n)[1], where(n)[0], where(n)[2] * HALF:(where(n)[2] + 1) * HALF])

                    def reduce(n):
                        t, m, half = where(n)
                        dve.wait_ge(squared, n + 1)
                        dve.tensor_reduce(ss[:, m, t, half * PAIRS:(half + 1) * PAIRS], heads(sq[:, n % 2, :]), AX_X, ALU.add)\
                            .then_inc(reduced, 1)

                    def rotate(n):
                        dve.wait_ge(cosined, n + 1)
                        dve.wait_ge(swap_done, 2 * n + 2)
                        dve.tensor_tensor(part(n), part(n), heads(swapped[:, n % 2, :]), ALU.add).then_inc(rotated, 1)

                    for n in range(QK + 1):
                        if n < QK:
                            t, m, half = where(n)
                            dve.wait_ge(copied, n + 1)
                            dve.tensor_tensor(part(n), heads(raw[:, n % 4, :]), tables["all"][:, 2 * m, t % ST, :].unsqueeze(1)
                                              .broadcast_to([P, PAIRS, HD]), ALU.mult).then_inc(cosined, 1)
                        if n:
                            reduce(n - 1)
                            rotate(n - 1)
                    dve.wait_ge(reduced, QK)
                    dve.tensor_scalar(ss[:], ss[:], 1e-24, UP, ALU.max, ALU.mult).then_inc(clamped, 1)
                    dve.wait_ge(rooted, 1)
                    dve.tensor_scalar(inv[:], inv[:], UP ** 0.5, None, ALU.mult).then_inc(scaled, 1)
                    dve.wait_ge(scaled, 1)
                    dve.wait_ge(rotated, QK)
                    for n in range(QK):
                        t, m, half = where(n)
                        dve.tensor_tensor(part(n), part(n), spread(inv[:, m, t, half * PAIRS:(half + 1) * PAIRS], HD),
                                          ALU.mult).then_inc(unit, 1)

                    def mask(h):
                        dve.wait_ge(scored, h + 1)
                        if h >= 2:
                            dve.wait_ge(exped, 2 * (h - 1))
                        dve.tensor_tensor(logit[:, h % 2, :, :], banks[:, 2 * (h % 2):2 * (h % 2) + GB, 0:SCORES],
                                          consts["band"].unsqueeze(1).broadcast_to([P, GB, SCORES]), ALU.add)\
                            .then_inc(banded, 1)

                    def normalize(h):
                        dve.wait_ge(summed, h + 1)
                        out = banks[:, 6, 0:GT * (HD + 1)].rearrange("p (t e) -> p t e", e=HD + 1)
                        dve.reciprocal(rden[:, h % 2, :], out[:, :, HD]).then_inc(rden_ready, 1)
                        dve.wait_ge(rden_ready, h + 1)
                        if h >= 4:
                            dve.wait_ge(o_turned, h // 2 - 1)
                        dve.tensor_tensor(o[:, h // 2 % 2, :, h % 2 * HD:(h % 2 + 1) * HD], out[:, :, 0:HD], spread(rden[:, h % 2, :], HD),
                                          ALU.mult).then_inc(head_done, 1)

                    for i in range(H + 2):
                        if i < H:
                            mask(i)
                        if i >= 2:
                            normalize(i - 2)
                    dve.wait_ge(out_ready, 1)
                    dve.tensor_tensor(yg, yg, banks[:, 4, :].rearrange("p (t d) -> p t d", d=D), ALU.add).then_inc(added, 1)
            restart(nc, sems)


def gated_mlp(nc, y, banks, consts, w, tmp):
    with ExitStack() as ctx:
        ys, gate, hT = tmp["ys"], tmp["gate"], tmp["hT"]
        ln = LayerNorm(nc, ctx, consts, banks[:, 7, :], "mlp_ln")
        sems = signals(nc, ctx, "shifted low_half high_half widened gelu_done hidden out_ready added")
        shifted, low_half, high_half, widened, gelu_done, hidden, out_ready, added = sems
        sems = ln.sems + sems
        CH = len(MLP_CHUNKS)

        with nc.Fori(0, GROUPS) as g:
            yg = y[:, bass.ds(g * GT, GT), :]
            with nc.Block() as block:
                @block.tensor
                def _(pe):
                    shift_tokens(pe, banks, consts, yg, shifted)
                    ln.tensor(pe)
                    pe.wait_ge(ln.ready, 1)
                    for c, (lo, m) in enumerate(MLP_CHUNKS):
                        for r in range(2):
                            if c == 2:
                                pe.wait_ge(hidden, 1)
                            pe.matmul(banks[0:m, 2 * (c % 2) + r, :], w["W1"][:, r * MLP + lo:r * MLP + lo + m], ln.xnT[:],
                                      start=True, stop=True).then_inc(widened, 1)
                    pe.wait_ge(hidden, CH)
                    for t in range(GT):
                        out = banks[:, 4, t * P:(t + 1) * P]
                        for c, (lo, m) in enumerate(MLP_CHUNKS):
                            pe.matmul(out, hT[0:m, c, t * P:(t + 1) * P], w["W2"][0:m, c, :], start=(c == 0), stop=False)
                        last = pe.matmul(out, consts["ones"][0:1, 0:P], w["b2"][:], start=False, stop=True)
                    last.then_inc(out_ready, 1)

                @block.scalar
                def _(act):
                    act.preload_act_table_set(EXP_LN)
                    act.copy(ys[:, :, 0:D // 2], yg[:, :, 0:D // 2]).then_inc(low_half, 1)
                    ln.scalar(act, copy=False)
                    act.wait_ge(ln.turned, GT)
                    act.activation(ln.xnT[:], banks[:, 7, :], ACT.Identity, bias=w["ln_b"][:], scale=w["ln_g"][:])\
                        .then_inc(ln.ready, 1)
                    for c, (lo, m) in enumerate(MLP_CHUNKS):
                        act.wait_ge(widened, 2 * c + 2)
                        if c == 2:
                            act.wait_ge(hidden, 1)
                        act.activation(gate[0:m, c % 2, :], banks[0:m, 2 * (c % 2) + 1, :], ACT.Gelu,
                                       bias=w["b1"][0:m, CH + c:CH + c + 1]).then_inc(gelu_done, 1)

                @block.vector
                def _(dve):
                    dve.wait_ge(shifted, 1)
                    dve.tensor_copy(ys[:, :, D // 2:], banks[:, 6, 0:GT * D // 2].rearrange("p (t d) -> p t d", d=D // 2))\
                        .then_inc(high_half, 1)
                    dve.wait_ge(high_half, 1)
                    dve.wait_ge(low_half, 1)
                    ln.vector(dve, ys)
                    for c, (lo, m) in enumerate(MLP_CHUNKS):
                        dve.wait_ge(gelu_done, c + 1)
                        dve.scalar_tensor_tensor(hT[0:m, c, :], banks[0:m, 2 * (c % 2), :], w["b1"][0:m, c:c + 1],
                                                 gate[0:m, c % 2, :], ALU.add, ALU.mult).then_inc(hidden, 1)
                    dve.wait_ge(out_ready, 1)
                    dve.tensor_tensor(yg, yg, banks[:, 4, :].rearrange("p (t d) -> p t d", d=D), ALU.add).then_inc(added, 1)
            restart(nc, sems)


def local_layers(nc, x, banks, consts, w, t):
    QS = 8.0
    f = "L3_ffn_"
    with ExitStack() as ctx:
        sb = lambda n, s: ctx.enter_context(nc.sbuf_tensor("local_" + n, s, F32))
        y = sb("y", [P, TILES, D])
        lw = {"Wqkv": sb("Wqkv", [P, 3 * INNER]), "Wo": sb("Wo", [P, PAIRS, D]), "W1": sb("W1", [P, 2 * MLP]),
              "W2": sb("W2", [P, len(MLP_CHUNKS), D]), "b1": sb("b1", [P, 2 * len(MLP_CHUNKS)]), "b2": sb("b2", [1, D]),
              "ln_g": sb("ln_g", [P, 1]), "ln_b": sb("ln_b", [P, 1])}
        scales = sb("qk_scales", [P, 4, HD])
        shapes = sb("rotary", [P, 4, ST, HD])
        tables = {"all": sb("rotary_scaled", [P, 4, ST, HD]), "npeak": sb("npeak", [P, 1])}
        most = sb("most", [P, 2])
        ones_done = signals(nc, ctx, "ones")[0]
        rotary_loaded, attn_loaded, mlp_loaded, tabled = signals(nc, ctx, "rotary_loaded attn_loaded mlp_loaded tabled")

        with ExitStack() as inner:
            ln = LayerNorm(nc, inner, consts, banks[:, 7, :], "local_ln")
            with nc.Block() as block:
                @block.sync
                def _(sp):
                    sp.dma_start(shapes[:], t["rotary"]).then_inc(rotary_loaded, 16)
                    sp.wait_ge(rotary_loaded, 16)

                @block.scalar
                def _(act):
                    act.preload_act_table_set(EXP_LN)
            with nc.Fori(0, GROUPS) as g:
                xg, yg = x[:, bass.ds(g * GT, GT), :], y[:, bass.ds(g * GT, GT), :]
                with nc.Block() as block:
                    @block.vector
                    def _(dve):
                        ln.vector(dve, xg)
                        dve.wait_ge(ln.normed, GT)
                        dve.tensor_copy(yg, ln.xn[:]).then_inc(ln.ready, 1)

                    @block.scalar
                    def _(act):
                        ln.scalar(act, copy=False)
                restart(nc, ln.sems)

        tmp = {n: sb("" + n, s) for n, s in (
            ("ys", [P, GT, D]), ("ysT", [P, GN]), ("raw", [P, 4, INNER // 2]), ("sq", [P, 2, INNER // 2]),
            ("swapped", [P, 2, INNER // 2]), ("ss", [P, 2, GT, H]), ("lg", [P, 2, GT, H]), ("inv", [P, 2, GT, H]),
            ("rot", [P, 2, GT, INNER]), ("turned_qk", [P, 2, 2, GN]), ("logit", [P, 2, GB, 2 * P + WINDOW]),
            ("probs", [P, 2, GB, CAUSAL]), ("v1", [P, GT, H, HD + 1]), ("rden", [P, 2, GT]), ("o", [P, 2, GT, D]),
            ("gate", [P, 2, GN]), ("hT", [P, len(MLP_CHUNKS), GN]))}
        with nc.Block() as block:
            @block.vector
            def _(dve):
                dve.memset(tmp["v1"][:, :, :, HD:HD + 1], 1.0)

            @block.gpsimd
            def _(pool):
                pool.memset(tmp["probs"][:], 0.0).then_inc(ones_done, 1)

        with nc.Fori(0, DEPTH) as layer:
            at = lambda n: t[f + n][bass.ds(layer, 1)]
            attn_moves = [(lw["Wqkv"][:], at("Wqkv").rearrange("l d n -> d (l n)")),
                          (lw["Wo"][:], at("Wo").rearrange("l (j p) d -> p (l j) d", p=P))]
            for n, name in ((0, "q_scale"), (2, "k_scale")):
                s = at(name)
                attn_moves += [(scales[:, n, :], s.broadcast_to([P, HD])),
                               (scales[:, n + 1, 0:HD // 2], s[:, HD // 2:].broadcast_to([P, HD // 2])),
                               (scales[:, n + 1, HD // 2:], s[:, 0:HD // 2].broadcast_to([P, HD // 2]))]
            full = sum(m == P for _, m in MLP_CHUNKS)
            rest = MLP_CHUNKS[-1][1]
            mlp_moves = [(lw["W1"][:], at("W1").rearrange("l d n -> d (l n)")),
                         (lw["W2"][:, 0:full, :], at("W2")[:, 0:full * P, :].rearrange("l (c p) d -> p (l c) d", p=P)),
                         (lw["W2"][0:rest, full, :], at("W2")[:, full * P:, :].rearrange("l p d -> p (l d)")),
                         (lw["b1"][:], at("b1T").rearrange("l p c -> p (l c)")), (lw["b2"][:], at("b2")),
                         (lw["ln_g"][:], at("ln_g").rearrange("l d -> d l")), (lw["ln_b"][:], at("ln_b").rearrange("l d -> d l"))]
            with nc.Block() as block:
                @block.sync
                def _(sp):
                    for tile, source in attn_moves:
                        sp.dma_start(tile, source).then_inc(attn_loaded, 16)
                    for tile, source in mlp_moves:
                        sp.dma_start(tile, source).then_inc(mlp_loaded, 16)
                    sp.wait_ge(attn_loaded, 16 * len(attn_moves))

                @block.vector
                def _(dve):
                    dve.wait_ge(attn_loaded, 16 * len(attn_moves))
                    dve.tensor_tensor(tables["all"][:], shapes[:], scales[:].unsqueeze(2).broadcast_to([P, 4, ST, HD]),
                                      ALU.mult).then_inc(tabled, 1)
                    for n in range(2):
                        dve.tensor_reduce(most[:, n:n + 1], scales[:, 2 * n, :], AX_X, ALU.max, apply_absolute_value=True)\
                            .then_inc(tabled, 1)
                    dve.wait_ge(tabled, 3)
                    dve.tensor_scalar(tables["npeak"][:], most[:, 0:1], most[:, 1:2], -QS, ALU.mult, ALU.mult).then_inc(tabled, 1)

                @block.scalar
                def _(act):
                    act.preload_act_table_set(EXP_LN)
            restart(nc, [attn_loaded])
            band_attention(nc, y, banks, consts, lw, tables, tmp)
            with nc.Block() as block:
                @block.sync
                def _(sp):
                    sp.wait_ge(mlp_loaded, 16 * len(mlp_moves))
            restart(nc, [mlp_loaded, tabled])
            gated_mlp(nc, y, banks, consts, lw, tmp)

        with nc.Block() as block:
            @block.vector
            def _(dve):
                dve.tensor_tensor(x[:], x[:], y[:], ALU.add)


STAGES = ["favor", "router", "cosine", "int4", "mamba", "experts", "hgrn", "local"]


class Weights:

    def __init__(self, nc, ctx, t, stage, prefix):
        self.nc, self.ctx, self.t, self.prefix, self.stage = nc, ctx, t, prefix, stage
        self.moves, self.tiles = [], {"loaded": signals(nc, ctx, stage + "_loaded")[0]}

    def add(self, name, shape, source):
        tile = self.ctx.enter_context(self.nc.sbuf_tensor(f"{self.stage}_w_{name}", shape, F32))
        self.tiles[name] = tile
        self.moves.append((tile[:], source))
        self.tiles["total"] = 16 * len(self.moves)
        return tile

    def load(self, sp):
        for tile, source in self.moves:
            sp.dma_start(tile, source).then_inc(self.tiles["loaded"], 16)


def weights(nc, ctx, t):
    row = lambda a: a.rearrange("(o n) -> o n", o=1)
    column = lambda a: a.rearrange("(n o) -> n o", o=1)

    favor = Weights(nc, ctx, t, "favor", "L0_attn_")
    for n in ("Wq", "Wk"):
        tile = favor.add(n + "2", [P, H, 2 * HD], None)
        favor.moves.pop()
        for r in range(2):
            favor.moves.append((tile[:, :, r * HD:(r + 1) * HD], t["L0_attn_" + n].rearrange("p (h d) -> p h d", d=HD)))
    favor.add("Wv", [P, INNER], t["L0_attn_Wv"])
    favor.add("Wo", [P, PAIRS, D], t["L0_attn_Wo"].rearrange("(j p) d -> p j d", p=P))
    favor.add("Wfeat", [P, NF], t["Wfeat"])

    f = "L0_ffn_"
    router = Weights(nc, ctx, t, "router", f)
    router.add("W1T", [P, 512], t["L0_ffn_W1T"])
    router.add("W2T", [P, 4, D], t["L0_ffn_W2T"].rearrange("(c p) d -> p c d", p=P))
    router.add("ln_g", [P, 1], column(t[f + "ln_g"]))
    router.add("ln_b", [P, 1], column(t[f + "ln_b"]))
    router.add("RT", [P, 64], t["L0_ffn_router_WT"])
    router.add("rb", [1, 64], row(t[f + "router_b"]))
    router.add("U", [64, D], t[f + "raw_U"])
    router.add("V", [64, D], t[f + "raw_V"])
    router.add("gamma", [64, D], t[f + "gamma"].rearrange("a b d -> (a b d)").partition_broadcast(64))

    f = "L1_attn_"
    cosine = Weights(nc, ctx, t, "cosine", f)
    cosine.add("Wqkv", [P, 3 * INNER], None)
    cosine.moves.pop()
    cosine.moves += [(cosine.tiles["Wqkv"][:, 0:INNER], t[f + "w_q"]), (cosine.tiles["Wqkv"][:, INNER:], t[f + "w_kv"])]
    cosine.add("Wo", [P, PAIRS, D], t[f + "w_out"].rearrange("(j p) d -> p j d", p=P))
    cosine.add("bo", [1, D], row(t[f + "b_out"]))
    cosine.add("scale", [P, H], t[f + "scale"].rearrange("a h b c -> (a h b c)").partition_broadcast(P))

    f = "L1_ffn_"
    int4 = Weights(nc, ctx, t, "int4", f)
    int4.add("kernel", [P, D], t[f + "kernel"])
    int4.add("bias", [1, D], row(t[f + "bias"]))
    int4.add("a", [P, 16], t[f + "a"])
    int4.add("b", [16, D], t[f + "b"])
    f = "L2_attn_"
    mamba = Weights(nc, ctx, t, "mamba", f)
    mamba.add("Win", [P, 512], t[f + "Win"])
    mamba.add("bin", [P, 4], t[f + "binT"])
    mamba.add("Wx", [P, 2, 40], t[f + "Wx"].rearrange("(c p) n -> p c n", p=P))
    mamba.add("bdp", [8, 1], column(t[f + "bx"][0:8]))
    mamba.add("bB", [16, 1], column(t[f + "bx"][8:24]))
    mamba.add("bC", [16, 1], column(t[f + "bx"][24:40]))
    mamba.add("Wdt", [8, 256], t[f + "Wdt"])
    mamba.add("bdt", [P, 2], t[f + "bdtT"])
    mamba.add("A_log", [P, 2, 16], t[f + "A_log"].rearrange("(c p) n -> p c n", p=P))
    mamba.add("Dp", [P, 2], t[f + "DpT"])
    mamba.add("Wout", [P, 2, D], t[f + "Wout"].rearrange("(c p) d -> p c d", p=P))
    mamba.add("bout", [1, D], row(t[f + "bout"]))

    f = "L2_ffn_"
    experts = Weights(nc, ctx, t, "experts", f)
    experts.add("Wg", [P, 8], t[f + "Wg"])
    experts.add("bg", [1, 8], row(t[f + "bg"]))
    experts.add("W1", [P, 8, 512], t[f + "W1"].rearrange("e d f -> d e f"))
    experts.add("b1", [P, 32], t[f + "b1T"])
    experts.add("W2", [P, 8, 4, D], t[f + "W2"].rearrange("e (c p) d -> p e c d", p=P))
    experts.add("b2", [8, D], t[f + "b2"])
    experts.add("gamma", [P, D], t[f + "gamma"].partition_broadcast(P))
    experts.add("beta", [P, D], t[f + "beta"].partition_broadcast(P))

    f = "L3_attn_"
    hgrn = Weights(nc, ctx, t, "hgrn", f)
    for n, m in (("Wq", D), ("Wk", D), ("Wv", D), ("G1", 64), ("Wo", D)):
        hgrn.add(n, [P, m], t[f + n])
    hgrn.add("G2", [64, D], t[f + "G2"])
    hgrn.add("delta", [P, 1], column(t[f + "delta"]))
    hgrn.add("norm_w", [P, 1], column(t[f + "norm_w"]))
    return {"favor": favor, "router": router, "cosine": cosine, "int4": int4, "mamba": mamba, "experts": experts,
            "hgrn": hgrn}


RUN = {"favor": favor_attention, "router": router_ffn, "cosine": cosine_attention, "int4": int4_linear,
       "mamba": state_space, "experts": expert_ffn, "hgrn": gated_recurrence}


def build(nc, t, out, stages):
    with ExitStack() as ctx:
        sb = lambda n, s, d=F32: ctx.enter_context(nc.sbuf_tensor(n, s, d))
        banks = ctx.enter_context(nc.psum_tensor("banks", [P, 8, 512], F32))
        x = sb("x", [P, TILES, D])
        consts = {n: sb(n, list(t[n].shape))[:] for n in ("ident", "causal", "ones", "pick", "count", "inside", "blocks", "next", "carry", "band")}
        x_loaded, consts_loaded, stored = signals(nc, ctx, "x_loaded consts_loaded stored")
        held = ctx.enter_context(ExitStack())
        ws = weights(nc, held, t)

        with nc.Block() as block:
            @block.sync
            def _(sp):
                sp.dma_start(x[:], t["L0_attn_x"].rearrange("b (t p) d -> p (b t) d", p=P)).then_inc(x_loaded, 16)
                for n in consts:
                    sp.dma_start(consts[n], t[n]).then_inc(consts_loaded, 16)
                for w in ws.values():
                    w.load(sp)
                sp.wait_ge(x_loaded, 16)
                sp.wait_ge(consts_loaded, 16 * len(consts))
        for stage in stages:
            if stage != "local":
                RUN[stage](nc, x, banks, consts, ws[stage].tiles)
        with nc.Block() as block:
            @block.sync
            def _(sp):
                for w in ws.values():
                    sp.wait_ge(w.tiles["loaded"], w.tiles["total"])
        held.close()
        if "local" in stages:
            local_layers(nc, x, banks, consts, None, t)
        with nc.Block() as block:
            @block.sync
            def _(sp):
                sp.dma_start(out.rearrange("b (t p) d -> p (b t) d", p=P), x[:]).then_inc(stored, 16)
                sp.wait_ge(stored, 16)


def rotary():
    half = np.arange(0, HD, 2, dtype=np.float32)
    inv_freq = 1.0 / np.float32(10000.0) ** (half / HD)
    at = np.arange(SEQ, dtype=np.float32)
    freqs = at[:, None] * inv_freq[None, :]
    base = (half + 0.4 * HD) / (1.4 * HD)
    scale = base[None, :].astype(np.float64) ** ((at - SEQ // 2) / (WINDOW // 2))[:, None]
    cos, sin = np.cos(freqs.astype(np.float64)), np.sin(freqs.astype(np.float64))
    four = [np.concatenate([cos * s, cos * s], 1) if c else np.concatenate([-sin * s, sin * s], 1)
            for s in (scale, 1 / scale) for c in (True, False)]
    return np.ascontiguousarray(np.stack(four).reshape(4, ST, P, HD).transpose(2, 0, 1, 3)).astype(np.float32)


def shape_constants():
    i = np.arange(P)
    ahead = np.arange(P + WINDOW)[None, :] - i[:, None]
    seen = np.where((ahead >= 0) & (ahead <= WINDOW), 0.0, -1e30).astype(np.float32)
    band = np.concatenate([seen, seen[:, :P]], 1)
    tri = (i[:, None] <= i[None, :]).astype(np.float32)
    return {"ident": np.eye(P, dtype=np.float32), "causal": np.concatenate([tri, np.ones((P, P), np.float32), tri], 1),
            "ones": np.ones((P, P), np.float32),
            "pick": np.repeat(np.eye(16, dtype=np.float32), P, 1),
            "count": np.tile(np.arange(8, dtype=np.float32), (P, 1)),
            "inside": np.tile((np.arange(GN) % 64 != 0).astype(np.float32), (P, 1)),
            "next": np.eye(P, k=1, dtype=np.float32),
            "carry": (np.arange(P * P).reshape(P, P) == (P - 1) * P).astype(np.float32),
            "rotary": rotary(), "band": band,
            "blocks": np.kron(np.eye(2, dtype=np.float32), np.ones((64, 64), np.float32))}


def layouts(a):
    w = {k: np.ascontiguousarray(v) for k, v in a.items()}
    w["Wfeat"] = np.concatenate([np.asarray(a["L0_attn_W_feat"]), np.full((HD, NF), -0.5, np.float32)], 0)
    for n in ("L0_ffn_W1", "L0_ffn_W2", "L0_ffn_router_W"):
        w[n + "T"] = np.ascontiguousarray(w[n].T)
    b1 = np.zeros((DEPTH, 2, len(MLP_CHUNKS) * P), np.float32)
    b1[:, :, :MLP] = w["L3_ffn_b1"].reshape(DEPTH, 2, MLP)
    w["L3_ffn_b1T"] = np.ascontiguousarray(b1.reshape(DEPTH, -1, P).transpose(0, 2, 1))
    for n in ("L2_attn_bin", "L2_attn_bdt", "L2_attn_Dp", "L2_ffn_b1"):
        w[n + "T"] = np.ascontiguousarray(w[n].reshape(-1, P).T)
    return w


def kernel(**inputs):
    import concourse.bacc as bacc
    from concourse.bass_utils import run_bass_kernel_spmd

    nc = bacc.Bacc("TRN2", target_bir_lowering=False, num_devices=1)
    arrays = layouts({k: np.asarray(v) for k, v in inputs.items()}) | shape_constants()
    t = {n: nc.dram_tensor("in_" + n, a.shape, mybir.dt.from_np(a.dtype), kind="ExternalInput").ap() for n, a in arrays.items()}
    out = nc.dram_tensor("out", (BATCH, SEQ, D), F32, kind="ExternalOutput").ap()
    build(nc, t, out, STAGES)
    return run_bass_kernel_spmd(nc, [{"in_" + n: a for n, a in arrays.items()}], core_ids=[0]).results[0]["out"]
```

```python
from contextlib import ExitStack

import numpy as np
import concourse.bass as bass
from concourse import mybir

ALU = mybir.AluOpType
ACT = mybir.ActivationFunctionType
AX_X = mybir.AxisListType.X
F32 = mybir.dt.float32
U32 = mybir.dt.uint32
BF16 = mybir.dt.bfloat16

P = 128
BATCH, SEQ, D = 16, 256, 128
TILES = BATCH * SEQ // P
GT = 4
GN = GT * P
GROUPS = TILES // GT
GB = GN // SEQ
ST = SEQ // P
H, HD = 16, 64
PAIRS = H // 2
INNER = H * HD
NF = 128
LN_EPS = 1e-5
DEPTH, WINDOW = 6, 32
MLP = D * 4 * 2 // 3
MLP_CHUNKS = [(lo, min(P, MLP - lo)) for lo in range(0, MLP, P)]
EXP_LN = "natural_log_exp_and_others"
KEYS0, CAUSAL = SEQ, SEQ + P


def signals(nc, ctx, names):
    return [ctx.enter_context(nc.semaphore(n)) for n in names.split()]


def restart(nc, sems):
    numbers = sorted(s.num for s in sems)
    starts = [n for n in numbers if n - 1 not in numbers]
    ends = [n + 1 for n in numbers if n + 1 not in numbers]
    for a, b in zip(starts, ends):
        nc.all_engine_barrier(sems_to_clear=range(a, b))


def spread(a, n):
    return a.unsqueeze(-1).broadcast_to([*a.shape, n])


def pipeline(nc, step):
    step(None, 0, 1)
    with nc.Fori(0, (GROUPS - 2) // 2) as pair:
        g = 2 * pair
        step(g, g + 1, 0)
        step(g + 1, g + 2, 1)
    step(GROUPS - 2, GROUPS - 1, 0)
    step(GROUPS - 1, None, 1)


class LayerNorm:

    def __init__(self, nc, ctx, consts, bank, name, room=None):
        sb = lambda n, s: ctx.enter_context(nc.sbuf_tensor(n.replace("ln", name, 1), s, F32))
        self.ident, self.bank = consts["ident"], bank
        self.stats, self.moments = sb("ln_stats_t", [P, GT, 6]), sb("ln_moments_t", [P, GT, 2])
        self.var, self.log, self.rstd = sb("ln_var_t", [P, GT]), sb("ln_log_t", [P, GT]), sb("ln_rstd_t", [P, GT])
        self.xn, self.xnT = room or (sb("ln_xn", [P, GT, D]), sb("ln_xnT", [P, GN]))
        self.sems = signals(nc, ctx, "ln_stats ln_moments ln_var ln_log ln_rstd ln_normed ln_turned ln_ready".replace("ln_", name + "_"))
        (self.stats_done, self.moments_done, self.var_done, self.log_done, self.rstd_done, self.normed,
         self.turned, self.ready) = self.sems

    def vector(self, dve, x):
        self.gather_moments(dve, x)
        self.normalize(dve, x)

    def gather_moments(self, dve, x):
        for t in range(GT):
            dve.bn_stats(self.stats[:, t, :], x[:, t, :]).then_inc(self.stats_done, 1)
        dve.wait_ge(self.stats_done, GT)
        for t in range(GT):
            dve.bn_aggr(self.moments[:, t, :], self.stats[:, t, :]).then_inc(self.moments_done, 1)
        dve.wait_ge(self.moments_done, GT)
        dve.tensor_scalar(self.var[:], self.moments[:, :, 1], LN_EPS, None, ALU.add).then_inc(self.var_done, 1)

    def normalize(self, dve, x):
        dve.wait_ge(self.rstd_done, 1)
        for t in range(GT):
            dve.tensor_scalar(self.xn[:, t, :], x[:, t, :], self.moments[:, t, 0:1], self.rstd[:, t:t + 1],
                              ALU.subtract, ALU.mult).then_inc(self.normed, 1)

    def scalar(self, act, copy=True):
        self.root(act)
        if copy:
            self.copy(act)

    def root(self, act):
        act.wait_ge(self.var_done, 1)
        act.activation(self.log[:], self.var[:], ACT.Ln).then_inc(self.log_done, 1)
        act.wait_ge(self.log_done, 1)
        act.activation(self.rstd[:], self.log[:], ACT.Exp, scale=-0.5).then_inc(self.rstd_done, 1)

    def copy(self, act):
        act.wait_ge(self.turned, GT)
        act.copy(self.xnT[:], self.bank).then_inc(self.ready, 1)

    def tensor(self, pe):
        for t in range(GT):
            pe.wait_ge(self.normed, t + 1)
            pe.transpose(self.bank[:, t * P:(t + 1) * P], self.xn[:, t, :], self.ident).then_inc(self.turned, 1)


def favor_attention(nc, x, banks, consts, w):
    EPS = 1e-6 * NF
    with ExitStack() as ctx:
        sb = lambda n, s: ctx.enter_context(nc.sbuf_tensor("favor_" + n, s, F32))
        ln = LayerNorm(nc, ctx, consts, banks[:, 7, :], "favor_ln")
        qs, ks = sb("qs", [P, 2, GN]), sb("ks", [P, 2, GN])
        qf, kf = sb("qf", [P, 2, GN]), sb("kf", [P, 2, GN])
        scores = sb("scores", [P, 2, GB, CAUSAL])
        v1 = sb("v1", [P, GT, H, HD + 1])
        den, rden = sb("den", [P, 2, GT]), sb("rden", [P, 2, GT])
        y, yT = sb("y", [P, 2, GT, D]), sb("yT", [P, PAIRS, GN])
        sems = signals(nc, ctx, "projected squared copied featured exped scored masked summed den_ready "
                                "rden_ready head_done v_projected v_copied y_turned y_copied out_ready added")
        (projected, squared, copied, featured, exped, scored, masked, summed, den_ready, rden_ready, head_done,
         v_projected, v_copied, y_turned, y_copied, out_ready, added) = sems
        sems = ln.sems + sems

        with nc.Block() as block:
            @block.sync
            def _(sp):
                sp.wait_ge(w["loaded"], w["total"])

            @block.vector
            def _(dve):
                dve.memset(v1[:, :, :, HD:HD + 1], 1.0)

            @block.scalar
            def _(act):
                act.preload_act_table_set(EXP_LN)

        with nc.Fori(0, GROUPS) as g:
            xg = x[:, bass.ds(g * GT, GT), :]
            with nc.Block() as block:
                @block.tensor
                def _(pe):
                    ln.tensor(pe)
                    pe.wait_ge(ln.ready, 1)
                    for n in range(2 * GT):
                        if n >= 2:
                            pe.wait_ge(v_copied, n - 1)
                        pe.matmul(banks[:, 4 + n % 2, :], ln.xnT[:, (n // 2) * P:(n // 2 + 1) * P],
                                  w["Wv"][:, (n % 2) * 512:(n % 2 + 1) * 512], start=True, stop=True)\
                            .then_inc(v_projected, 1)

                    def project(h):
                        for n, name in enumerate(("Wq2", "Wk2")):
                            if h:
                                pe.wait_ge(squared, 2 * (h - 1) + n + 1)
                                pe.wait_ge(copied, 2 * (h - 1) + n + 1)
                            pe.matmul(banks[:, n, :], w[name][:, h, :], ln.xnT[:], start=True, stop=True)\
                                .then_inc(projected, 1)

                    def features(h):
                        for n, s in enumerate((qs, ks)):
                            pe.wait_ge(squared, 2 * h + n + 1)
                            pe.wait_ge(copied, 2 * h + n + 1)
                            if h:
                                pe.wait_ge(exped, 2 * (h - 1) + n + 1)
                            pe.matmul(banks[:, 2 + n, :], w["Wfeat"][:], s[:, h % 2, :], start=True, stop=True)\
                                .then_inc(featured, 1)

                    def score(h):
                        pe.wait_ge(exped, 2 * h + 2)
                        if h == 0:
                            pe.wait_ge(v_copied, 2 * GT)
                        for b in range(GB):
                            if h:
                                pe.wait_ge(masked, GB * (h - 1) + b + 1)
                            c = b * SEQ
                            pe.matmul(banks[:, 4 + b, 0:SEQ], kf[:, h % 2, c:c + P], qf[:, h % 2, c:c + SEQ],
                                      start=True, stop=True)
                            pe.matmul(banks[:, 4 + b, SEQ:CAUSAL], kf[:, h % 2, c + P:c + SEQ],
                                      qf[:, h % 2, c + P:c + SEQ], start=True, stop=True).then_inc(scored, 1)

                    def values(h):
                        pe.wait_ge(masked, GB * (h + 1))
                        if h:
                            pe.wait_ge(head_done, h)
                        for b in range(GB):
                            for i in range(ST):
                                out = banks[:, 6, (b * ST + i) * (HD + 1):(b * ST + i + 1) * (HD + 1)]
                                for j in range(i + 1):
                                    c = (i * P if j == 0 else SEQ)
                                    last = pe.matmul(out, scores[:, h % 2, b, c:c + P], v1[:, b * ST + j, h, :],
                                                     start=(j == 0), stop=(j == i))
                        last.then_inc(summed, 1)

                    def turn(j):
                        pe.wait_ge(head_done, 2 * j + 2)
                        if j:
                            pe.wait_ge(y_copied, j)
                        for t in range(GT):
                            last = pe.transpose(banks[:, 7, t * P:(t + 1) * P], y[:, j % 2, t, :],
                                                consts["ident"])
                        last.then_inc(y_turned, 1)

                    for i in range(H + 5):
                        if i < H:
                            project(i)
                        if 1 <= i <= H:
                            features(i - 1)
                        if 2 <= i <= H + 1:
                            score(i - 2)
                        if 3 <= i <= H + 2:
                            values(i - 3)
                        if i >= 5 and i % 2:
                            turn((i - 5) // 2)
                    pe.wait_ge(y_copied, PAIRS)
                    for t in range(GT):
                        for j in range(PAIRS):
                            last = pe.matmul(banks[:, 0, t * P:(t + 1) * P], yT[:, j, t * P:(t + 1) * P],
                                             w["Wo"][:, j, :], start=(j == 0), stop=(j == PAIRS - 1))
                    last.then_inc(out_ready, 1)

                @block.scalar
                def _(act):
                    ln.scalar(act)
                    for n in range(2 * GT):
                        act.wait_ge(v_projected, n + 1)
                        act.copy(v1[:, n // 2, (n % 2) * PAIRS:(n % 2 + 1) * PAIRS, 0:HD],
                                 banks[:, 4 + n % 2, :].rearrange("p (h d) -> p h d", d=HD)).then_inc(v_copied, 1)

                    def square(h):
                        for n, s in enumerate((qs, ks)):
                            act.wait_ge(projected, 2 * h + n + 1)
                            if h >= 2:
                                act.wait_ge(featured, 2 * (h - 2) + n + 1)
                            act.activation(s[HD:P, h % 2, :], banks[HD:P, n, :], ACT.Square).then_inc(squared, 1)

                    def exp(h):
                        for n, f in enumerate((qf, kf)):
                            act.wait_ge(featured, 2 * h + n + 1)
                            if h >= 2:
                                act.wait_ge(scored, GB * (h - 1))
                            act.activation(f[:, h % 2, :], banks[:, 2 + n, :], ACT.Exp).then_inc(exped, 1)

                    def y_copy(j):
                        act.wait_ge(y_turned, j + 1)
                        act.copy(yT[:, j, :], banks[:, 7, :]).then_inc(y_copied, 1)

                    for i in range(H + 5):
                        if i < H:
                            square(i)
                        if 1 <= i <= H:
                            exp(i - 1)
                        if i >= 5 and i % 2:
                            y_copy((i - 5) // 2)

                @block.vector
                def _(dve):
                    ln.vector(dve, xg)

                    def copy(h):
                        for n, s in enumerate((qs, ks)):
                            dve.wait_ge(projected, 2 * h + n + 1)
                            if h >= 2:
                                dve.wait_ge(featured, 2 * (h - 2) + n + 1)
                            dve.tensor_copy(s[0:HD, h % 2, :], banks[0:HD, n, :]).then_inc(copied, 1)

                    def mask(h):
                        if h >= 2:
                            dve.wait_ge(summed, h - 1)
                        for b in range(GB):
                            dve.wait_ge(scored, GB * h + b + 1)
                            dve.tensor_tensor(scores[:, h % 2, b, :], banks[:, 4 + b, 0:CAUSAL], consts["causal"],
                                              ALU.mult).then_inc(masked, 1)

                    def normalize(h):
                        dve.wait_ge(summed, h + 1)
                        out = banks[:, 6, 0:GT * (HD + 1)].rearrange("p (t e) -> p t e", e=HD + 1)
                        dve.tensor_scalar(den[:, h % 2, :], out[:, :, HD], EPS, None, ALU.add).then_inc(den_ready, 1)
                        dve.wait_ge(den_ready, h + 1)
                        dve.reciprocal(rden[:, h % 2, :], den[:, h % 2, :]).then_inc(rden_ready, 1)
                        dve.wait_ge(rden_ready, h + 1)
                        if h >= 4:
                            dve.wait_ge(y_turned, h // 2 - 1)
                        dve.tensor_tensor(y[:, h // 2 % 2, :, h % 2 * HD:(h % 2 + 1) * HD], out[:, :, 0:HD],
                                          spread(rden[:, h % 2, :], HD), ALU.mult)\
                            .then_inc(head_done, 1)

                    for i in range(H + 4):
                        if i < H:
                            copy(i)
                        if 2 <= i <= H + 1:
                            mask(i - 2)
                        if 3 <= i <= H + 2:
                            normalize(i - 3)
                    dve.wait_ge(out_ready, 1)
                    dve.tensor_tensor(xg, xg, banks[:, 0, :].rearrange("p (t d) -> p t d", d=D), ALU.add)\
                        .then_inc(added, 1)
            restart(nc, sems)

def router_ffn(nc, x, banks, consts, w):
    DFF, NB, TOP, TAU, EPS = 512, 64, 8, 10.0, 1e-6
    CH = DFF // P
    with ExitStack() as ctx:
        sb = lambda n, s: ctx.enter_context(nc.sbuf_tensor("router_" + n, s, F32))
        ln = LayerNorm(nc, ctx, consts, banks[:, 2, :], "router_ln")
        ln2 = LayerNorm(nc, ctx, consts, banks[:, 3, :], "router_ln2")
        unT, vg = sb("unT", [P, NB]), sb("vg", [NB, D])
        rows, sq, ss, root = sb("unit_rows", [NB, 2, D]), sb("unit_sq", [NB, 2, D]), sb("unit_ss", [NB, 2]), sb("unit_root", [NB, 2])
        hT = sb("hT", [P, CH, GN])
        r, alpha, left = sb("r", [P, GT, NB]), sb("alpha", [P, GT, NB]), sb("left", [P, GT, NB])
        top, total, tanh, rtotal = sb("top", [P, GT, TOP]), sb("total", [P, GT]), sb("tanh", [P, GT]), sb("rtotal", [P, GT])
        phi, coef, picked, pickedT = sb("phi", [P, GT, NB]), sb("coef", [P, GT]), sb("picked", [P, GT, NB]), sb("pickedT", [NB, GN])
        steps, turned, read = signals(nc, ctx, "unit_steps unit_turned unit_read")
        sems = signals(nc, ctx, "widened gelu_done logits clipped exped alpha_ready top_ready left_ready phi_ready "
                                "total_ready tanh_ready eps_added coef_part coef_ready latent picked_part picked_ready "
                                "picked_turned picked_copied out_ready added")
        (widened, gelu_done, logits, clipped, exped, alpha_ready, top_ready, left_ready, phi_ready, total_ready,
         tanh_ready, eps_added, coef_part, coef_ready, latent, picked_part, picked_ready, picked_turned,
         picked_copied, out_ready, added) = sems
        sems = ln.sems + ln2.sems + [steps, turned, read] + sems

        with nc.Block() as block:
            @block.sync
            def _(sp):
                sp.wait_ge(w["loaded"], w["total"])
        with nc.Block() as block:
            @block.scalar
            def _(act):
                act.preload_act_table_set(EXP_LN)
                for n, name in enumerate(("U", "V")):
                    act.activation(sq[:, n, :], w[name][:], ACT.Square).then_inc(steps, 1)
                act.wait_ge(steps, 4)
                act.activation(root[:], ss[:], ACT.Ln).then_inc(steps, 1)
                act.wait_ge(steps, 5)
                act.activation(ss[:], root[:], ACT.Exp, scale=-0.5).then_inc(steps, 1)

            @block.vector
            def _(dve):
                dve.wait_ge(steps, 2)
                dve.tensor_reduce(ss[:], sq[:], AX_X, ALU.add).then_inc(steps, 1)
                dve.wait_ge(steps, 3)
                dve.tensor_scalar(ss[:], ss[:], EPS * EPS, None, ALU.max).then_inc(steps, 1)
                dve.wait_ge(steps, 6)
                for n, name in enumerate(("U", "V")):
                    dve.tensor_scalar(rows[:, n, :], w[name][:], ss[:, n:n + 1], None, ALU.mult).then_inc(steps, 1)
                dve.wait_ge(steps, 8)
                dve.tensor_tensor(vg[:], rows[:, 1, :], w["gamma"][:], ALU.mult).then_inc(read, 1)
                dve.wait_ge(turned, 1)
                dve.tensor_copy(unT[:], banks[:, 0, 0:NB]).then_inc(read, 1)

            @block.tensor
            def _(pe):
                pe.wait_ge(steps, 7)
                pe.transpose(banks[:, 0, 0:NB], rows[:, 0, :], consts["ident"][0:NB, 0:NB]).then_inc(turned, 1)
        restart(nc, sems)

        with nc.Fori(0, GROUPS) as g:
            xg = x[:, bass.ds(g * GT, GT), :]
            with nc.Block() as block:
                @block.tensor
                def _(pe):
                    ln.tensor(pe)
                    pe.wait_ge(ln.ready, 1)
                    for t in range(GT):
                        last = pe.matmul(banks[:, 5, t * NB:(t + 1) * NB], ln.xnT[:, t * P:(t + 1) * P], unT[:],
                                         start=True, stop=True)
                    last.then_inc(latent, 1)
                    for c in range(2):
                        pe.matmul(banks[:, c, :], w["W1T"][:, c * P:(c + 1) * P], ln.xnT[:], start=True, stop=True)\
                            .then_inc(widened, 1)
                    ln2.tensor(pe)
                    pe.wait_ge(ln2.ready, 1)
                    for t in range(GT):
                        o = banks[:, 4, t * NB:(t + 1) * NB]
                        pe.matmul(o, ln2.xnT[:, t * P:(t + 1) * P], w["RT"][:], start=True, stop=False)
                        last = pe.matmul(o, consts["ones"][0:1, 0:P], w["rb"][:], start=False, stop=True)
                    last.then_inc(logits, 1)
                    for c in range(2, CH):
                        pe.wait_ge(gelu_done, c - 1)
                        pe.matmul(banks[:, c % 2, :], w["W1T"][:, c * P:(c + 1) * P], ln.xnT[:], start=True, stop=True)\
                            .then_inc(widened, 1)
                    for t in range(GT):
                        pe.wait_ge(picked_ready, 1)
                        last = pe.transpose(banks[0:NB, 6, t * P:(t + 1) * P], picked[:, t, :], consts["ident"])
                    last.then_inc(picked_turned, 1)
                    pe.wait_ge(gelu_done, CH)
                    pe.wait_ge(picked_copied, 1)
                    for t in range(GT):
                        o = banks[:, 7, t * P:(t + 1) * P]
                        for c in range(CH):
                            pe.matmul(o, hT[:, c, t * P:(t + 1) * P], w["W2T"][:, c, :], start=(c == 0), stop=False)
                        last = pe.matmul(o, pickedT[:, t * P:(t + 1) * P], vg[:], start=False, stop=True)
                    last.then_inc(out_ready, 1)

                @block.scalar
                def _(act):
                    act.preload_act_table_set(EXP_LN)
                    ln.scalar(act)
                    ln2.scalar(act, copy=False)
                    act.wait_ge(ln2.turned, GT)
                    act.activation(ln2.xnT[:], banks[:, 3, :], ACT.Identity, bias=w["ln_b"][:], scale=w["ln_g"][:])\
                        .then_inc(ln2.ready, 1)
                    act.wait_ge(clipped, 1)
                    act.activation(r[:], r[:], ACT.Exp).then_inc(exped, 1)
                    act.wait_ge(exped, 1)
                    act.activation(alpha[:], r[:], ACT.Ln, bias=1.0).then_inc(alpha_ready, 1)
                    for c in range(CH):
                        act.wait_ge(widened, c + 1)
                        act.activation(hT[:, c, :], banks[:, c % 2, :], ACT.Gelu).then_inc(gelu_done, 1)
                    act.wait_ge(total_ready, 1)
                    act.activation(tanh[:], total[:], ACT.Tanh).then_inc(tanh_ready, 1)
                    act.wait_ge(picked_turned, 1)
                    act.copy(pickedT[:], banks[0:NB, 6, :]).then_inc(picked_copied, 1)

                @block.vector
                def _(dve):
                    ln.vector(dve, xg)
                    dve.wait_ge(ln.normed, GT)
                    ln2.vector(dve, ln.xn)
                    dve.wait_ge(logits, 1)
                    dve.tensor_scalar(r[:], banks[:, 4, 0:GT * NB].rearrange("p (t n) -> p t n", n=NB), -TAU, TAU,
                                      ALU.max, ALU.min).then_inc(clipped, 1)
                    dve.wait_ge(alpha_ready, 1)
                    for t in range(GT):
                        dve.max(top[:, t, :], alpha[:, t, :]).then_inc(top_ready, 1)
                    dve.wait_ge(top_ready, GT)
                    for t in range(GT):
                        dve.match_replace(left[:, t, :], top[:, t, :], alpha[:, t, :], -1.0).then_inc(left_ready, 1)
                    dve.tensor_reduce(total[:], top[:], AX_X, ALU.add).then_inc(total_ready, 1)
                    dve.wait_ge(left_ready, GT)
                    dve.scalar_tensor_tensor(phi[:], left[:], 0.0, alpha[:], ALU.is_lt, ALU.mult).then_inc(phi_ready, 1)
                    dve.wait_ge(total_ready, 1)
                    dve.tensor_scalar(rtotal[:], total[:], EPS, None, ALU.add).then_inc(eps_added, 1)
                    dve.wait_ge(eps_added, 1)
                    dve.reciprocal(coef[:], rtotal[:]).then_inc(coef_part, 1)
                    dve.wait_ge(coef_part, 1)
                    dve.wait_ge(tanh_ready, 1)
                    dve.tensor_tensor(coef[:], coef[:], tanh[:], ALU.mult).then_inc(coef_ready, 1)
                    dve.wait_ge(phi_ready, 1)
                    dve.wait_ge(latent, 1)
                    dve.tensor_tensor(picked[:], phi[:], banks[:, 5, 0:GT * NB].rearrange("p (t n) -> p t n", n=NB),
                                      ALU.mult).then_inc(picked_part, 1)
                    dve.wait_ge(coef_ready, 1)
                    dve.wait_ge(picked_part, 1)
                    dve.tensor_tensor(picked[:], picked[:], spread(coef[:], NB), ALU.mult).then_inc(picked_ready, 1)
                    dve.wait_ge(out_ready, 1)
                    dve.tensor_tensor(xg, xg, banks[:, 7, :].rearrange("p (t d) -> p t d", d=D), ALU.add)\
                        .then_inc(added, 1)
            restart(nc, sems)


def cosine_attention(nc, x, banks, consts, w):
    HALF = INNER // 2
    UP = 2.0 ** 32
    with ExitStack() as ctx:
        sb = lambda n, s: ctx.enter_context(nc.sbuf_tensor("cosine_" + n, s, F32))
        ln = LayerNorm(nc, ctx, consts, banks[:, 7, :], "cosine_ln")
        peak, npeak = sb("peak", [P, H]), sb("npeak", [P, H])
        raw = sb("raw", [P, 2, GT, INNER])
        sq = sb("sq", [P, 2, HALF])
        ss, lg, inv = sb("ss", [P, 2, GT, H]), sb("lg", [P, 2, GT, H]), sb("inv", [P, 2, GT, H])
        turned_qk = sb("turned_qk", [P, 2, 2, GN])
        probs = sb("probs", [P, 2, GB, ST * SEQ])
        v1 = sb("v1", [P, GT, H, HD + 1])
        rden = sb("rden", [P, 2, GT])
        y = sb("y", [P, 2, GT, D])
        yT = lambda j: raw[:, 0, :, j * P:(j + 1) * P]
        sems = signals(nc, ctx, "projected squared copied reduced clamped logged rooted scaled unit_v unit_g qk_turned "
                                "qk_copied scored exped summed rden_ready head_done v_copied y_turned y_copied "
                                "out_ready added peak_ready npeak_ready")
        (projected, squared, copied, reduced, clamped, logged, rooted, scaled, unit_v, unit_g, qk_turned, qk_copied,
         scored, exped, summed, rden_ready, head_done, v_copied, y_turned, y_copied, out_ready, added, peak_ready,
         npeak_ready) = sems
        sems = ln.sems + sems
        QK = 4 * GT
        POOL_UNITS = 2

        with nc.Block() as block:
            @block.sync
            def _(sp):
                sp.wait_ge(w["loaded"], w["total"])
        with nc.Block() as block:
            @block.scalar
            def _(act):
                act.preload_act_table_set(EXP_LN)
                act.activation(peak[:], w["scale"][:], ACT.Exp).then_inc(peak_ready, 1)

            @block.vector
            def _(dve):
                dve.memset(v1[:, :, :, HD:HD + 1], 1.0)
                dve.wait_ge(peak_ready, 1)
                dve.tensor_scalar(npeak[:], peak[:], -1.0, None, ALU.mult).then_inc(npeak_ready, 1)
        restart(nc, sems)

        with nc.Fori(0, GROUPS) as g:
            xg = x[:, bass.ds(g * GT, GT), :]
            with nc.Block() as block:
                @block.tensor
                def _(pe):
                    ln.tensor(pe)
                    pe.wait_ge(ln.ready, 1)
                    for n in range(QK + 2 * GT):
                        if 4 <= n < QK + 4:
                            pe.wait_ge(copied, n - 3)
                        elif n >= QK + 4:
                            pe.wait_ge(v_copied, n - QK - 3)
                        t, m, half = (n // 4, n // 2 % 2, n % 2) if n < QK else ((n - QK) // 2, 2, n % 2)
                        c = m * INNER + half * HALF
                        pe.matmul(banks[:, n % 4, :], ln.xnT[:, t * P:(t + 1) * P], w["Wqkv"][:, c:c + HALF],
                                  start=True, stop=True).then_inc(projected, 1)

                    def turn_qk(j):
                        if j:
                            pe.wait_ge(qk_copied, 2 * j)
                        for m in range(2):
                            for t in range(GT):
                                if j == 0:
                                    u = m * GT + t
                                    if u < POOL_UNITS:
                                        pe.wait_ge(unit_g, u + 1)
                                    else:
                                        pe.wait_ge(unit_v, u - POOL_UNITS + 1)
                                last = pe.transpose(banks[:, 4 + m, t * P:(t + 1) * P],
                                                    raw[:, m, t, j * P:(j + 1) * P], consts["ident"])
                            last.then_inc(qk_turned, 1)

                    def score(h):
                        pe.wait_ge(qk_copied, 2 * (h // 2) + 2)
                        if h == 0:
                            pe.wait_ge(v_copied, 2 * GT)
                        if h >= 2:
                            pe.wait_ge(exped, GB * (h - 1))
                        lo = HD * (h % 2)
                        q, k = (turned_qk[lo:lo + HD, h // 2 % 2, m, :] for m in range(2))
                        for b in range(GB):
                            for s in range(ST):
                                c = b * SEQ
                                last = pe.matmul(banks[:, 2 * (h % 2) + b, s * SEQ:(s + 1) * SEQ],
                                                 k[:, c + s * P:c + (s + 1) * P], q[:, c:c + SEQ], start=True, stop=True)
                            last.then_inc(scored, 1)

                    def values(h):
                        pe.wait_ge(exped, GB * (h + 1))
                        if h:
                            pe.wait_ge(head_done, h)
                        for b in range(GB):
                            for i in range(ST):
                                o = banks[:, 6, (b * ST + i) * (HD + 1):(b * ST + i + 1) * (HD + 1)]
                                for s in range(ST):
                                    c = s * SEQ + i * P
                                    last = pe.matmul(o, probs[:, h % 2, b, c:c + P], v1[:, b * ST + s, h, :],
                                                     start=(s == 0), stop=(s == ST - 1))
                        last.then_inc(summed, 1)

                    def turn_y(j):
                        pe.wait_ge(head_done, 2 * j + 2)
                        if j:
                            pe.wait_ge(y_copied, j)
                        for t in range(GT):
                            last = pe.transpose(banks[:, 7, t * P:(t + 1) * P], y[:, j % 2, t, :],
                                                consts["ident"])
                        last.then_inc(y_turned, 1)

                    for i in range(H + 4):
                        if i % 2 == 0 and i < H:
                            turn_qk(i // 2)
                        if 1 <= i <= H:
                            score(i - 1)
                        if 2 <= i <= H + 1:
                            values(i - 2)
                        if i >= 4 and i % 2 == 0:
                            turn_y((i - 4) // 2)
                    pe.wait_ge(y_copied, PAIRS)
                    for t in range(GT):
                        o = banks[:, 4, t * P:(t + 1) * P]
                        for j in range(PAIRS):
                            pe.matmul(o, yT(j)[:, t, :], w["Wo"][:, j, :], start=(j == 0), stop=False)
                        last = pe.matmul(o, consts["ones"][0:1, 0:P], w["bo"][:], start=False, stop=True)
                    last.then_inc(out_ready, 1)

                @block.scalar
                def _(act):
                    ln.scalar(act)
                    for n in range(QK):
                        act.wait_ge(copied, n + 1)
                        if n >= 2:
                            act.wait_ge(reduced, n - 1)
                        t, m, half = n // 4, n // 2 % 2, n % 2
                        act.activation(sq[:, n % 2, :], raw[:, m, t, half * HALF:(half + 1) * HALF], ACT.Square)\
                            .then_inc(squared, 1)
                    for n in range(2 * GT):
                        act.wait_ge(projected, QK + n + 1)
                        act.copy(v1[:, n // 2, (n % 2) * PAIRS:(n % 2 + 1) * PAIRS, 0:HD],
                                 banks[:, n % 4, :].rearrange("p (h d) -> p h d", d=HD)).then_inc(v_copied, 1)
                        if n == 3:
                            act.wait_ge(clamped, 1)
                            act.activation(lg[:], ss[:], ACT.Ln).then_inc(logged, 1)
                            act.wait_ge(logged, 1)
                            act.activation(inv[:], lg[:], ACT.Exp, scale=-0.5).then_inc(rooted, 1)

                    def copy_qk(j):
                        for m in range(2):
                            act.wait_ge(qk_turned, 2 * j + m + 1)
                            if j >= 2:
                                act.wait_ge(scored, 2 * GB * (j - 1))
                            act.copy(turned_qk[:, j % 2, m, :], banks[:, 4 + m, :]).then_inc(qk_copied, 1)

                    def exp(h):
                        for b in range(GB):
                            act.wait_ge(scored, GB * h + b + 1)
                            if h >= 2:
                                act.wait_ge(summed, h - 1)
                            act.activation(probs[:, h % 2, b, :], banks[:, 2 * (h % 2) + b, :], ACT.Exp,
                                           bias=npeak[:, h:h + 1], scale=peak[:, h:h + 1]).then_inc(exped, 1)

                    for i in range(H + 1):
                        if i % 2 == 0 and i < H:
                            copy_qk(i // 2)
                        if i >= 1:
                            exp(i - 1)

                @block.gpsimd
                def _(pool):
                    pool.wait_ge(scaled, 1)
                    pool.wait_ge(copied, QK)
                    for u in range(POOL_UNITS):
                        a = raw[:, u // GT, u % GT, :].rearrange("p (h d) -> p h d", d=HD)
                        pool.tensor_tensor(a, a, spread(inv[:, u // GT, u % GT, :], HD), ALU.mult).then_inc(unit_g, 1)

                @block.vector
                def _(dve):
                    ln.vector(dve, xg)

                    def reduce(n):
                        t, m, half = n // 4, n // 2 % 2, n % 2
                        dve.wait_ge(squared, n + 1)
                        dve.tensor_reduce(ss[:, m, t, half * PAIRS:(half + 1) * PAIRS],
                                          sq[:, n % 2, :].rearrange("p (h d) -> p h d", d=HD), AX_X, ALU.add)\
                            .then_inc(reduced, 1)

                    for n in range(QK):
                        t, m, half = n // 4, n // 2 % 2, n % 2
                        dve.wait_ge(projected, n + 1)
                        dve.tensor_copy(raw[:, m, t, half * HALF:(half + 1) * HALF], banks[:, n % 4, :]).then_inc(copied, 1)
                        if n:
                            reduce(n - 1)
                    reduce(QK - 1)
                    dve.wait_ge(reduced, QK)
                    dve.tensor_scalar(ss[:], ss[:], 1e-24, UP, ALU.max, ALU.mult).then_inc(clamped, 1)
                    dve.wait_ge(rooted, 1)
                    dve.tensor_scalar(inv[:], inv[:], UP ** 0.5, None, ALU.mult).then_inc(scaled, 1)
                    dve.wait_ge(scaled, 1)
                    dve.wait_ge(copied, QK)
                    for u in range(POOL_UNITS, 2 * GT):
                        a = raw[:, u // GT, u % GT, :].rearrange("p (h d) -> p h d", d=HD)
                        dve.tensor_tensor(a, a, spread(inv[:, u // GT, u % GT, :], HD), ALU.mult).then_inc(unit_v, 1)
                    for h in range(H):
                        dve.wait_ge(summed, h + 1)
                        o = banks[:, 6, 0:GT * (HD + 1)].rearrange("p (t e) -> p t e", e=HD + 1)
                        dve.reciprocal(rden[:, h % 2, :], o[:, :, HD]).then_inc(rden_ready, 1)
                        dve.wait_ge(rden_ready, h + 1)
                        if h >= 4:
                            dve.wait_ge(y_turned, h // 2 - 1)
                        dve.tensor_tensor(y[:, h // 2 % 2, :, h % 2 * HD:(h % 2 + 1) * HD], o[:, :, 0:HD], spread(rden[:, h % 2, :], HD),
                                          ALU.mult).then_inc(head_done, 1)
                        if h % 2:
                            j = h // 2
                            dve.wait_ge(y_turned, j + 1)
                            dve.tensor_copy(yT(j), banks[:, 7, :].rearrange("p (t d) -> p t d", d=D)).then_inc(y_copied, 1)
                    dve.wait_ge(out_ready, 1)
                    dve.tensor_tensor(xg, xg, banks[:, 4, :].rearrange("p (t d) -> p t d", d=D), ALU.add)\
                        .then_inc(added, 1)
            restart(nc, sems)


def int4_linear(nc, x, banks, consts, w):
    RANK, QMAX = 16, 7.0
    ROUND = 1.5 * 2.0 ** 23
    with ExitStack() as ctx:
        sb = lambda n, s: ctx.enter_context(nc.sbuf_tensor("int4_" + n, s, F32))
        ln = LayerNorm(nc, ctx, consts, banks[:, 2, :], "int4_ln")
        rowmax, allmax, step, rstep = sb("rowmax", [P, 1]), sb("allmax", [P, 1]), sb("step", [P, 1]), sb("rstep", [P, 1])
        wq, low = sb("wq", [P, D]), sb("low", [RANK, GN])
        quant, quant_max = signals(nc, ctx, "quant_steps quant_max")
        sems = signals(nc, ctx, "low_ready low_copied out_ready added")
        low_ready, low_copied, out_ready, added = sems
        sems = ln.sems + [quant, quant_max] + sems

        with nc.Block() as block:
            @block.sync
            def _(sp):
                sp.wait_ge(w["loaded"], w["total"])
        with nc.Block() as block:
            @block.vector
            def _(dve):
                dve.tensor_reduce(rowmax[:], w["kernel"][:], AX_X, ALU.max, apply_absolute_value=True).then_inc(quant, 1)
                dve.wait_ge(quant_max, 1)
                dve.tensor_scalar(step[:], allmax[:], 1.0 / QMAX, None, ALU.mult).then_inc(quant, 1)
                dve.wait_ge(quant, 2)
                dve.reciprocal(rstep[:], step[:]).then_inc(quant, 1)
                dve.wait_ge(quant, 3)
                dve.tensor_scalar(wq[:], w["kernel"][:], rstep[:], None, ALU.mult).then_inc(quant, 1)
                dve.wait_ge(quant, 4)
                dve.tensor_scalar(wq[:], wq[:], ROUND, None, ALU.add).then_inc(quant, 1)
                dve.wait_ge(quant, 5)
                dve.tensor_scalar(wq[:], wq[:], -ROUND, None, ALU.add).then_inc(quant, 1)
                dve.wait_ge(quant, 6)
                dve.tensor_scalar(wq[:], wq[:], -8.0, 7.0, ALU.max, ALU.min).then_inc(quant, 1)
                dve.wait_ge(quant, 7)
                dve.tensor_scalar(wq[:], wq[:], step[:], None, ALU.mult).then_inc(quant, 1)

            @block.gpsimd
            def _(pool):
                pool.wait_ge(quant, 1)
                pool.partition_all_reduce(allmax[:], rowmax[:], P, bass.bass_isa.ReduceOp.max).then_inc(quant_max, 1)

            @block.scalar
            def _(act):
                act.preload_act_table_set(EXP_LN)
        restart(nc, sems)

        with nc.Fori(0, GROUPS) as g:
            xg = x[:, bass.ds(g * GT, GT), :]
            with nc.Block() as block:
                @block.tensor
                def _(pe):
                    ln.tensor(pe)
                    pe.wait_ge(ln.ready, 1)
                    pe.matmul(banks[0:RANK, 0, :], w["a"][:], ln.xnT[:], start=True, stop=True).then_inc(low_ready, 1)
                    pe.wait_ge(low_copied, 1)
                    for t in range(GT):
                        o, c = banks[:, 1, t * P:(t + 1) * P], slice(t * P, (t + 1) * P)
                        pe.matmul(o, ln.xnT[:, c], wq[:], start=True, stop=False)
                        pe.matmul(o, low[:, c], w["b"][:], start=False, stop=False)
                        last = pe.matmul(o, consts["ones"][0:1, 0:P], w["bias"][:], start=False, stop=True)
                    last.then_inc(out_ready, 1)

                @block.scalar
                def _(act):
                    ln.scalar(act)
                    act.wait_ge(low_ready, 1)
                    act.copy(low[:], banks[0:RANK, 0, :]).then_inc(low_copied, 1)

                @block.vector
                def _(dve):
                    ln.vector(dve, xg)
                    dve.wait_ge(out_ready, 1)
                    dve.tensor_tensor(xg, xg, banks[:, 1, :].rearrange("p (t d) -> p t d", d=D), ALU.add)\
                        .then_inc(added, 1)
            restart(nc, sems)


def state_space(nc, x, banks, consts, w):
    INNER_D, NS, RANK = 256, 16, 8
    SPLIT = 3 * 32
    CH = INNER_D // P
    with ExitStack() as ctx:
        sb = lambda n, s, d=F32: ctx.enter_context(nc.sbuf_tensor("mamba_" + n, s, d))
        ln = LayerNorm(nc, ctx, consts, banks[:, 0, :], "mamba_ln")
        a_neg = sb("a_neg", [P, CH, NS])
        xs_of, gate_of, delta_of, dx_of = (sb(n, [P, 2, CH, GN]) for n in ("xs", "gate", "delta", "dx"))
        whole = sb("b_and_c", [SPLIT, 2, GN])
        parts_of = sb("parts", [SPLIT, 2, 2, GN], BF16)
        pick = sb("pick", [SPLIT, NS * P], BF16)
        v = sb("dt_in", [P, CH, GN])
        dp = ln.xn[0:RANK].rearrange("p t d -> p (t d)")
        decay, drive, state = (sb(n, [P, 2, CH, GN]) for n in ("decay", "drive", "state"))
        seen = sb("seen", [P, 3, CH, GN])
        c_wide = sb("c_wide", [P, 2, GN])
        rows = drive[0:SPLIT].rearrange("p a c n -> p (a c n)")
        prep, pick_loaded = signals(nc, ctx, "prep pick_loaded")
        sems = signals(nc, ctx, "widened xs_ready gate_ready lowered dp_biased whole_ready high_part rest middle_part "
                                "low_part dt_ready dt_biased mag_ready mag_exp mag_log delta_ready dx_ready b_spread "
                                "c_spread c_copied decayed driven scanned read_out gathered skip_added gated out_ready added")
        (widened, xs_ready, gate_ready, lowered, dp_biased, whole_ready, high_part, rest, middle_part, low_part,
         dt_ready, dt_biased, mag_ready, mag_exp, mag_log, delta_ready, dx_ready, b_spread, c_spread, c_copied, decayed,
         driven, scanned, read_out, gathered, skip_added, gated, out_ready, added) = sems
        sems = ln.sems + [prep] + sems

        with nc.Block() as block:
            @block.sync
            def _(sp):
                sp.wait_ge(w["loaded"], w["total"])
                sp.dma_start(rows, w["pick"]).then_inc(pick_loaded, 16)
                sp.wait_ge(pick_loaded, 16)
        with nc.Block() as block:
            @block.scalar
            def _(act):
                act.preload_act_table_set(EXP_LN)
                act.activation(a_neg[:], w["A_log"][:], ACT.Exp).then_inc(prep, 1)

            @block.vector
            def _(dve):
                dve.wait_ge(prep, 1)
                dve.tensor_scalar(a_neg[:], a_neg[:], -1.0, None, ALU.mult).then_inc(prep, 1)
                dve.tensor_copy(pick[:], rows)
                for r in range(2):
                    for c in range(CH):
                        for b in range(GB):
                            dve.memset(decay[:, r, c, b * SEQ:b * SEQ + 1], 0.0)
        restart(nc, sems)

        MEASURE, NORMALIZE, TURN, TURNED, WIDEN, SILU, LOWER, BIAS, LOWER_C, BIAS_C, LAST_DT, SPLIT_ALL, SOFTPLUS, DELTA = \
            0, 1, 2, 3, 4, 4, 6, 7, 8, 9, 10, 11, 12, 13

        def step(scan_of, make_of, parity):
            S, A = scan_of is not None, make_of is not None
            xg = x[:, bass.ds(scan_of * GT, GT), :] if S else None
            xa = x[:, bass.ds(make_of * GT, GT), :] if A else None
            xs, gate, delta, dx = (a[:, parity] for a in (xs_of, gate_of, delta_of, dx_of))
            xs_new, gate_new, delta_new, dx_new = (a[:, 1 - parity] for a in (xs_of, gate_of, delta_of, dx_of))
            yT = xs
            mag = delta_new
            parts, parts_new = parts_of[:, parity], parts_of[:, 1 - parity]

            with nc.Block() as block:
                @block.tensor
                def _(pe):
                    def lower(n):
                        name, lo, m = (("Wdp", 0, RANK), ("Wbc", 0, SPLIT), ("Wbc", SPLIT, SPLIT))[n]
                        for c in range(CH):
                            last = pe.matmul(banks[0:m, n % 2, :], w[name][:, c, lo:lo + m], xs_new[:, c, :],
                                             start=(c == 0), stop=(c == CH - 1))
                        last.then_inc(lowered, 1)

                    def dt(c):
                        pe.matmul(banks[:, 1 - c, :], w["Wdt"][:, c * P:(c + 1) * P], dp, start=True, stop=True)\
                            .then_inc(dt_ready, 1)

                    def make(n):
                        if n == TURN:
                            ln.tensor(pe)
                        if n == WIDEN:
                            pe.wait_ge(ln.ready, 1)
                            for c in range(2 * CH):
                                if c >= 2:
                                    pe.wait_ge(xs_ready, c - 1)
                                pe.matmul(banks[:, c % 2, :], w["Win"][:, c * P:(c + 1) * P], ln.xnT[:], start=True, stop=True)\
                                    .then_inc(widened, 1)
                        if n == LOWER:
                            pe.wait_ge(xs_ready, CH)
                            pe.wait_ge(gate_ready, CH)
                            lower(0)
                            lower(1)
                        if n == LOWER_C:
                            pe.wait_ge(dp_biased, 1)
                            lower(2)
                            pe.wait_ge(whole_ready, 1)
                            dt(0)
                        if n == LAST_DT:
                            pe.wait_ge(whole_ready, 2)
                            dt(1)

                    def gather(n):
                        pe.wait_ge(read_out, n + 1)
                        for c in range(CH):
                            last = pe.matmul(banks[:, 6 + c, :], consts["ident"], seen[:, n % 3, c, :],
                                             start=(n == 0), stop=(n == NS - 1))
                        last.then_inc(gathered, 1)

                    for n in range(NS):
                        if S:
                            row = pick[:, n * P:(n + 1) * P]
                            if n >= 2:
                                pe.wait_ge(driven, n - 1)
                            pe.matmul(banks[:, 2 + n % 2, :], row, parts[:, 0, :], start=True, stop=True).then_inc(b_spread, 1)
                            if n >= 2:
                                pe.wait_ge(c_copied, n - 1)
                            pe.matmul(banks[:, 4 + n % 2, :], row, parts[:, 1, :], start=True, stop=True).then_inc(c_spread, 1)
                            if n >= 2:
                                gather(n - 2)
                        if A:
                            make(n)
                    if S:
                        gather(NS - 2)
                        gather(NS - 1)
                        if A:
                            pe.wait_ge(dt_biased, CH)
                        pe.wait_ge(gated, CH)
                        for t in range(GT):
                            o = banks[:, 0, t * P:(t + 1) * P]
                            for c in range(CH):
                                pe.matmul(o, yT[:, c, t * P:(t + 1) * P], w["Wout"][:, c, :], start=(c == 0), stop=False)
                            last = pe.matmul(o, consts["ones"][0:1, 0:P], w["bout"][:], start=False, stop=True)
                        last.then_inc(out_ready, 1)

                @block.scalar
                def _(act):
                    def make(n):
                        if n == MEASURE:
                            ln.root(act)
                        if n == TURNED:
                            ln.copy(act)
                        if n == SILU:
                            for c in range(2 * CH):
                                into, ready = (xs_new, xs_ready) if c < CH else (gate_new, gate_ready)
                                act.wait_ge(widened, c + 1)
                                act.activation(into[:, c % CH, :], banks[:, c % 2, :], ACT.Silu, bias=w["bin"][:, c:c + 1])\
                                    .then_inc(ready, 1)
                            act.preload_act_table_set(EXP_LN)
                        if n == SOFTPLUS:
                            act.wait_ge(dt_biased, CH)
                            act.activation(mag[:], v[:], ACT.Abs).then_inc(mag_ready, 1)
                            act.wait_ge(mag_ready, 1)
                            act.activation(mag[:], mag[:], ACT.Exp, scale=-1.0).then_inc(mag_exp, 1)
                            act.wait_ge(mag_exp, 1)
                            act.activation(mag[:], mag[:], ACT.Ln, bias=1.0).then_inc(mag_log, 1)

                    for n in range(NS):
                        if S:
                            if n >= 2:
                                act.wait_ge(scanned, CH * (n - 1))
                            for c in range(CH):
                                into = decay[:, n % 2, c, :].rearrange("p (b s) -> p b s", s=SEQ)[:, :, 1:]
                                act.activation(into, delta[:, c, :].rearrange("p (b s) -> p b s", s=SEQ)[:, :, 1:], ACT.Exp,
                                               scale=a_neg[:, c, n:n + 1]).then_inc(decayed, 1)
                            act.wait_ge(c_spread, n + 1)
                            if n >= 2:
                                act.wait_ge(read_out, n - 1)
                            act.copy(c_wide[:, n % 2, :], banks[:, 4 + n % 2, :]).then_inc(c_copied, 1)
                        if A:
                            make(n)

                @block.gpsimd
                def _(pool):
                    for n in range(NS if S else 0):
                        pool.wait_ge(scanned, CH * (n + 1))
                        pool.wait_ge(c_copied, n + 1)
                        if n >= 3:
                            pool.wait_ge(gathered, n - 2)
                        pool.tensor_tensor(seen[:, n % 3, :, :], state[:, n % 2, :, :],
                                           c_wide[:, n % 2:n % 2 + 1, :].broadcast_to([P, CH, GN]), ALU.mult)\
                            .then_inc(read_out, 1)

                @block.vector
                def _(dve):
                    def bias_whole(n):
                        dve.wait_ge(lowered, n + 2)
                        dve.tensor_scalar(whole[:, n, :], banks[0:SPLIT, 1 - n, :], w["bbc"][:, n:n + 1], None, ALU.add)\
                            .then_inc(whole_ready, 1)

                    def bias_dt(c):
                        dve.wait_ge(dt_ready, c + 1)
                        dve.tensor_scalar(v[:, c, :], banks[:, 1 - c, :], w["bdt"][:, c:c + 1], None, ALU.add).then_inc(dt_biased, 1)

                    def make(n):
                        if n == MEASURE:
                            ln.gather_moments(dve, xa)
                        if n == NORMALIZE:
                            ln.normalize(dve, xa)
                        if n == BIAS:
                            dve.wait_ge(lowered, 1)
                            dve.tensor_scalar(dp, banks[0:RANK, 0, :], w["bdp"][:], None, ALU.add).then_inc(dp_biased, 1)
                            bias_whole(0)
                        if n == BIAS_C:
                            bias_whole(1)
                            bias_dt(0)
                        if n == SPLIT_ALL:
                            bias_dt(1)
                            dve.tensor_copy(parts_new, whole[:]).then_inc(high_part, 1)
                            for lo, hi in ((32, 64), (64, SPLIT)):
                                dve.wait_ge(high_part, 1)
                                dve.tensor_tensor(whole[lo:hi], whole[lo:hi], parts_new[lo:hi], ALU.subtract).then_inc(rest, 1)
                            for m, (lo, hi) in enumerate(((32, 64), (64, SPLIT))):
                                dve.wait_ge(rest, m + 1)
                                dve.tensor_copy(parts_new[lo:hi], whole[lo:hi]).then_inc(middle_part, 1)
                            dve.wait_ge(middle_part, 2)
                            dve.tensor_tensor(parts_new[64:SPLIT], whole[64:SPLIT], parts_new[64:SPLIT], ALU.subtract)\
                                .then_inc(low_part, 1)
                        if n == DELTA:
                            dve.wait_ge(mag_log, 1)
                            dve.scalar_tensor_tensor(delta_new, v[:], 0.0, mag[:], ALU.max, ALU.add).then_inc(delta_ready, 1)
                            dve.wait_ge(delta_ready, 1)
                            dve.wait_ge(xs_ready, CH)
                            dve.tensor_tensor(dx_new, delta_new, xs_new, ALU.mult).then_inc(dx_ready, 1)

                    for n in range(NS):
                        if S:
                            if n >= 2:
                                dve.wait_ge(scanned, CH * (n - 1))
                            dve.wait_ge(b_spread, n + 1)
                            dve.tensor_tensor(drive[:, n % 2, :, :], dx,
                                              banks[:, 2 + n % 2:3 + n % 2, :].broadcast_to([P, CH, GN]), ALU.mult)\
                                .then_inc(driven, 1)
                        if A:
                            make(n)
                        if S:
                            dve.wait_ge(driven, n + 1)
                            if n >= 2:
                                dve.wait_ge(read_out, n - 1)
                            for c in range(CH):
                                dve.wait_ge(decayed, CH * n + c + 1)
                                dve.tensor_tensor_scan(state[:, n % 2, c, :], decay[:, n % 2, c, :], drive[:, n % 2, c, :],
                                                       0.0, ALU.mult, ALU.add).then_inc(scanned, 1)
                    if S:
                        dve.wait_ge(gathered, NS)
                        for c in range(CH):
                            dve.scalar_tensor_tensor(yT[:, c, :], xs[:, c, :], w["Dp"][:, c:c + 1], banks[:, 6 + c, :],
                                                     ALU.mult, ALU.add).then_inc(skip_added, 1)
                            dve.wait_ge(skip_added, c + 1)
                            dve.tensor_tensor(yT[:, c, :], yT[:, c, :], gate[:, c, :], ALU.mult).then_inc(gated, 1)
                        dve.wait_ge(out_ready, 1)
                        dve.tensor_tensor(xg, xg, banks[:, 0, :].rearrange("p (t d) -> p t d", d=D), ALU.add)\
                            .then_inc(added, 1)
            restart(nc, sems)

        pipeline(nc, step)


def expert_ffn(nc, x, banks, consts, w):
    E, TOP, DFF, EPS = 8, 2, 512, 1e-8
    CH = DFF // P
    with ExitStack() as ctx:
        sb = lambda n, s, d=F32: ctx.enter_context(nc.sbuf_tensor("experts_" + n, s, d))
        ln = LayerNorm(nc, ctx, consts, banks[:, 7, :], "experts_ln")
        ln2 = LayerNorm(nc, ctx, consts, banks[:, 7, :], "experts_ln2")
        hT = sb("hT", [P, 2, CH, GN])
        peak, z, mass, rmass, prob = sb("peak", [P, GT]), sb("z", [P, GT, E]), sb("mass", [P, GT]), sb("rmass", [P, GT]), sb("prob", [P, GT, E])
        top, place, placef = sb("top", [P, GT, 8]), sb("place", [P, GT, 8], U32), sb("placef", [P, GT, 8])
        pair, rpair, share = sb("pair", [P, GT]), sb("rpair", [P, GT]), sb("share", [P, GT, TOP])
        part, weight, weightT = sb("part", [P, TOP, GT, E]), sb("weight", [P, GT, E]), sb("weightT", [E, GN])
        acc = sb("acc", [P, GT, D])
        sems = signals(nc, ctx, "logits peak_ready centred exped mass_ready rmass_ready prob_ready top_ready placed "
                                "place_copied pair_sum pair_eps rpair_ready share_ready parted weighted w_turned "
                                "w_copied bias_ready acc_ready widened gelu_done narrowed taken scaled_out shifted added")
        (logits, peak_ready, centred, exped, mass_ready, rmass_ready, prob_ready, top_ready, placed, place_copied,
         pair_sum, pair_eps, rpair_ready, share_ready, parted, weighted, w_turned, w_copied, bias_ready, acc_ready,
         widened, gelu_done, narrowed, taken, scaled_out, shifted, added) = sems
        sems = ln.sems + ln2.sems + sems

        with nc.Block() as block:
            @block.sync
            def _(sp):
                sp.wait_ge(w["loaded"], w["total"])

        with nc.Fori(0, GROUPS) as g:
            xg = x[:, bass.ds(g * GT, GT), :]
            with nc.Block() as block:
                @block.tensor
                def _(pe):
                    ln.tensor(pe)
                    pe.wait_ge(ln.ready, 1)
                    for t in range(GT):
                        o = banks[:, 2, t * E:(t + 1) * E]
                        pe.matmul(o, ln.xnT[:, t * P:(t + 1) * P], w["Wg"][:], start=True, stop=False)
                        last = pe.matmul(o, consts["ones"][0:1, 0:P], w["bg"][:], start=False, stop=True)
                    last.then_inc(logits, 1)

                    def widen(e):
                        for c in range(CH):
                            n = e * CH + c
                            if n >= 2:
                                pe.wait_ge(gelu_done, n - 1)
                            pe.matmul(banks[:, n % 2, :], w["W1"][:, e, c * P:(c + 1) * P], ln.xnT[:], start=True,
                                      stop=True).then_inc(widened, 1)

                    def narrow(e):
                        pe.wait_ge(gelu_done, (e + 1) * CH)
                        if e >= 2:
                            pe.wait_ge(taken, GT * (e - 1))
                        for t in range(GT):
                            for c in range(CH):
                                last = pe.matmul(banks[:, 4 + e % 2, t * P:(t + 1) * P],
                                                 hT[:, e % 2, c, t * P:(t + 1) * P], w["W2"][:, e, c, :],
                                                 start=(c == 0), stop=(c == CH - 1))
                        last.then_inc(narrowed, 1)

                    for i in range(E + 1):
                        if i < E:
                            widen(i)
                        if i == 1:
                            pe.wait_ge(weighted, 1)
                            for t in range(GT):
                                last = pe.transpose(banks[0:E, 3, t * P:(t + 1) * P], weight[:, t, :], consts["ident"])
                            last.then_inc(w_turned, 1)
                            pe.wait_ge(w_copied, 1)
                            for t in range(GT):
                                last = pe.matmul(banks[:, 6, t * P:(t + 1) * P], weightT[:, t * P:(t + 1) * P],
                                                 w["b2"][:], start=True, stop=True)
                            last.then_inc(bias_ready, 1)
                        if i:
                            narrow(i - 1)

                @block.scalar
                def _(act):
                    act.preload_act_table_set(EXP_LN)
                    ln.scalar(act)
                    act.wait_ge(centred, 1)
                    act.activation(z[:], z[:], ACT.Exp).then_inc(exped, 1)
                    for n in range(E * CH):
                        e, c = n // CH, n % CH
                        act.wait_ge(widened, n + 1)
                        if e >= 2:
                            act.wait_ge(narrowed, e - 1)
                        act.activation(hT[:, e % 2, c, :], banks[:, n % 2, :], ACT.Gelu, bias=w["b1"][:, n:n + 1])\
                            .then_inc(gelu_done, 1)
                    act.preload_act_table_set(EXP_LN)
                    ln2.scalar(act, copy=False)

                @block.vector
                def _(dve):
                    ln.vector(dve, xg)
                    dve.wait_ge(logits, 1)
                    lo = banks[:, 2, 0:GT * E].rearrange("p (t e) -> p t e", e=E)
                    dve.tensor_reduce(peak[:], lo, AX_X, ALU.max).then_inc(peak_ready, 1)
                    dve.wait_ge(peak_ready, 1)
                    dve.tensor_tensor(z[:], lo, spread(peak[:], E), ALU.subtract).then_inc(centred, 1)
                    dve.wait_ge(exped, 1)
                    dve.tensor_reduce(mass[:], z[:], AX_X, ALU.add).then_inc(mass_ready, 1)
                    dve.wait_ge(mass_ready, 1)
                    dve.reciprocal(rmass[:], mass[:]).then_inc(rmass_ready, 1)
                    dve.wait_ge(rmass_ready, 1)
                    dve.tensor_tensor(prob[:], z[:], spread(rmass[:], E), ALU.mult).then_inc(prob_ready, 1)
                    dve.wait_ge(prob_ready, 1)
                    for t in range(GT):
                        dve.max(top[:, t, :], prob[:, t, :]).then_inc(top_ready, 1)
                    dve.wait_ge(top_ready, GT)
                    for t in range(GT):
                        dve.max_index(place[:, t, :], top[:, t, :], prob[:, t, :]).then_inc(placed, 1)
                    dve.tensor_reduce(pair[:], top[:, :, 0:TOP], AX_X, ALU.add).then_inc(pair_sum, 1)
                    dve.wait_ge(placed, GT)
                    dve.tensor_copy(placef[:], place[:]).then_inc(place_copied, 1)
                    dve.wait_ge(pair_sum, 1)
                    dve.tensor_scalar(pair[:], pair[:], EPS, None, ALU.add).then_inc(pair_eps, 1)
                    dve.wait_ge(pair_eps, 1)
                    dve.reciprocal(rpair[:], pair[:]).then_inc(rpair_ready, 1)
                    dve.wait_ge(rpair_ready, 1)
                    dve.tensor_tensor(share[:], top[:, :, 0:TOP], spread(rpair[:], TOP), ALU.mult).then_inc(share_ready, 1)
                    dve.wait_ge(share_ready, 1)
                    dve.wait_ge(place_copied, 1)
                    for r in range(TOP):
                        for t in range(GT):
                            dve.tensor_scalar(part[:, r, t, :], consts["count"], placef[:, t, r:r + 1],
                                              share[:, t, r:r + 1], ALU.is_equal, ALU.mult).then_inc(parted, 1)
                    dve.wait_ge(parted, TOP * GT)
                    dve.tensor_tensor(weight[:], part[:, 0, :, :], part[:, 1, :, :], ALU.add).then_inc(weighted, 1)
                    dve.wait_ge(w_turned, 1)
                    dve.tensor_copy(weightT[:], banks[0:E, 3, :]).then_inc(w_copied, 1)
                    dve.wait_ge(bias_ready, 1)
                    dve.tensor_copy(acc[:], banks[:, 6, :].rearrange("p (t d) -> p t d", d=D)).then_inc(acc_ready, 1)
                    dve.wait_ge(acc_ready, 1)
                    for e in range(E):
                        dve.wait_ge(narrowed, e + 1)
                        if e:
                            dve.wait_ge(taken, GT * e)
                        for t in range(GT):
                            dve.scalar_tensor_tensor(acc[:, t, :], banks[:, 4 + e % 2, t * P:(t + 1) * P],
                                                     weight[:, t, e:e + 1], acc[:, t, :], ALU.mult, ALU.add)\
                                .then_inc(taken, 1)
                    dve.wait_ge(taken, GT * E)
                    ln2.vector(dve, acc)
                    dve.wait_ge(ln2.normed, GT)
                    dve.tensor_tensor(acc[:], ln2.xn[:], w["gamma"][:].unsqueeze(1).broadcast_to([P, GT, D]), ALU.mult)\
                        .then_inc(scaled_out, 1)
                    dve.wait_ge(scaled_out, 1)
                    dve.tensor_tensor(acc[:], acc[:], w["beta"][:].unsqueeze(1).broadcast_to([P, GT, D]), ALU.add)\
                        .then_inc(shifted, 1)
                    dve.wait_ge(shifted, 1)
                    dve.tensor_tensor(xg, xg, acc[:], ALU.add).then_inc(added, 1)
            restart(nc, sems)


def gated_recurrence(nc, x, banks, consts, w):
    HEADS, HW, CHUNK, EPS = 2, 64, 64, 1e-5
    NC = GN // CHUNK
    SC = NC // GB
    with ExitStack() as ctx:
        sb = lambda n, s: ctx.enter_context(nc.sbuf_tensor("hgrn_" + n, s, F32))
        ln = LayerNorm(nc, ctx, consts, banks[:, 7, :], "hgrn_ln")
        ndelta = sb("ndelta", [P, 1])
        q, k, z, mag, logf, G = (sb("" + n, [P, GN]) for n in ("q", "k", "z", "mag", "logf", "G"))
        eG, enG = sb("eG", [P, GN]), sb("enG", [P, GN])
        low, sgate = sb("low", [HW, GN]), sb("sgate", [CHUNK, NC, D])
        vals, keys = sb("vals", [CHUNK, NC, D]), sb("keys", [CHUNK, NC, D])
        att = sb("att", [CHUNK, HEADS, NC, CHUNK])
        kv, S = sb("kv", [P, NC, D]), sb("S", [P, NC, D])
        o, osq, ms, lms, rms = sb("o", [CHUNK, NC, D]), sb("osq", [CHUNK, NC, D]), sb("ms", [CHUNK, NC * HEADS]), sb("lms", [CHUNK, NC * HEADS]), sb("rms", [CHUNK, NC * HEADS])
        oT = sb("oT", [P, GN])
        prep = signals(nc, ctx, "prep")[0]
        sems = signals(nc, ctx, "projected q_silu k_sigmoid z_biased low_copied v_ready v_copied gates gate_ready "
                                "mag_ready mag_exp mag_log logf_ready G_ready eG_ready enG_ready q_ready k_ready "
                                "keys_turned keys_copied att_ready att_masked kv_ready kv_scaled S_ready o_ready "
                                "o_gated o_squared ms_ready ms_eps ms_log rms_ready o_normed o_turned oT_ready "
                                "out_ready added")
        (projected, q_silu, k_sigmoid, z_biased, low_copied, v_ready, v_copied, gates, gate_ready, mag_ready, mag_exp,
         mag_log, logf_ready, G_ready, eG_ready, enG_ready, q_ready, k_ready, keys_turned, keys_copied, att_ready,
         att_masked, kv_ready, kv_scaled, S_ready, o_ready, o_gated, o_squared, ms_ready, ms_eps, ms_log, rms_ready,
         o_normed, o_turned, oT_ready, out_ready, added) = sems
        sems = ln.sems + [prep] + sems
        ch = lambda c: slice(c * CHUNK, (c + 1) * CHUNK)
        at = lambda first, c: banks[0:CHUNK, first + c // 4, (c % 4) * D:(c % 4 + 1) * D]
        both = lambda first: banks[0:CHUNK, first:first + 2, :].rearrange("p a (c d) -> p (a c) d", d=D)

        with nc.Block() as block:
            @block.sync
            def _(sp):
                sp.wait_ge(w["loaded"], w["total"])
        with nc.Block() as block:
            @block.vector
            def _(dve):
                dve.tensor_scalar(ndelta[:], w["delta"][:], -1.0, None, ALU.mult)

        with nc.Fori(0, GROUPS) as g:
            xg = x[:, bass.ds(g * GT, GT), :]
            with nc.Block() as block:
                @block.tensor
                def _(pe):
                    ln.tensor(pe)
                    pe.wait_ge(ln.ready, 1)
                    for n, name in enumerate(("Wk", "Wq", "G1")):
                        m = w[name].shape[1]
                        pe.matmul(banks[0:m, n, :], w[name][:], ln.xnT[:], start=True, stop=True).then_inc(projected, 1)
                    for c in range(NC):
                        last = pe.matmul(at(3, c), ln.xnT[:, ch(c)], w["Wv"][:], start=True, stop=True)
                    last.then_inc(v_ready, 1)
                    pe.wait_ge(low_copied, 1)
                    for c in range(NC):
                        last = pe.matmul(at(5, c), low[:, ch(c)], w["G2"][:], start=True, stop=True)
                    last.then_inc(gates, 1)
                    pe.wait_ge(k_ready, 1)
                    pe.wait_ge(q_ready, 1)
                    for c in range(NC):
                        for h in range(HEADS):
                            r = slice(h * HW, (h + 1) * HW)
                            last = pe.matmul(banks[0:CHUNK, 1 + h, ch(c)], k[r, ch(c)], q[r, ch(c)], start=True, stop=True)
                    last.then_inc(att_ready, 1)
                    pe.wait_ge(v_copied, 1)
                    for c in range(NC):
                        last = pe.transpose(at(3, c), k[:, ch(c)], consts["ident"])
                    last.then_inc(keys_turned, 1)
                    pe.wait_ge(keys_copied, 1)
                    for c in range(NC):
                        last = pe.matmul(banks[:, 3 + c // 4, (c % 4) * D:(c % 4 + 1) * D], keys[:, c, :], vals[:, c, :],
                                         start=True, stop=True)
                    last.then_inc(kv_ready, 1)
                    pe.wait_ge(gate_ready, 1)
                    pe.wait_ge(att_masked, HEADS)
                    for i in range(SC):
                        if i:
                            pe.wait_ge(S_ready, GB * i)
                        for b in range(GB):
                            c = b * SC + i
                            if i:
                                pe.matmul(at(5, c), q[:, ch(c)], S[:, c, :], start=True, stop=False)
                            for h in range(HEADS):
                                last = pe.matmul(at(5, c)[:, h * HW:(h + 1) * HW], att[:, h, c, :],
                                                 vals[:, c, h * HW:(h + 1) * HW], start=(i == 0), stop=(i == 0 or h == HEADS - 1))
                    last.then_inc(o_ready, 1)
                    pe.wait_ge(o_normed, 1)
                    for c in range(NC):
                        last = pe.transpose(banks[:, 7, ch(c)], o[:, c, :], consts["ident"][0:CHUNK, 0:CHUNK])
                    last.then_inc(o_turned, 1)
                    pe.wait_ge(oT_ready, 1)
                    for t in range(GT):
                        last = pe.matmul(banks[:, 0, t * P:(t + 1) * P], oT[:, t * P:(t + 1) * P], w["Wo"][:],
                                         start=True, stop=True)
                    last.then_inc(out_ready, 1)

                @block.scalar
                def _(act):
                    act.preload_act_table_set(EXP_LN)
                    ln.scalar(act)
                    act.wait_ge(z_biased, 1)
                    act.activation(mag[:], z[:], ACT.Abs).then_inc(mag_ready, 1)
                    act.wait_ge(mag_ready, 1)
                    act.activation(mag[:], mag[:], ACT.Exp, scale=-1.0).then_inc(mag_exp, 1)
                    act.wait_ge(mag_exp, 1)
                    act.activation(mag[:], mag[:], ACT.Ln, bias=1.0).then_inc(mag_log, 1)
                    act.wait_ge(G_ready, 1)
                    act.activation(eG[:], G[:], ACT.Exp).then_inc(eG_ready, 1)
                    act.activation(enG[:], G[:], ACT.Exp, scale=-1.0).then_inc(enG_ready, 1)
                    act.activation(k[:], z[:], ACT.Sigmoid, scale=-1.0).then_inc(k_sigmoid, 1)
                    act.wait_ge(gates, 1)
                    act.activation(sgate[:], both(5), ACT.Sigmoid).then_inc(gate_ready, 1)
                    act.wait_ge(projected, 2)
                    act.activation(q[:], banks[:, 1, :], ACT.Silu).then_inc(q_silu, 1)
                    act.preload_act_table_set(EXP_LN)
                    act.wait_ge(keys_turned, 1)
                    act.copy(keys[:], both(3)).then_inc(keys_copied, 1)
                    act.wait_ge(o_gated, 1)
                    act.activation(osq[:], o[:], ACT.Square).then_inc(o_squared, 1)
                    act.wait_ge(ms_eps, 1)
                    act.activation(lms[:], ms[:], ACT.Ln).then_inc(ms_log, 1)
                    act.wait_ge(ms_log, 1)
                    act.activation(rms[:], lms[:], ACT.Exp, scale=-0.5).then_inc(rms_ready, 1)
                    act.wait_ge(o_turned, 1)
                    act.activation(oT[:], banks[:, 7, :], ACT.Copy, scale=w["norm_w"][:]).then_inc(oT_ready, 1)

                @block.vector
                def _(dve):
                    ln.vector(dve, xg)
                    dve.wait_ge(projected, 1)
                    dve.tensor_scalar(z[:], banks[:, 0, :], w["delta"][:], None, ALU.add).then_inc(z_biased, 1)
                    dve.wait_ge(projected, 3)
                    dve.tensor_copy(low[:], banks[0:HW, 2, :]).then_inc(low_copied, 1)
                    dve.wait_ge(v_ready, 1)
                    dve.tensor_copy(vals[:], both(3)).then_inc(v_copied, 1)
                    dve.wait_ge(z_biased, 1)
                    dve.wait_ge(mag_log, 1)
                    dve.scalar_tensor_tensor(logf[:], z[:], 0.0, mag[:], ALU.min, ALU.subtract).then_inc(logf_ready, 1)
                    dve.wait_ge(logf_ready, 1)
                    dve.tensor_tensor_scan(G[:], consts["inside"], logf[:], 0.0, ALU.mult, ALU.add).then_inc(G_ready, 1)
                    dve.wait_ge(enG_ready, 1)
                    dve.wait_ge(k_sigmoid, 1)
                    dve.tensor_tensor(k[:], k[:], enG[:], ALU.mult).then_inc(k_ready, 1)
                    dve.wait_ge(eG_ready, 1)
                    dve.wait_ge(q_silu, 1)
                    dve.tensor_tensor(q[:], q[:], eG[:], ALU.mult).then_inc(q_ready, 1)
                    dve.wait_ge(att_ready, 1)
                    for h in range(HEADS):
                        dve.tensor_tensor(att[:, h, :, :], banks[0:CHUNK, 1 + h, :].rearrange("p (c t) -> p c t", t=CHUNK),
                                          consts["causal"][0:CHUNK, 0:CHUNK].unsqueeze(1).broadcast_to([CHUNK, NC, CHUNK]),
                                          ALU.mult).then_inc(att_masked, 1)
                    dve.wait_ge(kv_ready, 1)
                    end = lambda c: eG[:, (c + 1) * CHUNK - 1:(c + 1) * CHUNK]
                    into = lambda c: (S[:, c + 1, :] if c % SC == 0 else kv[:, c, :])
                    for b in range(GB):
                        for i in range(SC - 1):
                            c = b * SC + i
                            dve.scalar_tensor_tensor(into(c), banks[:, 3 + c // 4, (c % 4) * D:(c % 4 + 1) * D], end(c),
                                                     consts["blocks"], ALU.mult, ALU.mult).then_inc(kv_scaled, 1)
                    dve.wait_ge(kv_scaled, GB * (SC - 1))
                    dve.engine_nop().then_inc(S_ready, GB)
                    for i in range(1, SC - 1):
                        if i > 1:
                            dve.wait_ge(S_ready, GB * i)
                        for b in range(GB):
                            c = b * SC + i
                            dve.scalar_tensor_tensor(S[:, c + 1, :], S[:, c, :], end(c), kv[:, c, :], ALU.mult, ALU.add)\
                                .then_inc(S_ready, 1)
                    dve.wait_ge(o_ready, 1)
                    dve.wait_ge(gate_ready, 1)
                    dve.tensor_tensor(o[:], both(5), sgate[:], ALU.mult).then_inc(o_gated, 1)
                    dve.wait_ge(o_squared, 1)
                    dve.tensor_reduce(ms[:], osq[:].rearrange("p c (h d) -> p (c h) d", d=HW), AX_X, ALU.add).then_inc(ms_ready, 1)
                    dve.wait_ge(ms_ready, 1)
                    dve.tensor_scalar(ms[:], ms[:], 1.0 / HW, EPS, ALU.mult, ALU.add).then_inc(ms_eps, 1)
                    dve.wait_ge(rms_ready, 1)
                    oh = o[:].rearrange("p c (h d) -> p (c h) d", d=HW)
                    dve.tensor_tensor(oh, oh, spread(rms[:], HW), ALU.mult).then_inc(o_normed, 1)
                    dve.wait_ge(out_ready, 1)
                    dve.tensor_tensor(xg, xg, banks[:, 0, :].rearrange("p (t d) -> p t d", d=D), ALU.add)\
                        .then_inc(added, 1)
            restart(nc, sems)


def shift_tokens(pe, bank, consts, y, shifted):
    half = bank[:, 0:GT * D // 2].rearrange("p (t d) -> p t d", d=D // 2)
    pe.matmul(half, consts["next"], y[:, :, D // 2:], start=True, stop=False)
    last = pe.matmul(half[:, 1::ST, :], consts["carry"], y[:, 0::ST, D // 2:], start=False, stop=True)
    last.then_inc(shifted, 1)


ATTENTION_SIGNALS = ("shifted low_half high_half in_turned in_ready projected copied squared reduced swap_done cosined "
                     "rotated clamped logged inverted unit qk_turned qk_copied scored banded exped summed rden_ready "
                     "head_done v_copied o_turned o_copied out_ready added tabled peaked")
MLP_SIGNALS = ("mlp_shifted mlp_low_half mlp_high_half stats_done moments_done var_done log_done rstd_done normed "
               "ln_turned ln_ready gated gate_taken gelu_done widened hidden biased mlp_out_ready joined")


def local_step(nc, y, banks, consts, w, loaded, tables, tmp, sems, heads_of, make_of, mlp_of, parity,
               new_tables=False, new_peak=False):
    HALF, SCALE, UP, QS = INNER // 2, 8.0, 2.0 ** 32, 8.0
    BAND = P + WINDOW
    SCORES = BAND + P
    QK = 4 * GT
    UNITS = QK + 2 * GT
    CH = len(MLP_CHUNKS)
    S_BANK, T_BANK, V_BANK, O_BANK, A_BANK, X_BANK = 0, 2, 3, 4, 5, 7
    attention, mlp = sems
    (shifted, low_half, high_half, in_turned, in_ready, projected, copied, squared, reduced, swap_done, cosined, rotated,
     clamped, logged, inverted, unit, qk_turned, qk_copied, scored, banded, exped, summed, rden_ready, head_done,
     v_copied, o_turned, o_copied, out_ready, added, tabled, peaked) = attention
    (mlp_shifted, mlp_low_half, mlp_high_half, stats_done, moments_done, var_done, log_done, rstd_done, normed,
     ln_turned, ln_ready, gated, gate_taken, gelu_done, widened, hidden, biased, mlp_out_ready, joined) = mlp
    ys, yT_in, raw, sq, swapped = tmp["ys"], tmp["ysT"], tmp["raw"], tmp["sq"], tmp["swapped"]
    ss, lg, inv, turned_qk = tmp["ss"], tmp["lg"], tmp["inv"], tmp["turned_qk"]
    logit, probs, rden, o = tmp["logit"], tmp["probs"], tmp["rden"], tmp["o"]
    rot, v1 = tmp["rot"][:, parity], tmp["v1"][:, parity]
    rot_new, v1_new = tmp["rot"][:, 1 - parity], tmp["v1"][:, 1 - parity]
    ms, xn, xnT = tmp["mlp_ys"], tmp["mlp_xn"], tmp["mlp_xnT"]
    gate = hT = tmp["gate"]
    stats, moments, var, log, rstd = (tmp["mlp_" + n] for n in ("stats", "moments", "var", "log", "rstd"))
    oT = lambda j: rot[:, 0, :, j * P:(j + 1) * P]
    heads = lambda a: a.rearrange("p (h d) -> p h d", d=HD)
    tiled = lambda a: a.rearrange("p (t d) -> p t d", d=D)
    group = lambda g: None if g is None else y[:, bass.ds(g * GT, GT), :]
    yb, ya, ym = group(heads_of), group(make_of), group(mlp_of)
    A, B, M = make_of is not None, heads_of is not None, mlp_of is not None

    is_qk = lambda n: n % 6 < 4
    qk_number = lambda n: n // 6 * 4 + n % 6
    v_number = lambda n: n // 6 * 2 + n % 6 - 4
    where = lambda k: (k // 4, k // 2 % 2, k % 2)
    part = lambda k: heads(rot_new[:, where(k)[1], where(k)[0], where(k)[2] * HALF:(where(k)[2] + 1) * HALF])

    schedule = {"make_shift": (A, 0, 1), "make_turn": (A, 1, 1), "project": (A * UNITS, 2, 1), "take": (A * UNITS, 3, 1),
                "cosine": (A * UNITS, 4, 1), "rotate": (A * UNITS, 5, 1), "clamp": (A * GT, 8, 6), "invert": (A * GT, 9, 6),
                "unit_q": (A * GT, 10, 6), "unit_k": (A * GT, 11, 6),
                "turn": (B * H, 0, 1), "turned": (B * H, 1, 1), "score": (B * H, 3, 1), "mask": (B * H, 4, 1),
                "exp": (B * H, 6, 1), "values": (B * H, 7, 1), "normalize": (B * H, 8, 1), "turn_o": (B * PAIRS, 10, 2),
                "copy_o": (B * PAIRS, 11, 2),
                "mlp_shift": (M, 2, 1), "high_half": (M, 3, 1), "stats": (M, 4, 1), "moments": (M, 5, 1), "var": (M, 6, 1),
                "rstd": (M, 7, 1), "normalize_mlp": (M, 8, 1), "turn_mlp": (M, 9, 1), "turned_mlp": (M, 10, 1),
                "gate": (M * CH, 12, 2), "gate_take": (M * CH, 13, 2), "gelu": (M, 17, 1), "widen": (M * CH, 18, 2),
                "hide": (M * CH, 19, 2), "back": (M, 24, 1), "join": (M, 25, 1)}
    STEPS = max(first + (units - 1) * every + 1 for units, first, every in schedule.values() if units)

    def run(stage, i, do):
        units, first, every = schedule[stage]
        n, rest = divmod(i - first, every)
        if rest == 0 and 0 <= n < units:
            do(n)

    with nc.Block() as block:
        @block.tensor
        def _(pe):
            def turn_in(_):
                pe.wait_ge(low_half, 1)
                pe.wait_ge(high_half, 1)
                for t in range(GT):
                    last = pe.transpose(banks[:, X_BANK, t * P:(t + 1) * P], ys[:, t, :], consts["ident"])
                last.then_inc(in_turned, 1)

            def project(n):
                if n == 0:
                    pe.wait_ge(in_ready, 1)
                    pe.wait_ge(*loaded["attention"])
                if n >= 2:
                    if is_qk(n - 2):
                        pe.wait_ge(copied, qk_number(n - 2) + 1)
                    else:
                        pe.wait_ge(v_copied, v_number(n - 2) + 1)
                t, c = n // 6, n % 6 * HALF
                pe.matmul(banks[:, A_BANK + n % 2, :], yT_in[:, t * P:(t + 1) * P], w["Wqkv"][:, c:c + HALF],
                          start=True, stop=True).then_inc(projected, 1)

            def turn_qk(k):
                if k:
                    pe.wait_ge(qk_copied, k)
                j, m = k // 2, k % 2
                for t in range(GT):
                    last = pe.transpose(banks[:, T_BANK, t * P:(t + 1) * P], rot[:, m, t, j * P:(j + 1) * P], consts["ident"])
                last.then_inc(qk_turned, 1)

            def score(k):
                j, b = k // 2, k % 2
                pe.wait_ge(qk_copied, 2 * j + 2)
                for r in range(2):
                    if k:
                        pe.wait_ge(banded, 2 * (k - 1) + r + 1)
                    q, kk = (turned_qk[r * HD:(r + 1) * HD, j % 2, m, :] for m in range(2))
                    c = b * SEQ
                    pe.matmul(banks[:, S_BANK + r, 0:BAND], kk[:, c:c + P], q[:, c:c + BAND], start=True, stop=True)
                    pe.matmul(banks[:, S_BANK + r, BAND:SCORES], kk[:, c + P:c + SEQ], q[:, c + P:c + SEQ],
                              start=True, stop=True).then_inc(scored, 1)

            def values(h):
                pe.wait_ge(exped, 2 * (h + 1))
                if h:
                    pe.wait_ge(head_done, h)
                for b in range(GB):
                    for i in range(ST):
                        out = banks[:, V_BANK, (b * ST + i) * (HD + 1):(b * ST + i + 1) * (HD + 1)]
                        for j in range(i + 1):
                            c = (i * P if j == 0 else SEQ)
                            last = pe.matmul(out, probs[:, h % 2, b, c:c + P], v1[:, b * ST + j, h, :],
                                             start=(j == 0), stop=(j == i))
                last.then_inc(summed, 1)

            def turn_o(j):
                pe.wait_ge(head_done, 2 * j + 2)
                if j:
                    pe.wait_ge(o_copied, j)
                for t in range(GT):
                    last = pe.transpose(banks[:, O_BANK, t * P:(t + 1) * P], o[:, j % 2, t, :], consts["ident"])
                last.then_inc(o_turned, 1)

            def shift_mlp(_):
                if A:
                    pe.wait_ge(in_ready, 1)
                shift_tokens(pe, banks[:, X_BANK], consts, ym, mlp_shifted)

            def turn_mlp(_):
                pe.wait_ge(normed, GT)
                for t in range(GT):
                    last = pe.transpose(banks[:, X_BANK, t * P:(t + 1) * P], xn[:, t, :], consts["ident"])
                last.then_inc(ln_turned, 1)

            def wide(c, column, signal):
                lo, m = MLP_CHUNKS[c]
                pe.matmul(banks[0:m, X_BANK, :], w["W1"][:, column + lo:column + lo + m], xnT[:], start=True, stop=True)\
                    .then_inc(signal, 1)

            def make_gate(c):
                if c == 0:
                    pe.wait_ge(ln_ready, 1)
                    pe.wait_ge(*loaded["mlp"])
                else:
                    pe.wait_ge(gate_taken, c)
                wide(c, MLP, gated)

            def widen(c):
                if c == 0:
                    pe.wait_ge(gate_taken, CH)
                else:
                    pe.wait_ge(hidden, c)
                wide(c, 0, widened)

            def back(_):
                pe.wait_ge(hidden, CH)
                for t in range(GT):
                    for c, (lo, m) in enumerate(MLP_CHUNKS):
                        last = pe.matmul(banks[:, X_BANK, t * P:(t + 1) * P], hT[0:m, c, t * P:(t + 1) * P],
                                         w["W2"][0:m, c, :], start=(c == 0), stop=(c == CH - 1))
                last.then_inc(mlp_out_ready, 1)

            for i in range(STEPS):
                run("make_shift", i, lambda _: shift_tokens(pe, banks[:, X_BANK], consts, ya, shifted))
                run("make_turn", i, turn_in)
                run("mlp_shift", i, shift_mlp)
                run("turn_mlp", i, turn_mlp)
                run("project", i, project)
                run("gate", i, make_gate)
                run("widen", i, widen)
                run("back", i, back)
                run("turn_o", i, turn_o)
                run("score", i, score)
                run("values", i, values)
                run("turn", i, turn_qk)
            if B:
                pe.wait_ge(o_copied, PAIRS)
                pe.wait_ge(*loaded["Wo"])
                if M:
                    pe.wait_ge(joined, 1)
                elif A:
                    pe.wait_ge(in_ready, 1)
                for t in range(GT):
                    for j in range(PAIRS):
                        last = pe.matmul(banks[:, X_BANK, t * P:(t + 1) * P], oT(j)[:, t, :],
                                         w["Wo"][:, j, :], start=(j == 0), stop=(j == PAIRS - 1))
                last.then_inc(out_ready, 1)

        @block.scalar
        def _(act):
            def copy_in(_):
                act.wait_ge(in_turned, 1)
                act.copy(yT_in[:], banks[:, X_BANK, :]).then_inc(in_ready, 1)

            def take(n):
                act.wait_ge(projected, n + 1)
                if not is_qk(n):
                    v = v_number(n)
                    act.copy(v1_new[:, v // 2, (v % 2) * PAIRS:(v % 2 + 1) * PAIRS, 0:HD],
                             heads(banks[:, A_BANK + n % 2, :])).then_inc(v_copied, 1)
                    return
                k = qk_number(n)
                if k >= 4:
                    act.wait_ge(cosined, k - 3)
                    act.wait_ge(swap_done, 2 * (k - 3))
                    act.wait_ge(squared, k - 3)
                act.copy(raw[:, k % 4, :], banks[:, A_BANK + n % 2, :]).then_inc(copied, 1)
                act.wait_ge(copied, k + 1)
                if k >= 3:
                    act.wait_ge(reduced, k - 2)
                act.activation(sq[:, k % 3, :], raw[:, k % 4, :], ACT.Square).then_inc(squared, 1)

            def invert(t):
                act.wait_ge(clamped, t + 1)
                act.activation(lg[:, :, t, :], ss[:, :, t, :], ACT.Ln).then_inc(logged, 1)
                act.wait_ge(logged, t + 1)
                act.activation(inv[:, :, t, :], lg[:, :, t, :], ACT.Exp, bias=tables["up"][:], scale=-0.5).then_inc(inverted, 1)

            def copy_qk(k):
                act.wait_ge(qk_turned, k + 1)
                if k >= 4:
                    act.wait_ge(scored, 4 * (k // 2 - 1))
                act.copy(turned_qk[:, k // 2 % 2, k % 2, :], banks[:, T_BANK, :]).then_inc(qk_copied, 1)

            def exp(h):
                if h == 0 and new_peak:
                    act.wait_ge(peaked, 1)
                act.wait_ge(banded, 4 * (h // 2) + 4)
                if h >= 2:
                    act.wait_ge(summed, h - 1)
                for lo, hi, into in ((0, BAND, 0), (BAND, SCORES, SEQ)):
                    act.activation(probs[:, h % 2, :, into:into + hi - lo], logit[:, h // 2 % 2, h % 2, :, lo:hi],
                                   ACT.Exp, bias=tables["npeak"][:], scale=SCALE).then_inc(exped, 1)

            def copy_o(j):
                act.wait_ge(o_turned, j + 1)
                act.copy(oT(j), tiled(banks[:, O_BANK, :])).then_inc(o_copied, 1)

            def rstd_mlp(_):
                act.wait_ge(var_done, 1)
                act.activation(log[:], var[:], ACT.Ln).then_inc(log_done, 1)
                act.wait_ge(log_done, 1)
                act.activation(rstd[:], log[:], ACT.Exp, scale=-0.5).then_inc(rstd_done, 1)

            def copy_normed(_):
                act.wait_ge(ln_turned, 1)
                act.wait_ge(*loaded["mlp"])
                act.activation(xnT[:], banks[:, X_BANK, :], ACT.Identity, bias=w["ln_b"][:], scale=w["ln_g"][:])\
                    .then_inc(ln_ready, 1)

            def take_gate(c):
                m = MLP_CHUNKS[c][1]
                act.wait_ge(gated, c + 1)
                act.activation(gate[0:m, c, :], banks[0:m, X_BANK, :], ACT.Identity, bias=w["b1"][0:m, CH + c:CH + c + 1])\
                    .then_inc(gate_taken, 1)

            def gelu(_):
                full = sum(m == P for _, m in MLP_CHUNKS)
                rest = MLP_CHUNKS[-1][1]
                act.wait_ge(gate_taken, CH)
                act.activation(gate[:, 0:full, :], gate[:, 0:full, :], ACT.Gelu).then_inc(gelu_done, 1)
                act.activation(gate[0:rest, full, :], gate[0:rest, full, :], ACT.Gelu).then_inc(gelu_done, 1)
                act.preload_act_table_set(EXP_LN)

            if A:
                act.copy(ys[:, :, 0:D // 2], ya[:, :, 0:D // 2]).then_inc(low_half, 1)
            if M:
                act.copy(ms[:, :, 0:D // 2], ym[:, :, 0:D // 2]).then_inc(mlp_low_half, 1)
            for i in range(STEPS):
                run("make_turn", i, copy_in)
                run("turned", i, copy_qk)
                run("exp", i, exp)
                run("take", i, take)
                run("invert", i, invert)
                run("copy_o", i, copy_o)
                run("rstd", i, rstd_mlp)
                run("turned_mlp", i, copy_normed)
                run("gate_take", i, take_gate)
                run("gelu", i, gelu)

        def pool_bias(pool):
            pool.wait_ge(mlp_shifted, 1)
            pool.wait_ge(mlp_low_half, 1)
            pool.wait_ge(*loaded["mlp"])
            pool.tensor_tensor(ym, ym, w["b2"][:].unsqueeze(1).broadcast_to([P, GT, D]), ALU.add).then_inc(biased, 1)

        @block.gpsimd
        def _(pool):
            if A and new_tables:
                pool.wait_ge(tabled, 3)
            for k in range(QK if A else 0):
                t, m, half = where(k)
                pool.wait_ge(copied, k + 1)
                if k >= 3:
                    pool.wait_ge(rotated, k - 2)
                for r in range(2):
                    lo, other = slice(32 * r, 32 * r + 32), slice(32 - 32 * r, 64 - 32 * r)
                    pool.tensor_tensor(heads(swapped[:, k % 3, :])[:, :, lo], heads(raw[:, k % 4, :])[:, :, other],
                                       tables["all"][:, 2 * m + 1, t % ST, lo].unsqueeze(1)
                                       .broadcast_to([P, PAIRS, 32]), ALU.mult).then_inc(swap_done, 1)
                if M and k == 1:
                    pool_bias(pool)
            if M and not A:
                pool_bias(pool)

        @block.vector
        def _(dve):
            def cosine(n):
                if not is_qk(n):
                    return
                k = qk_number(n)
                t, m, half = where(k)
                dve.wait_ge(copied, k + 1)
                dve.tensor_tensor(part(k), heads(raw[:, k % 4, :]), tables["all"][:, 2 * m, t % ST, :].unsqueeze(1)
                                  .broadcast_to([P, PAIRS, HD]), ALU.mult).then_inc(cosined, 1)

            def rotate(n):
                if not is_qk(n):
                    return
                k = qk_number(n)
                t, m, half = where(k)
                dve.wait_ge(squared, k + 1)
                dve.tensor_reduce(ss[:, m, t, half * PAIRS:(half + 1) * PAIRS], heads(sq[:, k % 3, :]), AX_X, ALU.add)\
                    .then_inc(reduced, 1)
                dve.wait_ge(cosined, k + 1)
                dve.wait_ge(swap_done, 2 * k + 2)
                dve.tensor_tensor(part(k), part(k), heads(swapped[:, k % 3, :]), ALU.add).then_inc(rotated, 1)

            def clamp(t):
                dve.wait_ge(reduced, 4 * t + 4)
                dve.tensor_scalar(ss[:, :, t, :], ss[:, :, t, :], 1e-24, UP, ALU.max, ALU.mult).then_inc(clamped, 1)

            def make_unit(t, m):
                dve.wait_ge(inverted, t + 1)
                dve.wait_ge(rotated, 4 * t + 4)
                a = heads(rot_new[:, m, t, :])
                dve.tensor_tensor(a, a, spread(inv[:, m, t, :], HD), ALU.mult).then_inc(unit, 1)

            def mask(k):
                j, b = k // 2, k % 2
                if j >= 2:
                    dve.wait_ge(exped, 4 * (j - 1))
                for r in range(2):
                    dve.wait_ge(scored, 2 * k + r + 1)
                    dve.tensor_tensor(logit[:, j % 2, r, b, :], banks[:, S_BANK + r, 0:SCORES], consts["band"], ALU.add)\
                        .then_inc(banded, 1)

            def normalize(h):
                dve.wait_ge(summed, h + 1)
                out = banks[:, V_BANK, 0:GT * (HD + 1)].rearrange("p (t e) -> p t e", e=HD + 1)
                dve.reciprocal(rden[:, h % 2, :], out[:, :, HD]).then_inc(rden_ready, 1)
                dve.wait_ge(rden_ready, h + 1)
                if h >= 4:
                    dve.wait_ge(o_turned, h // 2 - 1)
                dve.tensor_tensor(o[:, h // 2 % 2, :, h % 2 * HD:(h % 2 + 1) * HD], out[:, :, 0:HD],
                                  spread(rden[:, h % 2, :], HD), ALU.mult).then_inc(head_done, 1)

            def copy_high(_):
                dve.wait_ge(mlp_shifted, 1)
                dve.tensor_copy(ms[:, :, D // 2:], tiled_half(banks[:, X_BANK])).then_inc(mlp_high_half, 1)

            def take_stats(_):
                dve.wait_ge(mlp_low_half, 1)
                dve.wait_ge(mlp_high_half, 1)
                for t in range(GT):
                    dve.bn_stats(stats[:, t, :], ms[:, t, :]).then_inc(stats_done, 1)

            def take_moments(_):
                dve.wait_ge(stats_done, GT)
                for t in range(GT):
                    dve.bn_aggr(moments[:, t, :], stats[:, t, :]).then_inc(moments_done, 1)

            def take_var(_):
                dve.wait_ge(moments_done, GT)
                dve.tensor_scalar(var[:], moments[:, :, 1], LN_EPS, None, ALU.add).then_inc(var_done, 1)

            def normalize_mlp(_):
                dve.wait_ge(rstd_done, 1)
                for t in range(GT):
                    dve.tensor_scalar(xn[:, t, :], ms[:, t, :], moments[:, t, 0:1], rstd[:, t:t + 1], ALU.subtract, ALU.mult)\
                        .then_inc(normed, 1)

            def hide(c):
                m = MLP_CHUNKS[c][1]
                if c == 0:
                    dve.wait_ge(gelu_done, 2)
                dve.wait_ge(widened, c + 1)
                dve.scalar_tensor_tensor(hT[0:m, c, :], banks[0:m, X_BANK, :], w["b1"][0:m, c:c + 1],
                                         gate[0:m, c, :], ALU.add, ALU.mult).then_inc(hidden, 1)

            def join(_):
                dve.wait_ge(mlp_out_ready, 1)
                dve.wait_ge(biased, 1)
                dve.tensor_tensor(ym, ym, tiled(banks[:, X_BANK, :]), ALU.add).then_inc(joined, 1)

            tiled_half = lambda bank: bank[:, 0:GT * D // 2].rearrange("p (t d) -> p t d", d=D // 2)
            scales, most = tables["scales"], tables["most"]
            if new_peak:
                dve.tensor_scalar(tables["npeak"][:], most[:, 0:1], most[:, 1:2], -QS, ALU.mult, ALU.mult).then_inc(peaked, 1)
            if new_tables:
                dve.wait_ge(*loaded["scales"])
                dve.tensor_tensor(tables["all"][:], tables["shapes"][:], scales[:].unsqueeze(2).broadcast_to([P, 4, ST, HD]),
                                  ALU.mult).then_inc(tabled, 1)
                for n in range(2):
                    dve.tensor_reduce(most[:, n:n + 1], scales[:, 2 * n, :], AX_X, ALU.max, apply_absolute_value=True)\
                        .then_inc(tabled, 1)
                dve.wait_ge(tabled, 3)
            if A:
                dve.wait_ge(shifted, 1)
                dve.tensor_copy(ys[:, :, D // 2:], tiled_half(banks[:, X_BANK])).then_inc(high_half, 1)
            for i in range(STEPS):
                run("mask", i, mask)
                run("normalize", i, normalize)
                run("high_half", i, copy_high)
                run("stats", i, take_stats)
                run("moments", i, take_moments)
                run("var", i, take_var)
                run("normalize_mlp", i, normalize_mlp)
                run("hide", i, hide)
                run("join", i, join)
                run("cosine", i, cosine)
                run("rotate", i, rotate)
                run("clamp", i, clamp)
                run("unit_q", i, lambda t: make_unit(t, 0))
                run("unit_k", i, lambda t: make_unit(t, 1))
            if B:
                dve.wait_ge(out_ready, 1)
                dve.tensor_tensor(yb, yb, tiled(banks[:, X_BANK, :]), ALU.add).then_inc(added, 1)
    restart(nc, attention + mlp)


def local_layers(nc, x, banks, consts, t, out):
    f = "L3_ffn_"
    y = x
    with ExitStack() as ctx:
        sb = lambda n, s: ctx.enter_context(nc.sbuf_tensor("local_" + n, s, F32))
        residual = out.rearrange("b (t p) d -> p (b t) d", p=P)
        lw = {"Wqkv": sb("Wqkv", [P, 3 * INNER]), "Wo": sb("Wo", [P, PAIRS, D]), "W1": sb("W1", [P, 2 * MLP]),
              "W2": sb("W2", [P, len(MLP_CHUNKS), D]), "b1": sb("b1", [P, 2 * len(MLP_CHUNKS)]), "b2": sb("b2", [P, D]),
              "ln_g": sb("ln_g", [P, 1]), "ln_b": sb("ln_b", [P, 1])}
        tables = {"scales": sb("qk_scales", [P, 4, HD]),
                  "shapes": sb("rotary", [P, 4, ST, HD]), "all": sb("rotary_scaled", [P, 4, ST, HD]),
                  "most": sb("most", [P, 2]), "npeak": sb("npeak", [P, 1]), "up": sb("up", [P, 1])}
        scales = tables["scales"]
        tmp = {n: sb(n, s) for n, s in (
            ("ys", [P, GT, D]), ("ysT", [P, GN]), ("raw", [P, 4, INNER // 2]), ("sq", [P, 3, INNER // 2]),
            ("swapped", [P, 3, INNER // 2]), ("ss", [P, 2, GT, H]), ("lg", [P, 2, GT, H]), ("inv", [P, 2, GT, H]),
            ("rot", [P, 2, 2, GT, INNER]), ("turned_qk", [P, 2, 2, GN]), ("logit", [P, 2, 2, GB, 2 * P + WINDOW]),
            ("probs", [P, 2, GB, CAUSAL]), ("v1", [P, 2, GT, H, HD + 1]), ("rden", [P, 2, GT]), ("o", [P, 2, GT, D]),
            ("mlp_ys", [P, GT, D]), ("mlp_stats", [P, GT, 6]), ("mlp_moments", [P, GT, 2]), ("mlp_var", [P, GT]),
            ("mlp_log", [P, GT]), ("mlp_rstd", [P, GT]), ("mlp_xn", [P, GT, D]), ("mlp_xnT", [P, GN]),
            ("gate", [P, len(MLP_CHUNKS), GN]))}
        filled, rotary_loaded, kept, returned = signals(nc, ctx, "filled rotary_loaded kept returned")
        attention_loaded, scales_loaded, wo_loaded, mlp_loaded = signals(nc, ctx, "attention_loaded scales_loaded wo_loaded mlp_loaded")

        with ExitStack() as inner:
            room = tmp["rot"].rearrange("p a b t n -> p (a b t n)")
            ln = LayerNorm(nc, inner, consts, banks[:, 7, :], "local_ln",
                           (room[:, 0:GN].rearrange("p (t d) -> p t d", d=D), room[:, GN:2 * GN]))
            with nc.Block() as block:
                @block.sync
                def _(sp):
                    sp.dma_start(residual, x[:]).then_inc(kept, 16)
                    sp.dma_start(tables["shapes"][:], t["rotary"]).then_inc(rotary_loaded, 16)
                    sp.wait_ge(rotary_loaded, 16)
                    sp.wait_ge(kept, 16)

                @block.scalar
                def _(act):
                    act.preload_act_table_set(EXP_LN)

                @block.vector
                def _(dve):
                    dve.memset(tables["up"][:], 16.0 * float(np.log(2.0)))
                    for r in range(2):
                        dve.memset(tmp["v1"][:, r, :, :, HD:HD + 1], 1.0)

                @block.gpsimd
                def _(pool):
                    pool.memset(tmp["probs"][:], 0.0).then_inc(filled, 1)
            with nc.Fori(0, GROUPS) as g:
                xg = x[:, bass.ds(g * GT, GT), :]
                with nc.Block() as block:
                    @block.vector
                    def _(dve):
                        ln.vector(dve, xg)
                        dve.wait_ge(ln.normed, GT)
                        dve.tensor_copy(xg, ln.xn).then_inc(ln.ready, 1)

                    @block.scalar
                    def _(act):
                        ln.scalar(act, copy=False)
                restart(nc, ln.sems)

        def moves(layer):
            at = lambda n: t[f + n][bass.ds(layer, 1)]
            scale_moves = []
            for n, name in ((0, "q_scale"), (2, "k_scale")):
                s = at(name)
                scale_moves += [(scales[:, n, :], s.broadcast_to([P, HD])),
                                (scales[:, n + 1, 0:HD // 2], s[:, HD // 2:].broadcast_to([P, HD // 2])),
                                (scales[:, n + 1, HD // 2:], s[:, 0:HD // 2].broadcast_to([P, HD // 2]))]
            full = sum(m == P for _, m in MLP_CHUNKS)
            rest = MLP_CHUNKS[-1][1]
            return {"scales": scale_moves, "attention": [(lw["Wqkv"][:], at("Wqkv").rearrange("l d n -> d (l n)"))],
                    "Wo": [(lw["Wo"][:], at("Wo").rearrange("l (j p) d -> p (l j) d", p=P))],
                    "mlp": [(lw["W1"][:], at("W1").rearrange("l d n -> d (l n)")),
                            (lw["W2"][:, 0:full, :], at("W2")[:, 0:full * P, :].rearrange("l (c p) d -> p (l c) d", p=P)),
                            (lw["W2"][0:rest, full, :], at("W2")[:, full * P:, :].rearrange("l p d -> p (l d)")),
                            (lw["b1"][:], at("b1T").rearrange("l p c -> p (l c)")), (lw["b2"][:], at("b2").broadcast_to([P, D])),
                            (lw["ln_g"][:], at("ln_g").rearrange("l d -> d l")), (lw["ln_b"][:], at("ln_b").rearrange("l d -> d l"))]}

        loaded = {n: (s, 16 * len(moves(0)[n])) for n, s in
                  (("scales", scales_loaded), ("attention", attention_loaded), ("Wo", wo_loaded), ("mlp", mlp_loaded))}

        def load(layer, *kinds):
            with nc.Block() as block:
                @block.sync
                def _(sp):
                    for kind in kinds:
                        for tile, source in moves(layer)[kind]:
                            sp.dma_start(tile, source).then_inc(loaded[kind][0], 16)

        def reload(layer, *kinds):
            restart(nc, [loaded[kind][0] for kind in kinds])
            load(layer, *kinds)

        with ExitStack() as inner:
            sems = signals(nc, inner, ATTENTION_SIGNALS), signals(nc, inner, MLP_SIGNALS)
            step = lambda *args, **more: local_step(nc, y, banks, consts, lw, loaded, tables, tmp, sems, *args, **more)

            def middle():
                with nc.Fori(0, (GROUPS - 2) // 2) as pair:
                    g = 2 * pair
                    step(g + 1, g + 2, g, 1)
                    step(g + 2, g + 3, g + 1, 0)

            load(0, "scales", "attention", "Wo")
            step(None, 0, None, 1, new_tables=True)
            step(0, 1, None, 0, new_peak=True)
            load(0, "mlp")
            with nc.Fori(0, DEPTH - 1) as layer:
                middle()
                reload(layer + 1, "scales", "attention")
                step(GROUPS - 1, 0, GROUPS - 2, 1, new_tables=True)
                reload(layer + 1, "Wo")
                step(0, 1, GROUPS - 1, 0, new_peak=True)
                reload(layer + 1, "mlp")
            middle()
            step(GROUPS - 1, None, GROUPS - 2, 1)
            step(None, None, GROUPS - 1, 0)

        back = tmp["rot"].rearrange("p a b t n -> p (a b t n)")[:, 0:TILES * D].rearrange("p (t d) -> p t d", d=D)
        with nc.Block() as block:
            @block.sync
            def _(sp):
                sp.dma_start(back, residual).then_inc(returned, 16)

            @block.vector
            def _(dve):
                dve.wait_ge(returned, 16)
                dve.tensor_tensor(x[:], y[:], back, ALU.add)


STAGES = ["favor", "router", "cosine", "int4", "mamba", "experts", "hgrn", "local"]


class Weights:

    def __init__(self, nc, ctx, t, stage, prefix):
        self.nc, self.ctx, self.t, self.prefix, self.stage = nc, ctx, t, prefix, stage
        self.moves, self.tiles = [], {"loaded": signals(nc, ctx, stage + "_loaded")[0]}

    def add(self, name, shape, source):
        tile = self.ctx.enter_context(self.nc.sbuf_tensor(f"{self.stage}_w_{name}", shape, F32))
        self.tiles[name] = tile
        self.moves.append((tile[:], source))
        self.tiles["total"] = 16 * len(self.moves)
        return tile

    def load(self, sp):
        for tile, source in self.moves:
            sp.dma_start(tile, source).then_inc(self.tiles["loaded"], 16)


def weights(nc, ctx, t):
    row = lambda a: a.rearrange("(o n) -> o n", o=1)
    column = lambda a: a.rearrange("(n o) -> n o", o=1)

    favor = Weights(nc, ctx, t, "favor", "L0_attn_")
    for n in ("Wq", "Wk"):
        tile = favor.add(n + "2", [P, H, 2 * HD], None)
        favor.moves.pop()
        for r in range(2):
            favor.moves.append((tile[:, :, r * HD:(r + 1) * HD], t["L0_attn_" + n].rearrange("p (h d) -> p h d", d=HD)))
    favor.add("Wv", [P, INNER], t["L0_attn_Wv"])
    favor.add("Wo", [P, PAIRS, D], t["L0_attn_Wo"].rearrange("(j p) d -> p j d", p=P))
    favor.add("Wfeat", [P, NF], t["Wfeat"])

    f = "L0_ffn_"
    router = Weights(nc, ctx, t, "router", f)
    router.add("W1T", [P, 512], t["L0_ffn_W1T"])
    router.add("W2T", [P, 4, D], t["L0_ffn_W2T"].rearrange("(c p) d -> p c d", p=P))
    router.add("ln_g", [P, 1], column(t[f + "ln_g"]))
    router.add("ln_b", [P, 1], column(t[f + "ln_b"]))
    router.add("RT", [P, 64], t["L0_ffn_router_WT"])
    router.add("rb", [1, 64], row(t[f + "router_b"]))
    router.add("U", [64, D], t[f + "raw_U"])
    router.add("V", [64, D], t[f + "raw_V"])
    router.add("gamma", [64, D], t[f + "gamma"].rearrange("a b d -> (a b d)").partition_broadcast(64))

    f = "L1_attn_"
    cosine = Weights(nc, ctx, t, "cosine", f)
    cosine.add("Wqkv", [P, 3 * INNER], None)
    cosine.moves.pop()
    cosine.moves += [(cosine.tiles["Wqkv"][:, 0:INNER], t[f + "w_q"]), (cosine.tiles["Wqkv"][:, INNER:], t[f + "w_kv"])]
    cosine.add("Wo", [P, PAIRS, D], t[f + "w_out"].rearrange("(j p) d -> p j d", p=P))
    cosine.add("bo", [1, D], row(t[f + "b_out"]))
    cosine.add("scale", [P, H], t[f + "scale"].rearrange("a h b c -> (a h b c)").partition_broadcast(P))

    f = "L1_ffn_"
    int4 = Weights(nc, ctx, t, "int4", f)
    int4.add("kernel", [P, D], t[f + "kernel"])
    int4.add("bias", [1, D], row(t[f + "bias"]))
    int4.add("a", [P, 16], t[f + "a"])
    int4.add("b", [16, D], t[f + "b"])
    f = "L2_attn_"
    mamba = Weights(nc, ctx, t, "mamba", f)
    mamba.add("Win", [P, 512], t[f + "Win"])
    mamba.add("bin", [P, 4], t[f + "binT"])
    mamba.add("Wdp", [P, 2, 8], t[f + "Wx"].rearrange("(c p) n -> p c n", p=P)[:, :, 0:8])
    mamba.add("Wbc", [P, 2, 192], t[f + "Wbc"].rearrange("(c p) n -> p c n", p=P))
    mamba.add("bdp", [8, 1], column(t[f + "bx"][0:8]))
    mamba.add("bbc", [96, 2], t[f + "bbc"])
    mamba.add("Wdt", [8, 256], t[f + "Wdt"])
    mamba.add("bdt", [P, 2], t[f + "bdtT"])
    mamba.add("A_log", [P, 2, 16], t[f + "A_log"].rearrange("(c p) n -> p c n", p=P))
    mamba.add("Dp", [P, 2], t[f + "DpT"])
    mamba.add("Wout", [P, 2, D], t[f + "Wout"].rearrange("(c p) d -> p c d", p=P))
    mamba.add("bout", [1, D], row(t[f + "bout"]))

    mamba.tiles["pick"] = t["pick"]

    f = "L2_ffn_"
    experts = Weights(nc, ctx, t, "experts", f)
    experts.add("Wg", [P, 8], t[f + "Wg"])
    experts.add("bg", [1, 8], row(t[f + "bg"]))
    experts.add("W1", [P, 8, 512], t[f + "W1"].rearrange("e d f -> d e f"))
    experts.add("b1", [P, 32], t[f + "b1T"])
    experts.add("W2", [P, 8, 4, D], t[f + "W2"].rearrange("e (c p) d -> p e c d", p=P))
    experts.add("b2", [8, D], t[f + "b2"])
    experts.add("gamma", [P, D], t[f + "gamma"].partition_broadcast(P))
    experts.add("beta", [P, D], t[f + "beta"].partition_broadcast(P))

    f = "L3_attn_"
    hgrn = Weights(nc, ctx, t, "hgrn", f)
    for n, m in (("Wq", D), ("Wk", D), ("Wv", D), ("G1", 64), ("Wo", D)):
        hgrn.add(n, [P, m], t[f + n])
    hgrn.add("G2", [64, D], t[f + "G2"])
    hgrn.add("delta", [P, 1], column(t[f + "delta"]))
    hgrn.add("norm_w", [P, 1], column(t[f + "norm_w"]))
    return {"favor": favor, "router": router, "cosine": cosine, "int4": int4, "mamba": mamba, "experts": experts,
            "hgrn": hgrn}


RUN = {"favor": favor_attention, "router": router_ffn, "cosine": cosine_attention, "int4": int4_linear,
       "mamba": state_space, "experts": expert_ffn, "hgrn": gated_recurrence}


def build(nc, t, out, stages):
    with ExitStack() as ctx:
        sb = lambda n, s, d=F32: ctx.enter_context(nc.sbuf_tensor(n, s, d))
        banks = ctx.enter_context(nc.psum_tensor("banks", [P, 8, 512], F32))
        x = sb("x", [P, TILES, D])
        consts = {n: sb(n, list(t[n].shape))[:] for n in ("ident", "ones", "next", "carry", "band")}
        x_loaded, consts_loaded, stored = signals(nc, ctx, "x_loaded consts_loaded stored")
        held = ctx.enter_context(ExitStack())
        consts |= {n: held.enter_context(nc.sbuf_tensor(n, list(t[n].shape), F32))[:]
                   for n in ("causal", "count", "inside", "blocks")}
        ws = weights(nc, held, t)

        with nc.Block() as block:
            @block.sync
            def _(sp):
                sp.dma_start(x[:], t["L0_attn_x"].rearrange("b (t p) d -> p (b t) d", p=P)).then_inc(x_loaded, 16)
                for n in consts:
                    sp.dma_start(consts[n], t[n]).then_inc(consts_loaded, 16)
                for w in ws.values():
                    w.load(sp)
                sp.wait_ge(x_loaded, 16)
                sp.wait_ge(consts_loaded, 16 * len(consts))
        for stage in stages:
            if stage != "local":
                RUN[stage](nc, x, banks, consts, ws[stage].tiles)
        with nc.Block() as block:
            @block.sync
            def _(sp):
                for w in ws.values():
                    sp.wait_ge(w.tiles["loaded"], w.tiles["total"])
        held.close()
        if "local" in stages:
            local_layers(nc, x, banks, consts, t, out)
        with nc.Block() as block:
            @block.sync
            def _(sp):
                sp.dma_start(out.rearrange("b (t p) d -> p (b t) d", p=P), x[:]).then_inc(stored, 16)
                sp.wait_ge(stored, 16)


def rotary():
    half = np.arange(0, HD, 2, dtype=np.float32)
    inv_freq = 1.0 / np.float32(10000.0) ** (half / HD)
    at = np.arange(SEQ, dtype=np.float32)
    freqs = at[:, None] * inv_freq[None, :]
    base = (half + 0.4 * HD) / (1.4 * HD)
    scale = base[None, :].astype(np.float64) ** ((at - SEQ // 2) / (WINDOW // 2))[:, None]
    cos, sin = np.cos(freqs.astype(np.float64)), np.sin(freqs.astype(np.float64))
    four = [np.concatenate([cos * s, cos * s], 1) if c else np.concatenate([-sin * s, sin * s], 1)
            for s in (scale, 1 / scale) for c in (True, False)]
    return np.ascontiguousarray(np.stack(four).reshape(4, ST, P, HD).transpose(2, 0, 1, 3)).astype(np.float32)


def shape_constants():
    i = np.arange(P)
    ahead = np.arange(P + WINDOW)[None, :] - i[:, None]
    seen = np.where((ahead >= 0) & (ahead <= WINDOW), 0.0, -1e30).astype(np.float32)
    band = np.concatenate([seen, seen[:, :P]], 1)
    tri = (i[:, None] <= i[None, :]).astype(np.float32)
    return {"ident": np.eye(P, dtype=np.float32), "causal": np.concatenate([tri, np.ones((P, P), np.float32), tri], 1),
            "ones": np.ones((P, P), np.float32),
            "pick": np.tile(np.repeat(np.eye(32, 16, dtype=np.float32), P, 1), (3, 1)),
            "count": np.tile(np.arange(8, dtype=np.float32), (P, 1)),
            "inside": np.tile((np.arange(GN) % 64 != 0).astype(np.float32), (P, 1)),
            "next": np.eye(P, k=1, dtype=np.float32),
            "carry": (np.arange(P * P).reshape(P, P) == (P - 1) * P).astype(np.float32),
            "rotary": rotary(), "band": band,
            "blocks": np.kron(np.eye(2, dtype=np.float32), np.ones((64, 64), np.float32))}


def layouts(a):
    w = {k: np.ascontiguousarray(v) for k, v in a.items()}
    w["Wfeat"] = np.concatenate([np.asarray(a["L0_attn_W_feat"]), np.full((HD, NF), -0.5, np.float32)], 0)
    for n in ("L0_ffn_W1", "L0_ffn_W2", "L0_ffn_router_W"):
        w[n + "T"] = np.ascontiguousarray(w[n].T)
    columns = [slice(8, 24)] * 6 + [slice(24, 40)] * 6
    w["L2_attn_Wbc"] = np.concatenate([w["L2_attn_Wx"][:, c] for c in columns], 1)
    w["L2_attn_bbc"] = np.ascontiguousarray(np.concatenate([w["L2_attn_bx"][c] for c in columns]).reshape(2, 96).T)
    b1 = np.zeros((DEPTH, 2, len(MLP_CHUNKS) * P), np.float32)
    b1[:, :, :MLP] = w["L3_ffn_b1"].reshape(DEPTH, 2, MLP)
    w["L3_ffn_b1T"] = np.ascontiguousarray(b1.reshape(DEPTH, -1, P).transpose(0, 2, 1))
    for n in ("L2_attn_bin", "L2_attn_bdt", "L2_attn_Dp", "L2_ffn_b1"):
        w[n + "T"] = np.ascontiguousarray(w[n].reshape(-1, P).T)
    return w


def kernel(**inputs):
    import concourse.bacc as bacc
    from concourse.bass_utils import run_bass_kernel_spmd

    nc = bacc.Bacc("TRN2", target_bir_lowering=False, num_devices=1)
    arrays = layouts({k: np.asarray(v) for k, v in inputs.items()}) | shape_constants()
    t = {n: nc.dram_tensor("in_" + n, a.shape, mybir.dt.from_np(a.dtype), kind="ExternalInput").ap() for n, a in arrays.items()}
    out = nc.dram_tensor("out", (BATCH, SEQ, D), F32, kind="ExternalOutput").ap()
    build(nc, t, out, STAGES)
    return run_bass_kernel_spmd(nc, [{"in_" + n: a for n, a in arrays.items()}], core_ids=[0]).results[0]["out"]
```

```python
from contextlib import ExitStack

import numpy as np
import concourse.bass as bass
from concourse import mybir

ALU = mybir.AluOpType
ACT = mybir.ActivationFunctionType
AX_X = mybir.AxisListType.X
F32 = mybir.dt.float32
U32 = mybir.dt.uint32
BF16 = mybir.dt.bfloat16

P = 128
BATCH, SEQ, D = 16, 256, 128
TILES = BATCH * SEQ // P
GT = 4
GN = GT * P
GROUPS = TILES // GT
GB = GN // SEQ
ST = SEQ // P
H, HD = 16, 64
PAIRS = H // 2
INNER = H * HD
NF = 128
LN_EPS = 1e-5
DEPTH, WINDOW = 6, 32
MLP = D * 4 * 2 // 3
MLP_CHUNKS = [(lo, min(P, MLP - lo)) for lo in range(0, MLP, P)]
EXP_LN = "natural_log_exp_and_others"
KEYS0, CAUSAL = SEQ, SEQ + P


def signals(nc, ctx, names):
    return [ctx.enter_context(nc.semaphore(n)) for n in names.split()]


def restart(nc, sems):
    numbers = sorted(s.num for s in sems)
    starts = [n for n in numbers if n - 1 not in numbers]
    ends = [n + 1 for n in numbers if n + 1 not in numbers]
    for a, b in zip(starts, ends):
        nc.all_engine_barrier(sems_to_clear=range(a, b))


def spread(a, n):
    return a.unsqueeze(-1).broadcast_to([*a.shape, n])


class Schedule:

    def __init__(self, stages):
        self.stages = stages
        self.steps = max(first + (units - 1) * every + 1 for units, first, every in stages.values() if units)

    def run(self, stage, i, do):
        units, first, every = self.stages[stage]
        n, rest = divmod(i - first, every)
        if rest == 0 and 0 <= n < units:
            do(n)


def pipeline(nc, step):
    step(None, 0, 1)
    with nc.Fori(0, (GROUPS - 2) // 2) as pair:
        g = 2 * pair
        step(g, g + 1, 0)
        step(g + 1, g + 2, 1)
    step(GROUPS - 2, GROUPS - 1, 0)
    step(GROUPS - 1, None, 1)


class LayerNorm:

    def __init__(self, nc, ctx, consts, bank, name, room=None):
        sb = lambda n, s: ctx.enter_context(nc.sbuf_tensor(n.replace("ln", name, 1), s, F32))
        self.ident, self.bank = consts["ident"], bank
        self.stats, self.moments = sb("ln_stats_t", [P, GT, 6]), sb("ln_moments_t", [P, GT, 2])
        self.var, self.log, self.rstd = sb("ln_var_t", [P, GT]), sb("ln_log_t", [P, GT]), sb("ln_rstd_t", [P, GT])
        self.xn, self.xnT = room or (sb("ln_xn", [P, GT, D]), sb("ln_xnT", [P, GN]))
        self.sems = signals(nc, ctx, "ln_stats ln_moments ln_var ln_log ln_rstd ln_normed ln_turned ln_ready".replace("ln_", name + "_"))
        (self.stats_done, self.moments_done, self.var_done, self.log_done, self.rstd_done, self.normed,
         self.turned, self.ready) = self.sems

    def vector(self, dve, x):
        self.gather_moments(dve, x)
        self.normalize(dve, x)

    def gather_moments(self, dve, x):
        for t in range(GT):
            dve.bn_stats(self.stats[:, t, :], x[:, t, :]).then_inc(self.stats_done, 1)
        dve.wait_ge(self.stats_done, GT)
        for t in range(GT):
            dve.bn_aggr(self.moments[:, t, :], self.stats[:, t, :]).then_inc(self.moments_done, 1)
        dve.wait_ge(self.moments_done, GT)
        dve.tensor_scalar(self.var[:], self.moments[:, :, 1], LN_EPS, None, ALU.add).then_inc(self.var_done, 1)

    def normalize(self, dve, x):
        dve.wait_ge(self.rstd_done, 1)
        for t in range(GT):
            dve.tensor_scalar(self.xn[:, t, :], x[:, t, :], self.moments[:, t, 0:1], self.rstd[:, t:t + 1],
                              ALU.subtract, ALU.mult).then_inc(self.normed, 1)

    def scalar(self, act, copy=True):
        self.root(act)
        if copy:
            self.copy(act)

    def root(self, act):
        act.wait_ge(self.var_done, 1)
        act.activation(self.log[:], self.var[:], ACT.Ln).then_inc(self.log_done, 1)
        act.wait_ge(self.log_done, 1)
        act.activation(self.rstd[:], self.log[:], ACT.Exp, scale=-0.5).then_inc(self.rstd_done, 1)

    def copy(self, act):
        act.wait_ge(self.turned, GT)
        act.copy(self.xnT[:], self.bank).then_inc(self.ready, 1)

    def tensor(self, pe):
        for t in range(GT):
            pe.wait_ge(self.normed, t + 1)
            pe.transpose(self.bank[:, t * P:(t + 1) * P], self.xn[:, t, :], self.ident).then_inc(self.turned, 1)


def favor_attention(nc, x, banks, consts, w):
    EPS = 1e-6 * NF
    QK_BANK, FEATURE_BANK, S_BANK, V_BANK, X_BANK = 0, 2, 4, 6, 7
    with ExitStack() as ctx:
        sb = lambda n, s: ctx.enter_context(nc.sbuf_tensor("favor_" + n, s, F32))
        ln = LayerNorm(nc, ctx, consts, banks[:, X_BANK, :], "favor_ln")
        xnT_of, v1_of = sb("xnT", [P, 2, GN]), sb("v1", [P, 2, GT, H, HD + 1])
        qs, ks = sb("qs", [P, 2, GN]), sb("ks", [P, 2, GN])
        qf, kf = sb("qf", [P, 2, GN]), sb("kf", [P, 2, GN])
        scores = sb("scores", [P, 2, GB, CAUSAL])
        den, rden = sb("den", [P, 2, GT]), sb("rden", [P, 2, GT])
        y, yT = sb("y", [P, 2, GT, D]), sb("yT", [P, PAIRS, GN])
        sems = signals(nc, ctx, "projected squared copied featured exped scored masked summed den_ready "
                                "rden_ready head_done v_projected v_copied y_turned y_copied out_ready added")
        (projected, squared, copied, featured, exped, scored, masked, summed, den_ready, rden_ready, head_done,
         v_projected, v_copied, y_turned, y_copied, out_ready, added) = sems
        sems = ln.sems + sems

        with nc.Block() as block:
            @block.sync
            def _(sp):
                sp.wait_ge(w["loaded"], w["total"])

            @block.vector
            def _(dve):
                for r in range(2):
                    dve.memset(v1_of[:, r, :, :, HD:HD + 1], 1.0)

            @block.scalar
            def _(act):
                act.preload_act_table_set(EXP_LN)

        def step(heads_of, make_of, parity):
            A, B = make_of is not None, heads_of is not None
            xa = x[:, bass.ds(make_of * GT, GT), :] if A else None
            xb = x[:, bass.ds(heads_of * GT, GT), :] if B else None
            xnT, xnT_new, v1, v1_new = xnT_of[:, parity], xnT_of[:, 1 - parity], v1_of[:, parity], v1_of[:, 1 - parity]
            schedule = Schedule({
                "moments": (A, 0, 1), "root": (A, 1, 1), "norm": (A, 2, 1), "turn_x": (A, 3, 1), "copy_x": (A, 4, 1),
                "project_v": (A * 2 * GT, 6, 2), "copy_v": (A * 2 * GT, 7, 2),
                "project": (B * PAIRS, 0, 2), "rows": (B * H, 1, 1), "features": (B * H, 2, 1), "exp": (B * H, 3, 1),
                "score": (B * H, 4, 1), "mask": (B * H, 5, 1), "values": (B * H, 6, 1), "normalize": (B * H, 7, 1),
                "turn_y": (B * PAIRS, 9, 2), "copy_y": (B * PAIRS, 10, 2)})

            with nc.Block() as block:
                @block.tensor
                def _(pe):
                    def project_v(n):
                        if n == 0:
                            pe.wait_ge(ln.ready, 1)
                        else:
                            pe.wait_ge(v_copied, n)
                        if B and n >= 2:
                            pe.wait_ge(y_copied, n - 1)
                        pe.matmul(banks[:, X_BANK, :], xnT_new[:, (n // 2) * P:(n // 2 + 1) * P],
                                  w["Wv"][:, (n % 2) * 512:(n % 2 + 1) * 512], start=True, stop=True).then_inc(v_projected, 1)

                    def project(j):
                        for n, name in enumerate(("Wq", "Wk")):
                            if j:
                                pe.wait_ge(squared, 2 * (2 * j - 1) + n + 1)
                                pe.wait_ge(copied, 2 * (2 * j - 1) + n + 1)
                            pe.matmul(banks[:, QK_BANK + n, :], w[name][:, j * P:(j + 1) * P], xnT, start=True, stop=True)\
                                .then_inc(projected, 1)

                    def features(h):
                        for n, s in enumerate((qs, ks)):
                            pe.wait_ge(squared, 2 * h + n + 1)
                            pe.wait_ge(copied, 2 * h + n + 1)
                            if h:
                                pe.wait_ge(exped, 2 * (h - 1) + n + 1)
                            pe.matmul(banks[:, FEATURE_BANK + n, :], w["Wfeat"][:], s[:, h % 2, :], start=True, stop=True)\
                                .then_inc(featured, 1)

                    def score(h):
                        pe.wait_ge(exped, 2 * h + 2)
                        for b in range(GB):
                            if h:
                                pe.wait_ge(masked, GB * (h - 1) + b + 1)
                            c = b * SEQ
                            pe.matmul(banks[:, S_BANK + b, 0:SEQ], kf[:, h % 2, c:c + P], qf[:, h % 2, c:c + SEQ],
                                      start=True, stop=True)
                            pe.matmul(banks[:, S_BANK + b, SEQ:CAUSAL], kf[:, h % 2, c + P:c + SEQ],
                                      qf[:, h % 2, c + P:c + SEQ], start=True, stop=True).then_inc(scored, 1)

                    def values(h):
                        pe.wait_ge(masked, GB * (h + 1))
                        if h:
                            pe.wait_ge(head_done, h)
                        for b in range(GB):
                            for i in range(ST):
                                out = banks[:, V_BANK, (b * ST + i) * (HD + 1):(b * ST + i + 1) * (HD + 1)]
                                for j in range(i + 1):
                                    c = (i * P if j == 0 else SEQ)
                                    last = pe.matmul(out, scores[:, h % 2, b, c:c + P], v1[:, b * ST + j, h, :],
                                                     start=(j == 0), stop=(j == i))
                        last.then_inc(summed, 1)

                    def turn_y(j):
                        pe.wait_ge(head_done, 2 * j + 2)
                        if j:
                            pe.wait_ge(y_copied, j)
                        if A:
                            pe.wait_ge(v_copied, min(j + 2, 2 * GT))
                        for t in range(GT):
                            last = pe.transpose(banks[:, X_BANK, t * P:(t + 1) * P], y[:, j % 2, t, :], consts["ident"])
                        last.then_inc(y_turned, 1)

                    for i in range(schedule.steps):
                        schedule.run("turn_x", i, lambda _: ln.tensor(pe))
                        schedule.run("values", i, values)
                        schedule.run("score", i, score)
                        schedule.run("features", i, features)
                        schedule.run("turn_y", i, turn_y)
                        schedule.run("project_v", i, project_v)
                        schedule.run("project", i, project)
                    if B:
                        pe.wait_ge(y_copied, PAIRS)
                        for t in range(GT):
                            for j in range(PAIRS):
                                last = pe.matmul(banks[:, QK_BANK, t * P:(t + 1) * P], yT[:, j, t * P:(t + 1) * P],
                                                 w["Wo"][:, j, :], start=(j == 0), stop=(j == PAIRS - 1))
                        last.then_inc(out_ready, 1)

                @block.scalar
                def _(act):
                    def copy_x(_):
                        act.wait_ge(ln.turned, GT)
                        act.copy(xnT_new, banks[:, X_BANK, :]).then_inc(ln.ready, 1)

                    def copy_v(n):
                        act.wait_ge(v_projected, n + 1)
                        act.copy(v1_new[:, n // 2, (n % 2) * PAIRS:(n % 2 + 1) * PAIRS, 0:HD],
                                 banks[:, X_BANK, :].rearrange("p (h d) -> p h d", d=HD)).then_inc(v_copied, 1)

                    def square(h):
                        r = h % 2
                        for n, s in enumerate((qs, ks)):
                            act.wait_ge(projected, h // 2 * 2 + n + 1)
                            if h >= 2:
                                act.wait_ge(featured, 2 * (h - 2) + n + 1)
                            act.activation(s[HD:P, h % 2, :], banks[r * HD:(r + 1) * HD, QK_BANK + n, :], ACT.Square)\
                                .then_inc(squared, 1)

                    def exp(h):
                        for n, f in enumerate((qf, kf)):
                            act.wait_ge(featured, 2 * h + n + 1)
                            if h >= 2:
                                act.wait_ge(scored, GB * (h - 1))
                            act.activation(f[:, h % 2, :], banks[:, FEATURE_BANK + n, :], ACT.Exp).then_inc(exped, 1)

                    def copy_y(j):
                        act.wait_ge(y_turned, j + 1)
                        act.copy(yT[:, j, :], banks[:, X_BANK, :]).then_inc(y_copied, 1)

                    for i in range(schedule.steps):
                        schedule.run("root", i, lambda _: ln.root(act))
                        schedule.run("copy_x", i, copy_x)
                        schedule.run("copy_v", i, copy_v)
                        schedule.run("copy_y", i, copy_y)
                        schedule.run("exp", i, exp)
                        schedule.run("rows", i, square)

                @block.vector
                def _(dve):
                    def copy(h):
                        r = h % 2
                        for n, s in enumerate((qs, ks)):
                            dve.wait_ge(projected, h // 2 * 2 + n + 1)
                            if h >= 2:
                                dve.wait_ge(featured, 2 * (h - 2) + n + 1)
                            dve.wait_ge(squared, 2 * h + n + 1)
                            dve.tensor_copy(s[0:HD, h % 2, :], banks[r * HD:(r + 1) * HD, QK_BANK + n, :]).then_inc(copied, 1)

                    def mask(h):
                        if h >= 2:
                            dve.wait_ge(summed, h - 1)
                        for b in range(GB):
                            dve.wait_ge(scored, GB * h + b + 1)
                            dve.tensor_tensor(scores[:, h % 2, b, :], banks[:, S_BANK + b, 0:CAUSAL], consts["causal"],
                                              ALU.mult).then_inc(masked, 1)

                    def normalize(h):
                        dve.wait_ge(summed, h + 1)
                        out = banks[:, V_BANK, 0:GT * (HD + 1)].rearrange("p (t e) -> p t e", e=HD + 1)
                        dve.tensor_scalar(den[:, h % 2, :], out[:, :, HD], EPS, None, ALU.add).then_inc(den_ready, 1)
                        dve.wait_ge(den_ready, h + 1)
                        dve.reciprocal(rden[:, h % 2, :], den[:, h % 2, :]).then_inc(rden_ready, 1)
                        dve.wait_ge(rden_ready, h + 1)
                        if h >= 4:
                            dve.wait_ge(y_turned, h // 2 - 1)
                        dve.tensor_tensor(y[:, h // 2 % 2, :, h % 2 * HD:(h % 2 + 1) * HD], out[:, :, 0:HD],
                                          spread(rden[:, h % 2, :], HD), ALU.mult).then_inc(head_done, 1)

                    for i in range(schedule.steps):
                        schedule.run("moments", i, lambda _: ln.gather_moments(dve, xa))
                        schedule.run("norm", i, lambda _: ln.normalize(dve, xa))
                        schedule.run("normalize", i, normalize)
                        schedule.run("mask", i, mask)
                        schedule.run("rows", i, copy)
                    if B:
                        dve.wait_ge(out_ready, 1)
                        dve.tensor_tensor(xb, xb, banks[:, QK_BANK, :].rearrange("p (t d) -> p t d", d=D), ALU.add)\
                            .then_inc(added, 1)
            restart(nc, sems)

        pipeline(nc, step)


def router_ffn(nc, x, banks, consts, w):
    DFF, NB, TOP, TAU, EPS = 512, 64, 8, 10.0, 1e-6
    CH = DFF // P
    with ExitStack() as ctx:
        sb = lambda n, s: ctx.enter_context(nc.sbuf_tensor("router_" + n, s, F32))
        ln = LayerNorm(nc, ctx, consts, banks[:, 2, :], "router_ln")
        ln2 = LayerNorm(nc, ctx, consts, banks[:, 3, :], "router_ln2")
        unT, vg = sb("unT", [P, NB]), sb("vg", [NB, D])
        rows, sq, ss, root = sb("unit_rows", [NB, 2, D]), sb("unit_sq", [NB, 2, D]), sb("unit_ss", [NB, 2]), sb("unit_root", [NB, 2])
        hT = sb("hT", [P, CH, GN])
        r, alpha, left = sb("r", [P, GT, NB]), sb("alpha", [P, GT, NB]), sb("left", [P, GT, NB])
        top, total, tanh, rtotal = sb("top", [P, GT, TOP]), sb("total", [P, GT]), sb("tanh", [P, GT]), sb("rtotal", [P, GT])
        phi, coef, picked, pickedT = sb("phi", [P, GT, NB]), sb("coef", [P, GT]), sb("picked", [P, GT, NB]), sb("pickedT", [NB, GN])
        steps, turned, read = signals(nc, ctx, "unit_steps unit_turned unit_read")
        sems = signals(nc, ctx, "widened gelu_done logits clipped exped alpha_ready top_ready left_ready phi_ready "
                                "total_ready tanh_ready eps_added coef_part coef_ready latent picked_part picked_ready "
                                "picked_turned picked_copied out_ready added")
        (widened, gelu_done, logits, clipped, exped, alpha_ready, top_ready, left_ready, phi_ready, total_ready,
         tanh_ready, eps_added, coef_part, coef_ready, latent, picked_part, picked_ready, picked_turned,
         picked_copied, out_ready, added) = sems
        sems = ln.sems + ln2.sems + [steps, turned, read] + sems

        with nc.Block() as block:
            @block.sync
            def _(sp):
                sp.wait_ge(w["loaded"], w["total"])
        with nc.Block() as block:
            @block.scalar
            def _(act):
                act.preload_act_table_set(EXP_LN)
                for n, name in enumerate(("U", "V")):
                    act.activation(sq[:, n, :], w[name][:], ACT.Square).then_inc(steps, 1)
                act.wait_ge(steps, 4)
                act.activation(root[:], ss[:], ACT.Ln).then_inc(steps, 1)
                act.wait_ge(steps, 5)
                act.activation(ss[:], root[:], ACT.Exp, scale=-0.5).then_inc(steps, 1)

            @block.vector
            def _(dve):
                dve.wait_ge(steps, 2)
                dve.tensor_reduce(ss[:], sq[:], AX_X, ALU.add).then_inc(steps, 1)
                dve.wait_ge(steps, 3)
                dve.tensor_scalar(ss[:], ss[:], EPS * EPS, None, ALU.max).then_inc(steps, 1)
                dve.wait_ge(steps, 6)
                for n, name in enumerate(("U", "V")):
                    dve.tensor_scalar(rows[:, n, :], w[name][:], ss[:, n:n + 1], None, ALU.mult).then_inc(steps, 1)
                dve.wait_ge(steps, 8)
                dve.tensor_tensor(vg[:], rows[:, 1, :], w["gamma"][:], ALU.mult).then_inc(read, 1)
                dve.wait_ge(turned, 1)
                dve.tensor_copy(unT[:], banks[:, 0, 0:NB]).then_inc(read, 1)

            @block.tensor
            def _(pe):
                pe.wait_ge(steps, 7)
                pe.transpose(banks[:, 0, 0:NB], rows[:, 0, :], consts["ident"][0:NB, 0:NB]).then_inc(turned, 1)
        restart(nc, sems)

        with nc.Fori(0, GROUPS) as g:
            xg = x[:, bass.ds(g * GT, GT), :]
            with nc.Block() as block:
                @block.tensor
                def _(pe):
                    ln.tensor(pe)
                    pe.wait_ge(ln.ready, 1)
                    for t in range(GT):
                        last = pe.matmul(banks[:, 5, t * NB:(t + 1) * NB], ln.xnT[:, t * P:(t + 1) * P], unT[:],
                                         start=True, stop=True)
                    last.then_inc(latent, 1)
                    for c in range(2):
                        pe.matmul(banks[:, c, :], w["W1T"][:, c * P:(c + 1) * P], ln.xnT[:], start=True, stop=True)\
                            .then_inc(widened, 1)
                    ln2.tensor(pe)
                    pe.wait_ge(ln2.ready, 1)
                    for t in range(GT):
                        o = banks[:, 4, t * NB:(t + 1) * NB]
                        pe.matmul(o, ln2.xnT[:, t * P:(t + 1) * P], w["RT"][:], start=True, stop=False)
                        last = pe.matmul(o, consts["ones"][0:1, 0:P], w["rb"][:], start=False, stop=True)
                    last.then_inc(logits, 1)
                    for c in range(2, CH):
                        pe.wait_ge(gelu_done, c - 1)
                        pe.matmul(banks[:, c % 2, :], w["W1T"][:, c * P:(c + 1) * P], ln.xnT[:], start=True, stop=True)\
                            .then_inc(widened, 1)
                    for t in range(GT):
                        pe.wait_ge(picked_ready, 1)
                        last = pe.transpose(banks[0:NB, 6, t * P:(t + 1) * P], picked[:, t, :], consts["ident"])
                    last.then_inc(picked_turned, 1)
                    pe.wait_ge(gelu_done, CH)
                    pe.wait_ge(picked_copied, 1)
                    for t in range(GT):
                        o = banks[:, 7, t * P:(t + 1) * P]
                        for c in range(CH):
                            pe.matmul(o, hT[:, c, t * P:(t + 1) * P], w["W2T"][:, c, :], start=(c == 0), stop=False)
                        last = pe.matmul(o, pickedT[:, t * P:(t + 1) * P], vg[:], start=False, stop=True)
                    last.then_inc(out_ready, 1)

                @block.scalar
                def _(act):
                    act.preload_act_table_set(EXP_LN)
                    ln.scalar(act)
                    ln2.scalar(act, copy=False)
                    act.wait_ge(ln2.turned, GT)
                    act.activation(ln2.xnT[:], banks[:, 3, :], ACT.Identity, bias=w["ln_b"][:], scale=w["ln_g"][:])\
                        .then_inc(ln2.ready, 1)
                    act.wait_ge(clipped, 1)
                    act.activation(r[:], r[:], ACT.Exp).then_inc(exped, 1)
                    act.wait_ge(exped, 1)
                    act.activation(alpha[:], r[:], ACT.Ln, bias=1.0).then_inc(alpha_ready, 1)
                    for c in range(CH):
                        act.wait_ge(widened, c + 1)
                        act.activation(hT[:, c, :], banks[:, c % 2, :], ACT.Gelu).then_inc(gelu_done, 1)
                    act.wait_ge(total_ready, 1)
                    act.activation(tanh[:], total[:], ACT.Tanh).then_inc(tanh_ready, 1)
                    act.wait_ge(picked_turned, 1)
                    act.copy(pickedT[:], banks[0:NB, 6, :]).then_inc(picked_copied, 1)

                @block.vector
                def _(dve):
                    ln.vector(dve, xg)
                    dve.wait_ge(ln.normed, GT)
                    ln2.vector(dve, ln.xn)
                    dve.wait_ge(logits, 1)
                    dve.tensor_scalar(r[:], banks[:, 4, 0:GT * NB].rearrange("p (t n) -> p t n", n=NB), -TAU, TAU,
                                      ALU.max, ALU.min).then_inc(clipped, 1)
                    dve.wait_ge(alpha_ready, 1)
                    for t in range(GT):
                        dve.max(top[:, t, :], alpha[:, t, :]).then_inc(top_ready, 1)
                    dve.wait_ge(top_ready, GT)
                    for t in range(GT):
                        dve.match_replace(left[:, t, :], top[:, t, :], alpha[:, t, :], -1.0).then_inc(left_ready, 1)
                    dve.tensor_reduce(total[:], top[:], AX_X, ALU.add).then_inc(total_ready, 1)
                    dve.wait_ge(left_ready, GT)
                    dve.scalar_tensor_tensor(phi[:], left[:], 0.0, alpha[:], ALU.is_lt, ALU.mult).then_inc(phi_ready, 1)
                    dve.wait_ge(total_ready, 1)
                    dve.tensor_scalar(rtotal[:], total[:], EPS, None, ALU.add).then_inc(eps_added, 1)
                    dve.wait_ge(eps_added, 1)
                    dve.reciprocal(coef[:], rtotal[:]).then_inc(coef_part, 1)
                    dve.wait_ge(coef_part, 1)
                    dve.wait_ge(tanh_ready, 1)
                    dve.tensor_tensor(coef[:], coef[:], tanh[:], ALU.mult).then_inc(coef_ready, 1)
                    dve.wait_ge(phi_ready, 1)
                    dve.wait_ge(latent, 1)
                    dve.tensor_tensor(picked[:], phi[:], banks[:, 5, 0:GT * NB].rearrange("p (t n) -> p t n", n=NB),
                                      ALU.mult).then_inc(picked_part, 1)
                    dve.wait_ge(coef_ready, 1)
                    dve.wait_ge(picked_part, 1)
                    dve.tensor_tensor(picked[:], picked[:], spread(coef[:], NB), ALU.mult).then_inc(picked_ready, 1)
                    dve.wait_ge(out_ready, 1)
                    dve.tensor_tensor(xg, xg, banks[:, 7, :].rearrange("p (t d) -> p t d", d=D), ALU.add)\
                        .then_inc(added, 1)
            restart(nc, sems)


def cosine_attention(nc, x, banks, consts, w):
    HALF = INNER // 2
    UP = 2.0 ** 32
    QK = 4 * GT
    UNITS = QK + 2 * GT
    S_BANK, T_BANK, V_BANK, O_BANK, A_BANK, X_BANK = 0, 2, 3, 4, 5, 7
    with ExitStack() as ctx:
        sb = lambda n, s: ctx.enter_context(nc.sbuf_tensor("cosine_" + n, s, F32))
        ln = LayerNorm(nc, ctx, consts, banks[:, X_BANK, :], "cosine_ln")
        peak, npeak, up = sb("peak", [P, H]), sb("npeak", [P, H]), sb("up", [P, 1])
        qk_of = sb("qk", [P, 2, 2, GT, INNER])
        v1_of = sb("v1", [P, 2, GT, H, HD + 1])
        sq = sb("sq", [P, 3, HALF])
        ss, lg, inv = sb("ss", [P, 2, GT, H]), sb("lg", [P, 2, GT, H]), sb("inv", [P, 2, GT, H])
        turned_qk = sb("turned_qk", [P, 2, 2, GN])
        probs = sb("probs", [P, 2, GB, ST * SEQ])
        rden = sb("rden", [P, 2, GT])
        y = sb("y", [P, 2, GT, D])
        sems = signals(nc, ctx, "projected copied squared reduced clamped logged inverted unit v_copied qk_turned "
                                "qk_copied scored exped summed rden_ready head_done y_turned y_copied out_ready added "
                                "peak_ready npeak_ready")
        (projected, copied, squared, reduced, clamped, logged, inverted, unit, v_copied, qk_turned, qk_copied, scored,
         exped, summed, rden_ready, head_done, y_turned, y_copied, out_ready, added, peak_ready, npeak_ready) = sems
        sems = ln.sems + sems
        heads = lambda a: a.rearrange("p (h d) -> p h d", d=HD)
        tiled = lambda a: a.rearrange("p (t d) -> p t d", d=D)

        with nc.Block() as block:
            @block.sync
            def _(sp):
                sp.wait_ge(w["loaded"], w["total"])
        with nc.Block() as block:
            @block.scalar
            def _(act):
                act.preload_act_table_set(EXP_LN)
                act.activation(peak[:], w["scale"][:], ACT.Exp).then_inc(peak_ready, 1)

            @block.vector
            def _(dve):
                for r in range(2):
                    dve.memset(v1_of[:, r, :, :, HD:HD + 1], 1.0)
                dve.memset(up[:], 16.0 * float(np.log(2.0)))
                dve.wait_ge(peak_ready, 1)
                dve.tensor_scalar(npeak[:], peak[:], -1.0, None, ALU.mult).then_inc(npeak_ready, 1)
        restart(nc, sems)

        is_qk = lambda n: n % 6 < 4
        qk_number = lambda n: n // 6 * 4 + n % 6
        v_number = lambda n: n // 6 * 2 + n % 6 - 4
        where = lambda k: (k // 4, k // 2 % 2, k % 2)

        def step(heads_of, make_of, parity):
            A, B = make_of is not None, heads_of is not None
            xa = x[:, bass.ds(make_of * GT, GT), :] if A else None
            xb = x[:, bass.ds(heads_of * GT, GT), :] if B else None
            qk, qk_new, v1, v1_new = qk_of[:, parity], qk_of[:, 1 - parity], v1_of[:, parity], v1_of[:, 1 - parity]
            yT = lambda j: qk[:, 0, :, j * P:(j + 1) * P]
            part = lambda k: qk_new[:, where(k)[1], where(k)[0], where(k)[2] * HALF:(where(k)[2] + 1) * HALF]
            schedule = Schedule({
                "measure": (A, 0, 1), "root": (A, 1, 1), "norm": (A, 2, 1), "turn_x": (A, 3, 1), "copy_x": (A, 4, 1),
                "project": (A * UNITS, 5, 1), "take": (A * UNITS, 6, 1), "reduce": (A * UNITS, 7, 1),
                "clamp": (A * GT, 11, 6), "invert": (A * GT, 12, 6), "unit_q": (A * GT, 13, 6), "unit_k": (A * GT, 14, 6),
                "turn": (B * H, 0, 1), "turned": (B * H, 1, 1), "score": (B * H, 3, 1), "exp": (B * H, 4, 1),
                "values": (B * H, 5, 1), "normalize": (B * H, 6, 1), "turn_y": (B * PAIRS, 8, 2), "copy_y": (B * PAIRS, 9, 2)})

            with nc.Block() as block:
                @block.tensor
                def _(pe):
                    def project(n):
                        if n == 0:
                            pe.wait_ge(ln.ready, 1)
                        if n >= 2:
                            if is_qk(n - 2):
                                pe.wait_ge(copied, qk_number(n - 2) + 1)
                            else:
                                pe.wait_ge(v_copied, v_number(n - 2) + 1)
                        t, m, half = n // 6, n % 6 // 2, n % 2
                        c = m * INNER + half * HALF
                        pe.matmul(banks[:, A_BANK + n % 2, :], ln.xnT[:, t * P:(t + 1) * P], w["Wqkv"][:, c:c + HALF],
                                  start=True, stop=True).then_inc(projected, 1)

                    def turn_qk(k):
                        if k:
                            pe.wait_ge(qk_copied, k)
                        j, m = k // 2, k % 2
                        for t in range(GT):
                            last = pe.transpose(banks[:, T_BANK, t * P:(t + 1) * P], qk[:, m, t, j * P:(j + 1) * P],
                                                consts["ident"])
                        last.then_inc(qk_turned, 1)

                    def score(h):
                        pe.wait_ge(qk_copied, 2 * (h // 2) + 2)
                        q, k = (turned_qk[h % 2 * HD:(h % 2 + 1) * HD, h // 2 % 2, m, :] for m in range(2))
                        for b in range(GB):
                            if h:
                                pe.wait_ge(exped, GB * (h - 1) + b + 1)
                            for s in range(ST):
                                c = b * SEQ
                                last = pe.matmul(banks[:, S_BANK + b, s * SEQ:(s + 1) * SEQ],
                                                 k[:, c + s * P:c + (s + 1) * P], q[:, c:c + SEQ], start=True, stop=True)
                            last.then_inc(scored, 1)

                    def values(h):
                        pe.wait_ge(exped, GB * (h + 1))
                        if h:
                            pe.wait_ge(head_done, h)
                        for b in range(GB):
                            for i in range(ST):
                                o = banks[:, V_BANK, (b * ST + i) * (HD + 1):(b * ST + i + 1) * (HD + 1)]
                                for s in range(ST):
                                    c = s * SEQ + i * P
                                    last = pe.matmul(o, probs[:, h % 2, b, c:c + P], v1[:, b * ST + s, h, :],
                                                     start=(s == 0), stop=(s == ST - 1))
                        last.then_inc(summed, 1)

                    def turn_y(j):
                        pe.wait_ge(head_done, 2 * j + 2)
                        if j:
                            pe.wait_ge(y_copied, j)
                        for t in range(GT):
                            last = pe.transpose(banks[:, O_BANK, t * P:(t + 1) * P], y[:, j % 2, t, :], consts["ident"])
                        last.then_inc(y_turned, 1)

                    for i in range(schedule.steps):
                        schedule.run("turn_x", i, lambda _: ln.tensor(pe))
                        schedule.run("project", i, project)
                        schedule.run("turn_y", i, turn_y)
                        schedule.run("values", i, values)
                        schedule.run("score", i, score)
                        schedule.run("turn", i, turn_qk)
                    if B:
                        pe.wait_ge(y_copied, PAIRS)
                        if A:
                            pe.wait_ge(ln.ready, 1)
                        for t in range(GT):
                            o = banks[:, X_BANK, t * P:(t + 1) * P]
                            for j in range(PAIRS):
                                pe.matmul(o, yT(j)[:, t, :], w["Wo"][:, j, :], start=(j == 0), stop=False)
                            last = pe.matmul(o, consts["ones"][0:1, 0:P], w["bo"][:], start=False, stop=True)
                        last.then_inc(out_ready, 1)

                @block.scalar
                def _(act):
                    def take(n):
                        act.wait_ge(projected, n + 1)
                        if not is_qk(n):
                            v = v_number(n)
                            act.copy(v1_new[:, v // 2, (v % 2) * PAIRS:(v % 2 + 1) * PAIRS, 0:HD],
                                     heads(banks[:, A_BANK + n % 2, :])).then_inc(v_copied, 1)
                            return
                        k = qk_number(n)
                        act.copy(part(k), banks[:, A_BANK + n % 2, :]).then_inc(copied, 1)
                        act.wait_ge(copied, k + 1)
                        if k >= 3:
                            act.wait_ge(reduced, k - 2)
                        act.activation(sq[:, k % 3, :], part(k), ACT.Square).then_inc(squared, 1)

                    def invert(t):
                        act.wait_ge(clamped, t + 1)
                        act.activation(lg[:, :, t, :], ss[:, :, t, :], ACT.Ln).then_inc(logged, 1)
                        act.wait_ge(logged, t + 1)
                        act.activation(inv[:, :, t, :], lg[:, :, t, :], ACT.Exp, bias=up[:], scale=-0.5).then_inc(inverted, 1)

                    def copy_qk(k):
                        act.wait_ge(qk_turned, k + 1)
                        if k >= 4:
                            act.wait_ge(scored, 2 * GB * (k // 2 - 1))
                        act.copy(turned_qk[:, k // 2 % 2, k % 2, :], banks[:, T_BANK, :]).then_inc(qk_copied, 1)

                    def exp(h):
                        for b in range(GB):
                            act.wait_ge(scored, GB * h + b + 1)
                            if h >= 2:
                                act.wait_ge(summed, h - 1)
                            act.activation(probs[:, h % 2, b, :], banks[:, S_BANK + b, :], ACT.Exp,
                                           bias=npeak[:, h:h + 1], scale=peak[:, h:h + 1]).then_inc(exped, 1)

                    def copy_y(j):
                        act.wait_ge(y_turned, j + 1)
                        act.copy(yT(j), tiled(banks[:, O_BANK, :])).then_inc(y_copied, 1)

                    for i in range(schedule.steps):
                        schedule.run("root", i, lambda _: ln.root(act))
                        schedule.run("copy_x", i, lambda _: ln.copy(act))
                        schedule.run("turned", i, copy_qk)
                        schedule.run("exp", i, exp)
                        schedule.run("take", i, take)
                        schedule.run("invert", i, invert)
                        schedule.run("copy_y", i, copy_y)

                @block.vector
                def _(dve):
                    def reduce(n):
                        if not is_qk(n):
                            return
                        k = qk_number(n)
                        t, m, half = where(k)
                        dve.wait_ge(squared, k + 1)
                        dve.tensor_reduce(ss[:, m, t, half * PAIRS:(half + 1) * PAIRS], heads(sq[:, k % 3, :]), AX_X, ALU.add)\
                            .then_inc(reduced, 1)

                    def clamp(t):
                        dve.wait_ge(reduced, 4 * t + 4)
                        dve.tensor_scalar(ss[:, :, t, :], ss[:, :, t, :], 1e-24, UP, ALU.max, ALU.mult).then_inc(clamped, 1)

                    def make_unit(t, m):
                        dve.wait_ge(inverted, t + 1)
                        a = heads(qk_new[:, m, t, :])
                        dve.tensor_tensor(a, a, spread(inv[:, m, t, :], HD), ALU.mult).then_inc(unit, 1)

                    def normalize(h):
                        dve.wait_ge(summed, h + 1)
                        o = banks[:, V_BANK, 0:GT * (HD + 1)].rearrange("p (t e) -> p t e", e=HD + 1)
                        dve.reciprocal(rden[:, h % 2, :], o[:, :, HD]).then_inc(rden_ready, 1)
                        dve.wait_ge(rden_ready, h + 1)
                        if h >= 4:
                            dve.wait_ge(y_turned, h // 2 - 1)
                        dve.tensor_tensor(y[:, h // 2 % 2, :, h % 2 * HD:(h % 2 + 1) * HD], o[:, :, 0:HD],
                                          spread(rden[:, h % 2, :], HD), ALU.mult).then_inc(head_done, 1)

                    for i in range(schedule.steps):
                        schedule.run("measure", i, lambda _: ln.gather_moments(dve, xa))
                        schedule.run("norm", i, lambda _: ln.normalize(dve, xa))
                        schedule.run("normalize", i, normalize)
                        schedule.run("reduce", i, reduce)
                        schedule.run("clamp", i, clamp)
                        schedule.run("unit_q", i, lambda t: make_unit(t, 0))
                        schedule.run("unit_k", i, lambda t: make_unit(t, 1))
                    if B:
                        dve.wait_ge(out_ready, 1)
                        dve.tensor_tensor(xb, xb, tiled(banks[:, X_BANK, :]), ALU.add).then_inc(added, 1)
            restart(nc, sems)

        pipeline(nc, step)


def int4_linear(nc, x, banks, consts, w):
    RANK, QMAX = 16, 7.0
    ROUND = 1.5 * 2.0 ** 23
    with ExitStack() as ctx:
        sb = lambda n, s: ctx.enter_context(nc.sbuf_tensor("int4_" + n, s, F32))
        ln = LayerNorm(nc, ctx, consts, banks[:, 2, :], "int4_ln")
        rowmax, allmax, step, rstep = sb("rowmax", [P, 1]), sb("allmax", [P, 1]), sb("step", [P, 1]), sb("rstep", [P, 1])
        wq, low = sb("wq", [P, D]), sb("low", [RANK, GN])
        quant, quant_max = signals(nc, ctx, "quant_steps quant_max")
        sems = signals(nc, ctx, "low_ready low_copied out_ready added")
        low_ready, low_copied, out_ready, added = sems
        sems = ln.sems + [quant, quant_max] + sems

        with nc.Block() as block:
            @block.sync
            def _(sp):
                sp.wait_ge(w["loaded"], w["total"])
        with nc.Block() as block:
            @block.vector
            def _(dve):
                dve.tensor_reduce(rowmax[:], w["kernel"][:], AX_X, ALU.max, apply_absolute_value=True).then_inc(quant, 1)
                dve.wait_ge(quant_max, 1)
                dve.tensor_scalar(step[:], allmax[:], 1.0 / QMAX, None, ALU.mult).then_inc(quant, 1)
                dve.wait_ge(quant, 2)
                dve.reciprocal(rstep[:], step[:]).then_inc(quant, 1)
                dve.wait_ge(quant, 3)
                dve.tensor_scalar(wq[:], w["kernel"][:], rstep[:], None, ALU.mult).then_inc(quant, 1)
                dve.wait_ge(quant, 4)
                dve.tensor_scalar(wq[:], wq[:], ROUND, None, ALU.add).then_inc(quant, 1)
                dve.wait_ge(quant, 5)
                dve.tensor_scalar(wq[:], wq[:], -ROUND, None, ALU.add).then_inc(quant, 1)
                dve.wait_ge(quant, 6)
                dve.tensor_scalar(wq[:], wq[:], -8.0, 7.0, ALU.max, ALU.min).then_inc(quant, 1)
                dve.wait_ge(quant, 7)
                dve.tensor_scalar(wq[:], wq[:], step[:], None, ALU.mult).then_inc(quant, 1)

            @block.gpsimd
            def _(pool):
                pool.wait_ge(quant, 1)
                pool.partition_all_reduce(allmax[:], rowmax[:], P, bass.bass_isa.ReduceOp.max).then_inc(quant_max, 1)

            @block.scalar
            def _(act):
                act.preload_act_table_set(EXP_LN)
        restart(nc, sems)

        with nc.Fori(0, GROUPS) as g:
            xg = x[:, bass.ds(g * GT, GT), :]
            with nc.Block() as block:
                @block.tensor
                def _(pe):
                    ln.tensor(pe)
                    pe.wait_ge(ln.ready, 1)
                    pe.matmul(banks[0:RANK, 0, :], w["a"][:], ln.xnT[:], start=True, stop=True).then_inc(low_ready, 1)
                    pe.wait_ge(low_copied, 1)
                    for t in range(GT):
                        o, c = banks[:, 1, t * P:(t + 1) * P], slice(t * P, (t + 1) * P)
                        pe.matmul(o, ln.xnT[:, c], wq[:], start=True, stop=False)
                        pe.matmul(o, low[:, c], w["b"][:], start=False, stop=False)
                        last = pe.matmul(o, consts["ones"][0:1, 0:P], w["bias"][:], start=False, stop=True)
                    last.then_inc(out_ready, 1)

                @block.scalar
                def _(act):
                    ln.scalar(act)
                    act.wait_ge(low_ready, 1)
                    act.copy(low[:], banks[0:RANK, 0, :]).then_inc(low_copied, 1)

                @block.vector
                def _(dve):
                    ln.vector(dve, xg)
                    dve.wait_ge(out_ready, 1)
                    dve.tensor_tensor(xg, xg, banks[:, 1, :].rearrange("p (t d) -> p t d", d=D), ALU.add)\
                        .then_inc(added, 1)
            restart(nc, sems)


def state_space(nc, x, banks, consts, w):
    INNER_D, NS, RANK = 256, 16, 8
    SPLIT = 3 * 32
    CH = INNER_D // P
    with ExitStack() as ctx:
        sb = lambda n, s, d=F32: ctx.enter_context(nc.sbuf_tensor("mamba_" + n, s, d))
        ln = LayerNorm(nc, ctx, consts, banks[:, 0, :], "mamba_ln")
        a_neg = sb("a_neg", [P, CH, NS])
        xs_of, gate_of, delta_of, dx_of = (sb(n, [P, 2, CH, GN]) for n in ("xs", "gate", "delta", "dx"))
        whole = sb("b_and_c", [SPLIT, 2, GN])
        parts_of = sb("parts", [SPLIT, 2, 2, GN], BF16)
        pick = sb("pick", [SPLIT, NS * P], BF16)
        v = sb("dt_in", [P, CH, GN])
        dp = ln.xn[0:RANK].rearrange("p t d -> p (t d)")
        decay, drive, state = (sb(n, [P, 2, CH, GN]) for n in ("decay", "drive", "state"))
        seen = sb("seen", [P, 3, CH, GN])
        c_wide = sb("c_wide", [P, 2, GN])
        rows = drive[0:SPLIT].rearrange("p a c n -> p (a c n)")
        prep, pick_loaded = signals(nc, ctx, "prep pick_loaded")
        sems = signals(nc, ctx, "widened xs_ready gate_ready lowered dp_biased whole_ready high_part rest middle_part "
                                "low_part dt_ready dt_biased mag_ready mag_exp mag_log delta_ready dx_ready b_spread "
                                "c_spread c_copied decayed driven scanned read_out gathered skip_added gated out_ready added")
        (widened, xs_ready, gate_ready, lowered, dp_biased, whole_ready, high_part, rest, middle_part, low_part,
         dt_ready, dt_biased, mag_ready, mag_exp, mag_log, delta_ready, dx_ready, b_spread, c_spread, c_copied, decayed,
         driven, scanned, read_out, gathered, skip_added, gated, out_ready, added) = sems
        sems = ln.sems + [prep] + sems

        with nc.Block() as block:
            @block.sync
            def _(sp):
                sp.wait_ge(w["loaded"], w["total"])
                sp.dma_start(rows, w["pick"]).then_inc(pick_loaded, 16)
                sp.wait_ge(pick_loaded, 16)
        with nc.Block() as block:
            @block.scalar
            def _(act):
                act.preload_act_table_set(EXP_LN)
                act.activation(a_neg[:], w["A_log"][:], ACT.Exp).then_inc(prep, 1)

            @block.vector
            def _(dve):
                dve.wait_ge(prep, 1)
                dve.tensor_scalar(a_neg[:], a_neg[:], -1.0, None, ALU.mult).then_inc(prep, 1)
                dve.tensor_copy(pick[:], rows)
                for r in range(2):
                    for c in range(CH):
                        for b in range(GB):
                            dve.memset(decay[:, r, c, b * SEQ:b * SEQ + 1], 0.0)
        restart(nc, sems)

        MEASURE, NORMALIZE, TURN, TURNED, WIDEN, SILU, LOWER, BIAS, LOWER_C, BIAS_C, LAST_DT, SPLIT_ALL, SOFTPLUS, DELTA = \
            0, 1, 2, 3, 4, 4, 6, 7, 8, 9, 10, 11, 12, 13

        def step(scan_of, make_of, parity):
            S, A = scan_of is not None, make_of is not None
            xg = x[:, bass.ds(scan_of * GT, GT), :] if S else None
            xa = x[:, bass.ds(make_of * GT, GT), :] if A else None
            xs, gate, delta, dx = (a[:, parity] for a in (xs_of, gate_of, delta_of, dx_of))
            xs_new, gate_new, delta_new, dx_new = (a[:, 1 - parity] for a in (xs_of, gate_of, delta_of, dx_of))
            yT = xs
            mag = delta_new
            parts, parts_new = parts_of[:, parity], parts_of[:, 1 - parity]

            with nc.Block() as block:
                @block.tensor
                def _(pe):
                    def lower(n):
                        name, lo, m = (("Wdp", 0, RANK), ("Wbc", 0, SPLIT), ("Wbc", SPLIT, SPLIT))[n]
                        for c in range(CH):
                            last = pe.matmul(banks[0:m, n % 2, :], w[name][:, c, lo:lo + m], xs_new[:, c, :],
                                             start=(c == 0), stop=(c == CH - 1))
                        last.then_inc(lowered, 1)

                    def dt(c):
                        pe.matmul(banks[:, 1 - c, :], w["Wdt"][:, c * P:(c + 1) * P], dp, start=True, stop=True)\
                            .then_inc(dt_ready, 1)

                    def make(n):
                        if n == TURN:
                            ln.tensor(pe)
                        if n == WIDEN:
                            pe.wait_ge(ln.ready, 1)
                            for c in range(2 * CH):
                                if c >= 2:
                                    pe.wait_ge(xs_ready, c - 1)
                                pe.matmul(banks[:, c % 2, :], w["Win"][:, c * P:(c + 1) * P], ln.xnT[:], start=True, stop=True)\
                                    .then_inc(widened, 1)
                        if n == LOWER:
                            pe.wait_ge(xs_ready, CH)
                            pe.wait_ge(gate_ready, CH)
                            lower(0)
                            lower(1)
                        if n == LOWER_C:
                            pe.wait_ge(dp_biased, 1)
                            lower(2)
                            pe.wait_ge(whole_ready, 1)
                            dt(0)
                        if n == LAST_DT:
                            pe.wait_ge(whole_ready, 2)
                            dt(1)

                    def gather(n):
                        pe.wait_ge(read_out, n + 1)
                        for c in range(CH):
                            last = pe.matmul(banks[:, 6 + c, :], consts["ident"], seen[:, n % 3, c, :],
                                             start=(n == 0), stop=(n == NS - 1))
                        last.then_inc(gathered, 1)

                    for n in range(NS):
                        if S:
                            row = pick[:, n * P:(n + 1) * P]
                            if n >= 2:
                                pe.wait_ge(driven, n - 1)
                            pe.matmul(banks[:, 2 + n % 2, :], row, parts[:, 0, :], start=True, stop=True).then_inc(b_spread, 1)
                            if n >= 2:
                                pe.wait_ge(c_copied, n - 1)
                            pe.matmul(banks[:, 4 + n % 2, :], row, parts[:, 1, :], start=True, stop=True).then_inc(c_spread, 1)
                            if n >= 2:
                                gather(n - 2)
                        if A:
                            make(n)
                    if S:
                        gather(NS - 2)
                        gather(NS - 1)
                        if A:
                            pe.wait_ge(dt_biased, CH)
                        pe.wait_ge(gated, CH)
                        for t in range(GT):
                            o = banks[:, 0, t * P:(t + 1) * P]
                            for c in range(CH):
                                pe.matmul(o, yT[:, c, t * P:(t + 1) * P], w["Wout"][:, c, :], start=(c == 0), stop=False)
                            last = pe.matmul(o, consts["ones"][0:1, 0:P], w["bout"][:], start=False, stop=True)
                        last.then_inc(out_ready, 1)

                @block.scalar
                def _(act):
                    def make(n):
                        if n == MEASURE:
                            ln.root(act)
                        if n == TURNED:
                            ln.copy(act)
                        if n == SILU:
                            for c in range(2 * CH):
                                into, ready = (xs_new, xs_ready) if c < CH else (gate_new, gate_ready)
                                act.wait_ge(widened, c + 1)
                                act.activation(into[:, c % CH, :], banks[:, c % 2, :], ACT.Silu, bias=w["bin"][:, c:c + 1])\
                                    .then_inc(ready, 1)
                            act.preload_act_table_set(EXP_LN)
                        if n == SOFTPLUS:
                            act.wait_ge(dt_biased, CH)
                            act.activation(mag[:], v[:], ACT.Abs).then_inc(mag_ready, 1)
                            act.wait_ge(mag_ready, 1)
                            act.activation(mag[:], mag[:], ACT.Exp, scale=-1.0).then_inc(mag_exp, 1)
                            act.wait_ge(mag_exp, 1)
                            act.activation(mag[:], mag[:], ACT.Ln, bias=1.0).then_inc(mag_log, 1)

                    for n in range(NS):
                        if S:
                            if n >= 2:
                                act.wait_ge(scanned, CH * (n - 1))
                            for c in range(CH):
                                into = decay[:, n % 2, c, :].rearrange("p (b s) -> p b s", s=SEQ)[:, :, 1:]
                                act.activation(into, delta[:, c, :].rearrange("p (b s) -> p b s", s=SEQ)[:, :, 1:], ACT.Exp,
                                               scale=a_neg[:, c, n:n + 1]).then_inc(decayed, 1)
                            act.wait_ge(c_spread, n + 1)
                            if n >= 2:
                                act.wait_ge(read_out, n - 1)
                            act.copy(c_wide[:, n % 2, :], banks[:, 4 + n % 2, :]).then_inc(c_copied, 1)
                        if A:
                            make(n)

                @block.gpsimd
                def _(pool):
                    for n in range(NS if S else 0):
                        pool.wait_ge(scanned, CH * (n + 1))
                        pool.wait_ge(c_copied, n + 1)
                        if n >= 3:
                            pool.wait_ge(gathered, n - 2)
                        pool.tensor_tensor(seen[:, n % 3, :, :], state[:, n % 2, :, :],
                                           c_wide[:, n % 2:n % 2 + 1, :].broadcast_to([P, CH, GN]), ALU.mult)\
                            .then_inc(read_out, 1)

                @block.vector
                def _(dve):
                    def bias_whole(n):
                        dve.wait_ge(lowered, n + 2)
                        dve.tensor_scalar(whole[:, n, :], banks[0:SPLIT, 1 - n, :], w["bbc"][:, n:n + 1], None, ALU.add)\
                            .then_inc(whole_ready, 1)

                    def bias_dt(c):
                        dve.wait_ge(dt_ready, c + 1)
                        dve.tensor_scalar(v[:, c, :], banks[:, 1 - c, :], w["bdt"][:, c:c + 1], None, ALU.add).then_inc(dt_biased, 1)

                    def make(n):
                        if n == MEASURE:
                            ln.gather_moments(dve, xa)
                        if n == NORMALIZE:
                            ln.normalize(dve, xa)
                        if n == BIAS:
                            dve.wait_ge(lowered, 1)
                            dve.tensor_scalar(dp, banks[0:RANK, 0, :], w["bdp"][:], None, ALU.add).then_inc(dp_biased, 1)
                            bias_whole(0)
                        if n == BIAS_C:
                            bias_whole(1)
                            bias_dt(0)
                        if n == SPLIT_ALL:
                            bias_dt(1)
                            dve.tensor_copy(parts_new, whole[:]).then_inc(high_part, 1)
                            for lo, hi in ((32, 64), (64, SPLIT)):
                                dve.wait_ge(high_part, 1)
                                dve.tensor_tensor(whole[lo:hi], whole[lo:hi], parts_new[lo:hi], ALU.subtract).then_inc(rest, 1)
                            for m, (lo, hi) in enumerate(((32, 64), (64, SPLIT))):
                                dve.wait_ge(rest, m + 1)
                                dve.tensor_copy(parts_new[lo:hi], whole[lo:hi]).then_inc(middle_part, 1)
                            dve.wait_ge(middle_part, 2)
                            dve.tensor_tensor(parts_new[64:SPLIT], whole[64:SPLIT], parts_new[64:SPLIT], ALU.subtract)\
                                .then_inc(low_part, 1)
                        if n == DELTA:
                            dve.wait_ge(mag_log, 1)
                            dve.scalar_tensor_tensor(delta_new, v[:], 0.0, mag[:], ALU.max, ALU.add).then_inc(delta_ready, 1)
                            dve.wait_ge(delta_ready, 1)
                            dve.wait_ge(xs_ready, CH)
                            dve.tensor_tensor(dx_new, delta_new, xs_new, ALU.mult).then_inc(dx_ready, 1)

                    for n in range(NS):
                        if S:
                            if n >= 2:
                                dve.wait_ge(scanned, CH * (n - 1))
                            dve.wait_ge(b_spread, n + 1)
                            dve.tensor_tensor(drive[:, n % 2, :, :], dx,
                                              banks[:, 2 + n % 2:3 + n % 2, :].broadcast_to([P, CH, GN]), ALU.mult)\
                                .then_inc(driven, 1)
                        if A:
                            make(n)
                        if S:
                            dve.wait_ge(driven, n + 1)
                            if n >= 2:
                                dve.wait_ge(read_out, n - 1)
                            for c in range(CH):
                                dve.wait_ge(decayed, CH * n + c + 1)
                                dve.tensor_tensor_scan(state[:, n % 2, c, :], decay[:, n % 2, c, :], drive[:, n % 2, c, :],
                                                       0.0, ALU.mult, ALU.add).then_inc(scanned, 1)
                    if S:
                        dve.wait_ge(gathered, NS)
                        for c in range(CH):
                            dve.scalar_tensor_tensor(yT[:, c, :], xs[:, c, :], w["Dp"][:, c:c + 1], banks[:, 6 + c, :],
                                                     ALU.mult, ALU.add).then_inc(skip_added, 1)
                            dve.wait_ge(skip_added, c + 1)
                            dve.tensor_tensor(yT[:, c, :], yT[:, c, :], gate[:, c, :], ALU.mult).then_inc(gated, 1)
                        dve.wait_ge(out_ready, 1)
                        dve.tensor_tensor(xg, xg, banks[:, 0, :].rearrange("p (t d) -> p t d", d=D), ALU.add)\
                            .then_inc(added, 1)
            restart(nc, sems)

        pipeline(nc, step)


def expert_ffn(nc, x, banks, consts, w):
    E, TOP, DFF, EPS = 8, 2, 512, 1e-8
    CH = DFF // P
    WIDE_BANKS = (0, 1, 3)
    with ExitStack() as ctx:
        sb = lambda n, s, d=F32: ctx.enter_context(nc.sbuf_tensor("experts_" + n, s, d))
        ln = LayerNorm(nc, ctx, consts, banks[:, 7, :], "experts_ln")
        ln2 = LayerNorm(nc, ctx, consts, banks[:, 7, :], "experts_ln2")
        hT = sb("hT", [P, 2, CH, GN])
        peak, z, mass, rmass, prob = sb("peak", [P, GT]), sb("z", [P, GT, E]), sb("mass", [P, GT]), sb("rmass", [P, GT]), sb("prob", [P, GT, E])
        top, place, placef = sb("top", [P, GT, 8]), sb("place", [P, GT, 8], U32), sb("placef", [P, GT, 8])
        pair, rpair, share = sb("pair", [P, GT]), sb("rpair", [P, GT]), sb("share", [P, GT, TOP])
        part, weightT = sb("part", [P, TOP, GT, E]), sb("weightT", [E, GN])
        xnT_of, weight_of, acc_of = sb("xnT", [P, 2, GN]), sb("weight", [P, 2, GT, E]), sb("acc", [P, 2, GT, D])
        sums = sb("sums", [P, GT, D])
        sems = signals(nc, ctx, "logits peak_ready centred exped mass_ready rmass_ready prob_ready top_ready placed "
                                "place_copied pair_sum pair_eps rpair_ready share_ready parted weighted w_turned "
                                "w_copied bias_ready acc_ready widened gelu_done narrowed taken scaled_out shifted added")
        (logits, peak_ready, centred, exped, mass_ready, rmass_ready, prob_ready, top_ready, placed, place_copied,
         pair_sum, pair_eps, rpair_ready, share_ready, parted, weighted, w_turned, w_copied, bias_ready, acc_ready,
         widened, gelu_done, narrowed, taken, scaled_out, shifted, added) = sems
        sems = ln.sems + ln2.sems + sems

        with nc.Block() as block:
            @block.sync
            def _(sp):
                sp.wait_ge(w["loaded"], w["total"])

        ROOTS, NORMS, TURN, LOGITS, CENTRE, EXP, SHARES, TURN_WEIGHTS, BIASES = 1, 1, 2, 3, 3, 4, 4, 6, 7

        def step(finish_of, work_of, make_of, parity):
            F, B, A = finish_of is not None, work_of is not None, make_of is not None
            xa = x[:, bass.ds(make_of * GT, GT), :] if A else None
            xf = x[:, bass.ds(finish_of * GT, GT), :] if F else None
            xnT, weight, acc = xnT_of[:, parity], weight_of[:, parity], acc_of[:, parity]
            xnT_new, weight_new, acc_other = xnT_of[:, 1 - parity], weight_of[:, 1 - parity], acc_of[:, 1 - parity]

            with nc.Block() as block:
                @block.tensor
                def _(pe):
                    def widen(e):
                        for c in range(CH):
                            n = e * CH + c
                            if n >= 3:
                                pe.wait_ge(gelu_done, n - 2)
                            pe.matmul(banks[:, WIDE_BANKS[n % 3], :], w["W1"][:, e, c * P:(c + 1) * P], xnT, start=True, stop=True)\
                                .then_inc(widened, 1)

                    def narrow(e):
                        pe.wait_ge(gelu_done, (e + 1) * CH)
                        if e >= 2:
                            pe.wait_ge(taken, GT * (e - 1))
                        for t in range(GT):
                            for c in range(CH):
                                last = pe.matmul(banks[:, 4 + e % 2, t * P:(t + 1) * P],
                                                 hT[:, e % 2, c, t * P:(t + 1) * P], w["W2"][:, e, c, :],
                                                 start=(c == 0), stop=(c == CH - 1))
                        last.then_inc(narrowed, 1)

                    def make(e):
                        if e == TURN:
                            ln.tensor(pe)
                        if e == LOGITS:
                            pe.wait_ge(ln.ready, 1)
                            for t in range(GT):
                                o = banks[:, 2, t * E:(t + 1) * E]
                                pe.matmul(o, xnT_new[:, t * P:(t + 1) * P], w["Wg"][:], start=True, stop=False)
                                last = pe.matmul(o, consts["ones"][0:1, 0:P], w["bg"][:], start=False, stop=True)
                            last.then_inc(logits, 1)
                        if e == TURN_WEIGHTS:
                            pe.wait_ge(weighted, 1)
                            for t in range(GT):
                                last = pe.transpose(banks[0:E, 2, t * P:(t + 1) * P], weight_new[:, t, :], consts["ident"])
                            last.then_inc(w_turned, 1)
                        if e == BIASES:
                            pe.wait_ge(w_copied, 1)
                            for t in range(GT):
                                last = pe.matmul(banks[:, 6, t * P:(t + 1) * P], weightT[:, t * P:(t + 1) * P],
                                                 w["b2"][:], start=True, stop=True)
                            last.then_inc(bias_ready, 1)

                    for e in range(E + 1):
                        if B and e < E:
                            widen(e)
                        if B and e:
                            narrow(e - 1)
                        if A:
                            make(e)

                @block.scalar
                def _(act):
                    for e in range(E):
                        for n in range(e * CH, (e + 1) * CH if B else e * CH):
                            act.wait_ge(widened, n + 1)
                            if e >= 2:
                                act.wait_ge(narrowed, e - 1)
                            act.activation(hT[:, e % 2, n % CH, :], banks[:, WIDE_BANKS[n % 3], :], ACT.Gelu, bias=w["b1"][:, n:n + 1])\
                                .then_inc(gelu_done, 1)
                        if e == ROOTS:
                            act.preload_act_table_set(EXP_LN)
                            if F:
                                ln2.root(act)
                            if A:
                                ln.root(act)
                        if A and e == TURN:
                            act.wait_ge(ln.turned, GT)
                            act.copy(xnT_new, banks[:, 7, :]).then_inc(ln.ready, 1)
                        if A and e == EXP:
                            act.wait_ge(centred, 1)
                            act.activation(z[:], z[:], ACT.Exp).then_inc(exped, 1)

                @block.vector
                def _(dve):
                    def take(e):
                        dve.wait_ge(narrowed, e + 1)
                        if e:
                            dve.wait_ge(taken, GT * e)
                        for t in range(GT):
                            dve.scalar_tensor_tensor(acc[:, t, :], banks[:, 4 + e % 2, t * P:(t + 1) * P],
                                                     weight[:, t, e:e + 1], acc[:, t, :], ALU.mult, ALU.add)\
                                .then_inc(taken, 1)

                    def finish():
                        ln2.normalize(dve, acc_other)
                        dve.wait_ge(ln2.normed, GT)
                        dve.tensor_tensor(sums[:], ln2.xn[:], w["gamma"][:].unsqueeze(1).broadcast_to([P, GT, D]), ALU.mult)\
                            .then_inc(scaled_out, 1)
                        dve.wait_ge(scaled_out, 1)
                        dve.tensor_tensor(sums[:], sums[:], w["beta"][:].unsqueeze(1).broadcast_to([P, GT, D]), ALU.add)\
                            .then_inc(shifted, 1)
                        dve.wait_ge(shifted, 1)
                        dve.tensor_tensor(xf, xf, sums[:], ALU.add).then_inc(added, 1)

                    def centre():
                        dve.wait_ge(logits, 1)
                        lo = banks[:, 2, 0:GT * E].rearrange("p (t e) -> p t e", e=E)
                        dve.tensor_reduce(peak[:], lo, AX_X, ALU.max).then_inc(peak_ready, 1)
                        dve.wait_ge(peak_ready, 1)
                        dve.tensor_tensor(z[:], lo, spread(peak[:], E), ALU.subtract).then_inc(centred, 1)

                    def shares():
                        dve.wait_ge(exped, 1)
                        dve.tensor_reduce(mass[:], z[:], AX_X, ALU.add).then_inc(mass_ready, 1)
                        dve.wait_ge(mass_ready, 1)
                        dve.reciprocal(rmass[:], mass[:]).then_inc(rmass_ready, 1)
                        dve.wait_ge(rmass_ready, 1)
                        dve.tensor_tensor(prob[:], z[:], spread(rmass[:], E), ALU.mult).then_inc(prob_ready, 1)
                        dve.wait_ge(prob_ready, 1)
                        for t in range(GT):
                            dve.max(top[:, t, :], prob[:, t, :]).then_inc(top_ready, 1)
                        dve.wait_ge(top_ready, GT)
                        for t in range(GT):
                            dve.max_index(place[:, t, :], top[:, t, :], prob[:, t, :]).then_inc(placed, 1)
                        dve.tensor_reduce(pair[:], top[:, :, 0:TOP], AX_X, ALU.add).then_inc(pair_sum, 1)
                        dve.wait_ge(placed, GT)
                        dve.tensor_copy(placef[:], place[:]).then_inc(place_copied, 1)
                        dve.wait_ge(pair_sum, 1)
                        dve.tensor_scalar(pair[:], pair[:], EPS, None, ALU.add).then_inc(pair_eps, 1)
                        dve.wait_ge(pair_eps, 1)
                        dve.reciprocal(rpair[:], pair[:]).then_inc(rpair_ready, 1)
                        dve.wait_ge(rpair_ready, 1)
                        dve.tensor_tensor(share[:], top[:, :, 0:TOP], spread(rpair[:], TOP), ALU.mult).then_inc(share_ready, 1)
                        dve.wait_ge(share_ready, 1)
                        dve.wait_ge(place_copied, 1)
                        for r in range(TOP):
                            for t in range(GT):
                                dve.tensor_scalar(part[:, r, t, :], consts["count"], placef[:, t, r:r + 1],
                                                  share[:, t, r:r + 1], ALU.is_equal, ALU.mult).then_inc(parted, 1)
                        dve.wait_ge(parted, TOP * GT)
                        dve.tensor_tensor(weight_new, part[:, 0, :, :], part[:, 1, :, :], ALU.add).then_inc(weighted, 1)

                    if F:
                        ln2.gather_moments(dve, acc_other)
                    if A:
                        ln.gather_moments(dve, xa)
                    for e in range(E):
                        if F and e == NORMS:
                            finish()
                        if A and e == NORMS:
                            ln.normalize(dve, xa)
                        if A and e == CENTRE:
                            centre()
                        if A and e == SHARES:
                            shares()
                        if A and e == TURN_WEIGHTS:
                            dve.wait_ge(w_turned, 1)
                            dve.tensor_copy(weightT[:], banks[0:E, 2, :]).then_inc(w_copied, 1)
                        if B:
                            take(e)
                    if A:
                        dve.wait_ge(bias_ready, 1)
                        dve.tensor_copy(acc_other, banks[:, 6, :].rearrange("p (t d) -> p t d", d=D)).then_inc(acc_ready, 1)
            restart(nc, sems)

        step(None, None, 0, 1)
        step(None, 0, 1, 0)
        with nc.Fori(0, (GROUPS - 2) // 2) as pair_of:
            g = 2 * pair_of
            step(g, g + 1, g + 2, 1)
            step(g + 1, g + 2, g + 3, 0)
        step(GROUPS - 2, GROUPS - 1, None, 1)
        step(GROUPS - 1, None, None, 0)


def gated_recurrence(nc, x, banks, consts, w):
    HEADS, HW, CHUNK, EPS = 2, 64, 64, 1e-5
    NC = GN // CHUNK
    SC = NC // GB
    with ExitStack() as ctx:
        sb = lambda n, s: ctx.enter_context(nc.sbuf_tensor("hgrn_" + n, s, F32))
        ln = LayerNorm(nc, ctx, consts, banks[:, 0, :], "hgrn_ln")
        ndelta = sb("ndelta", [P, 1])
        q_of, k_of, eG_of = (sb(n, [P, 2, GN]) for n in ("q", "k", "eG"))
        sgate_of, vals_of = sb("sgate", [CHUNK, 2, NC, D]), sb("vals", [CHUNK, 2, NC, D])
        z, mag, logf, G, enG = (sb(n, [P, GN]) for n in ("z", "mag", "logf", "G", "enG"))
        low, keys = sb("low", [HW, GN]), sb("keys", [CHUNK, NC, D])
        att = sb("att", [CHUNK, HEADS, NC, CHUNK])
        kv, S = sb("kv", [P, NC, D]), sb("S", [P, NC, D])
        o, osq, ms, lms, rms = sb("o", [CHUNK, NC, D]), sb("osq", [CHUNK, NC, D]), sb("ms", [CHUNK, NC * HEADS]), sb("lms", [CHUNK, NC * HEADS]), sb("rms", [CHUNK, NC * HEADS])
        oT = sb("oT", [P, GN])
        prep = signals(nc, ctx, "prep")[0]
        sems = signals(nc, ctx, "projected q_silu k_sigmoid z_biased low_copied v_ready v_copied gates gate_ready "
                                "mag_ready mag_exp mag_log logf_ready G_ready eG_ready enG_ready q_ready k_ready "
                                "keys_turned keys_copied att_ready att_masked kv_ready kv_scaled S_ready o_ready "
                                "o_gated o_squared ms_ready ms_eps ms_log rms_ready o_normed o_turned oT_ready "
                                "out_ready added")
        (projected, q_silu, k_sigmoid, z_biased, low_copied, v_ready, v_copied, gates, gate_ready, mag_ready, mag_exp,
         mag_log, logf_ready, G_ready, eG_ready, enG_ready, q_ready, k_ready, keys_turned, keys_copied, att_ready,
         att_masked, kv_ready, kv_scaled, S_ready, o_ready, o_gated, o_squared, ms_ready, ms_eps, ms_log, rms_ready,
         o_normed, o_turned, oT_ready, out_ready, added) = sems
        sems = ln.sems + [prep] + sems
        ch = lambda c: slice(c * CHUNK, (c + 1) * CHUNK)
        at = lambda first, c: banks[0:CHUNK, first + c // 4, (c % 4) * D:(c % 4 + 1) * D]
        both = lambda first: banks[0:CHUNK, first:first + 2, :].rearrange("p a (c d) -> p (a c) d", d=D)

        with nc.Block() as block:
            @block.sync
            def _(sp):
                sp.wait_ge(w["loaded"], w["total"])
        with nc.Block() as block:
            @block.vector
            def _(dve):
                dve.tensor_scalar(ndelta[:], w["delta"][:], -1.0, None, ALU.mult)

        def step(work_on, make_of, parity):
            ATT, KEYS, O, END = 3, 5, 3, 7
            B, A = work_on is not None, make_of is not None
            xb = x[:, bass.ds(work_on * GT, GT), :] if B else None
            xa = x[:, bass.ds(make_of * GT, GT), :] if A else None
            q, k, eG, sgate, vals = (a[:, parity] for a in (q_of, k_of, eG_of, sgate_of, vals_of))
            q_new, k_new, eG_new, sgate_new, vals_new = (a[:, 1 - parity] for a in (q_of, k_of, eG_of, sgate_of, vals_of))
            half = lambda a, n: a[:, n * NC // 2:(n + 1) * NC // 2, :]
            bank_of = lambda n: banks[0:CHUNK, 1 + n, :].rearrange("p (c d) -> p c d", d=D)

            with nc.Block() as block:
                @block.tensor
                def _(pe):
                    def attend():
                        for c in range(NC):
                            for h in range(HEADS):
                                r = slice(h * HW, (h + 1) * HW)
                                last = pe.matmul(banks[0:CHUNK, ATT + h, ch(c)], k[r, ch(c)], q[r, ch(c)], start=True, stop=True)
                        last.then_inc(att_ready, 1)

                    def turn_keys():
                        for c in range(NC):
                            last = pe.transpose(at(KEYS, c), k[:, ch(c)], consts["ident"])
                        last.then_inc(keys_turned, 1)

                    def project():
                        pe.wait_ge(ln.ready, 1)
                        for bank, name in ((1, "Wk"), (2, "G1"), (0, "Wq")):
                            m = w[name].shape[1]
                            pe.matmul(banks[0:m, bank, :], w[name][:], ln.xnT[:], start=True, stop=True).then_inc(projected, 1)

                    def outer():
                        pe.wait_ge(keys_copied, 1)
                        for c in range(NC):
                            last = pe.matmul(banks[:, KEYS + c // 4, (c % 4) * D:(c % 4 + 1) * D], keys[:, c, :], vals[:, c, :],
                                             start=True, stop=True)
                        last.then_inc(kv_ready, 1)

                    def project_values():
                        for n, free in enumerate((z_biased, low_copied)):
                            pe.wait_ge(free, 1)
                            for c in range(4 * n, 4 * n + 4):
                                last = pe.matmul(at(1, c), ln.xnT[:, ch(c)], w["Wv"][:], start=True, stop=True)
                            last.then_inc(v_ready, 1)

                    def project_gates():
                        for n in range(2):
                            pe.wait_ge(v_copied, n + 1)
                            for c in range(4 * n, 4 * n + 4):
                                last = pe.matmul(at(1, c), low[:, ch(c)], w["G2"][:], start=True, stop=True)
                            last.then_inc(gates, 1)

                    def outputs():
                        pe.wait_ge(att_masked, HEADS)
                        for i in range(SC):
                            if i:
                                pe.wait_ge(S_ready, GB * i)
                            for b in range(GB):
                                c = b * SC + i
                                if i:
                                    pe.matmul(at(O, c), q[:, ch(c)], S[:, c, :], start=True, stop=False)
                                for h in range(HEADS):
                                    last = pe.matmul(at(O, c)[:, h * HW:(h + 1) * HW], att[:, h, c, :],
                                                     vals[:, c, h * HW:(h + 1) * HW], start=(i == 0), stop=(i == 0 or h == HEADS - 1))
                        last.then_inc(o_ready, 1)

                    def way_out():
                        pe.wait_ge(o_normed, 1)
                        for c in range(NC):
                            last = pe.transpose(banks[:, END, ch(c)], o[:, c, :], consts["ident"][0:CHUNK, 0:CHUNK])
                        last.then_inc(o_turned, 1)
                        pe.wait_ge(oT_ready, 1)
                        for t in range(GT):
                            last = pe.matmul(banks[:, END, t * P:(t + 1) * P], oT[:, t * P:(t + 1) * P], w["Wo"][:],
                                             start=True, stop=True)
                        last.then_inc(out_ready, 1)

                    if B:
                        attend()
                        turn_keys()
                    if A:
                        ln.tensor(pe)
                    if B:
                        outer()
                    if A:
                        project()
                        project_values()
                        project_gates()
                    if B:
                        outputs()
                        way_out()

                @block.scalar
                def _(act):
                    act.preload_act_table_set(EXP_LN)
                    if A:
                        ln.root(act)
                    if B:
                        act.wait_ge(keys_turned, 1)
                        act.copy(keys[:], both(KEYS)).then_inc(keys_copied, 1)
                    if A:
                        ln.copy(act)
                        act.wait_ge(z_biased, 1)
                        act.activation(mag[:], z[:], ACT.Abs).then_inc(mag_ready, 1)
                        act.wait_ge(mag_ready, 1)
                        act.activation(mag[:], mag[:], ACT.Exp, scale=-1.0).then_inc(mag_exp, 1)
                        act.wait_ge(mag_exp, 1)
                        act.activation(mag[:], mag[:], ACT.Ln, bias=1.0).then_inc(mag_log, 1)
                        act.wait_ge(G_ready, 1)
                        act.activation(eG_new, G[:], ACT.Exp).then_inc(eG_ready, 1)
                        act.activation(enG[:], G[:], ACT.Exp, scale=-1.0).then_inc(enG_ready, 1)
                        act.activation(k_new, z[:], ACT.Sigmoid, scale=-1.0).then_inc(k_sigmoid, 1)
                        for n in range(2):
                            act.wait_ge(gates, n + 1)
                            act.activation(half(sgate_new, n), bank_of(n), ACT.Sigmoid).then_inc(gate_ready, 1)
                        act.wait_ge(projected, 3)
                        act.activation(q_new, banks[:, 0, :], ACT.Silu).then_inc(q_silu, 1)
                        act.preload_act_table_set(EXP_LN)
                    if B:
                        act.wait_ge(o_gated, 1)
                        act.activation(osq[:], o[:], ACT.Square).then_inc(o_squared, 1)
                        act.wait_ge(ms_eps, 1)
                        act.activation(lms[:], ms[:], ACT.Ln).then_inc(ms_log, 1)
                        act.wait_ge(ms_log, 1)
                        act.activation(rms[:], lms[:], ACT.Exp, scale=-0.5).then_inc(rms_ready, 1)
                        act.wait_ge(o_turned, 1)
                        act.activation(oT[:], banks[:, END, :], ACT.Copy, scale=w["norm_w"][:]).then_inc(oT_ready, 1)

                @block.vector
                def _(dve):
                    def mask():
                        dve.wait_ge(att_ready, 1)
                        for h in range(HEADS):
                            dve.tensor_tensor(att[:, h, :, :], banks[0:CHUNK, ATT + h, :].rearrange("p (c t) -> p c t", t=CHUNK),
                                              consts["causal"][0:CHUNK, 0:CHUNK].unsqueeze(1).broadcast_to([CHUNK, NC, CHUNK]),
                                              ALU.mult).then_inc(att_masked, 1)

                    def take_projections():
                        dve.wait_ge(projected, 1)
                        dve.tensor_scalar(z[:], banks[:, 1, :], w["delta"][:], None, ALU.add).then_inc(z_biased, 1)
                        dve.wait_ge(projected, 2)
                        dve.tensor_copy(low[:], banks[0:HW, 2, :]).then_inc(low_copied, 1)
                        for n in range(2):
                            dve.wait_ge(v_ready, n + 1)
                            dve.tensor_copy(half(vals_new, n), bank_of(n)).then_inc(v_copied, 1)

                    def decays():
                        dve.wait_ge(mag_log, 1)
                        dve.scalar_tensor_tensor(logf[:], z[:], 0.0, mag[:], ALU.min, ALU.subtract).then_inc(logf_ready, 1)
                        dve.wait_ge(logf_ready, 1)
                        dve.tensor_tensor_scan(G[:], consts["inside"], logf[:], 0.0, ALU.mult, ALU.add).then_inc(G_ready, 1)

                    def states():
                        dve.wait_ge(kv_ready, 1)
                        end = lambda c: eG[:, (c + 1) * CHUNK - 1:(c + 1) * CHUNK]
                        into = lambda c: (S[:, c + 1, :] if c % SC == 0 else kv[:, c, :])
                        for b in range(GB):
                            for i in range(SC - 1):
                                c = b * SC + i
                                dve.scalar_tensor_tensor(into(c), banks[:, KEYS + c // 4, (c % 4) * D:(c % 4 + 1) * D], end(c),
                                                         consts["blocks"], ALU.mult, ALU.mult).then_inc(kv_scaled, 1)
                        dve.wait_ge(kv_scaled, GB * (SC - 1))
                        dve.engine_nop().then_inc(S_ready, GB)
                        for i in range(1, SC - 1):
                            if i > 1:
                                dve.wait_ge(S_ready, GB * i)
                            for b in range(GB):
                                c = b * SC + i
                                dve.scalar_tensor_tensor(S[:, c + 1, :], S[:, c, :], end(c), kv[:, c, :], ALU.mult, ALU.add)\
                                    .then_inc(S_ready, 1)

                    def decayed():
                        dve.wait_ge(enG_ready, 1)
                        dve.wait_ge(k_sigmoid, 1)
                        dve.tensor_tensor(k_new, k_new, enG[:], ALU.mult).then_inc(k_ready, 1)
                        dve.wait_ge(eG_ready, 1)
                        dve.wait_ge(q_silu, 1)
                        dve.tensor_tensor(q_new, q_new, eG_new, ALU.mult).then_inc(q_ready, 1)

                    def norm():
                        dve.wait_ge(o_ready, 1)
                        dve.tensor_tensor(o[:], both(O), sgate, ALU.mult).then_inc(o_gated, 1)
                        dve.wait_ge(o_squared, 1)
                        dve.tensor_reduce(ms[:], osq[:].rearrange("p c (h d) -> p (c h) d", d=HW), AX_X, ALU.add).then_inc(ms_ready, 1)
                        dve.wait_ge(ms_ready, 1)
                        dve.tensor_scalar(ms[:], ms[:], 1.0 / HW, EPS, ALU.mult, ALU.add).then_inc(ms_eps, 1)
                        dve.wait_ge(rms_ready, 1)
                        oh = o[:].rearrange("p c (h d) -> p (c h) d", d=HW)
                        dve.tensor_tensor(oh, oh, spread(rms[:], HW), ALU.mult).then_inc(o_normed, 1)

                    if A:
                        ln.vector(dve, xa)
                    if B:
                        mask()
                    if A:
                        take_projections()
                    if B:
                        states()
                    if A:
                        decays()
                    if B:
                        norm()
                    if A:
                        decayed()
                    if B:
                        dve.wait_ge(out_ready, 1)
                        dve.tensor_tensor(xb, xb, banks[:, END, :].rearrange("p (t d) -> p t d", d=D), ALU.add)\
                            .then_inc(added, 1)
            restart(nc, sems)

        pipeline(nc, step)


def shift_tokens(pe, bank, consts, y, shifted):
    half = bank[:, 0:GT * D // 2].rearrange("p (t d) -> p t d", d=D // 2)
    pe.matmul(half, consts["next"], y[:, :, D // 2:], start=True, stop=False)
    last = pe.matmul(half[:, 1::ST, :], consts["carry"], y[:, 0::ST, D // 2:], start=False, stop=True)
    last.then_inc(shifted, 1)


ATTENTION_SIGNALS = ("shifted low_half high_half in_turned in_ready projected copied squared reduced swap_done cosined "
                     "rotated clamped logged inverted unit qk_turned qk_copied scored banded exped summed rden_ready "
                     "head_done v_copied o_turned o_copied out_ready added tabled peaked")
MLP_SIGNALS = ("mlp_shifted mlp_low_half mlp_high_half stats_done moments_done var_done log_done rstd_done normed "
               "ln_turned ln_ready gated gate_taken gelu_done widened hidden biased mlp_out_ready joined")


def local_step(nc, y, banks, consts, w, loaded, tables, tmp, sems, heads_of, make_of, mlp_of, parity,
               new_tables=False, new_peak=False):
    HALF, SCALE, UP, QS = INNER // 2, 8.0, 2.0 ** 32, 8.0
    BAND = P + WINDOW
    SCORES = BAND + P
    QK = 4 * GT
    UNITS = QK + 2 * GT
    CH = len(MLP_CHUNKS)
    S_BANK, T_BANK, V_BANK, O_BANK, A_BANK, X_BANK = 0, 2, 3, 4, 5, 7
    attention, mlp = sems
    (shifted, low_half, high_half, in_turned, in_ready, projected, copied, squared, reduced, swap_done, cosined, rotated,
     clamped, logged, inverted, unit, qk_turned, qk_copied, scored, banded, exped, summed, rden_ready, head_done,
     v_copied, o_turned, o_copied, out_ready, added, tabled, peaked) = attention
    (mlp_shifted, mlp_low_half, mlp_high_half, stats_done, moments_done, var_done, log_done, rstd_done, normed,
     ln_turned, ln_ready, gated, gate_taken, gelu_done, widened, hidden, biased, mlp_out_ready, joined) = mlp
    ys, yT_in, raw, sq, swapped = tmp["ys"], tmp["ysT"], tmp["raw"], tmp["sq"], tmp["swapped"]
    ss, lg, inv, turned_qk = tmp["ss"], tmp["lg"], tmp["inv"], tmp["turned_qk"]
    logit, probs, rden, o = tmp["logit"], tmp["probs"], tmp["rden"], tmp["o"]
    rot, v1 = tmp["rot"][:, parity], tmp["v1"][:, parity]
    rot_new, v1_new = tmp["rot"][:, 1 - parity], tmp["v1"][:, 1 - parity]
    ms, xn, xnT = tmp["mlp_ys"], tmp["mlp_xn"], tmp["mlp_xnT"]
    gate = hT = tmp["gate"]
    stats, moments, var, log, rstd = (tmp["mlp_" + n] for n in ("stats", "moments", "var", "log", "rstd"))
    oT = lambda j: rot[:, 0, :, j * P:(j + 1) * P]
    heads = lambda a: a.rearrange("p (h d) -> p h d", d=HD)
    tiled = lambda a: a.rearrange("p (t d) -> p t d", d=D)
    group = lambda g: None if g is None else y[:, bass.ds(g * GT, GT), :]
    yb, ya, ym = group(heads_of), group(make_of), group(mlp_of)
    A, B, M = make_of is not None, heads_of is not None, mlp_of is not None

    is_qk = lambda n: n % 6 < 4
    qk_number = lambda n: n // 6 * 4 + n % 6
    v_number = lambda n: n // 6 * 2 + n % 6 - 4
    where = lambda k: (k // 4, k // 2 % 2, k % 2)
    part = lambda k: heads(rot_new[:, where(k)[1], where(k)[0], where(k)[2] * HALF:(where(k)[2] + 1) * HALF])

    schedule = Schedule({"make_shift": (A, 0, 1), "make_turn": (A, 1, 1), "project": (A * UNITS, 2, 1), "take": (A * UNITS, 3, 1),
                "cosine": (A * UNITS, 4, 1), "rotate": (A * UNITS, 5, 1), "clamp": (A * GT, 8, 6), "invert": (A * GT, 9, 6),
                "unit_q": (A * GT, 10, 6), "unit_k": (A * GT, 11, 6),
                "turn": (B * H, 0, 1), "turned": (B * H, 1, 1), "score": (B * H, 3, 1), "mask": (B * H, 4, 1),
                "exp": (B * H, 6, 1), "values": (B * H, 7, 1), "normalize": (B * H, 8, 1), "turn_o": (B * PAIRS, 10, 2),
                "copy_o": (B * PAIRS, 11, 2),
                "mlp_shift": (M, 2, 1), "high_half": (M, 3, 1), "stats": (M, 4, 1), "moments": (M, 5, 1), "var": (M, 6, 1),
                "rstd": (M, 7, 1), "normalize_mlp": (M, 8, 1), "turn_mlp": (M, 9, 1), "turned_mlp": (M, 10, 1),
                "gate": (M * CH, 12, 2), "gate_take": (M * CH, 13, 2), "gelu": (M, 17, 1), "widen": (M * CH, 18, 2),
                "hide": (M * CH, 19, 2), "back": (M, 24, 1), "join": (M, 25, 1)})
    STEPS, run = schedule.steps, schedule.run

    with nc.Block() as block:
        @block.tensor
        def _(pe):
            def turn_in(_):
                pe.wait_ge(low_half, 1)
                pe.wait_ge(high_half, 1)
                for t in range(GT):
                    last = pe.transpose(banks[:, X_BANK, t * P:(t + 1) * P], ys[:, t, :], consts["ident"])
                last.then_inc(in_turned, 1)

            def project(n):
                if n == 0:
                    pe.wait_ge(in_ready, 1)
                    pe.wait_ge(*loaded["attention"])
                if n >= 2:
                    if is_qk(n - 2):
                        pe.wait_ge(copied, qk_number(n - 2) + 1)
                    else:
                        pe.wait_ge(v_copied, v_number(n - 2) + 1)
                t, c = n // 6, n % 6 * HALF
                pe.matmul(banks[:, A_BANK + n % 2, :], yT_in[:, t * P:(t + 1) * P], w["Wqkv"][:, c:c + HALF],
                          start=True, stop=True).then_inc(projected, 1)

            def turn_qk(k):
                if k:
                    pe.wait_ge(qk_copied, k)
                j, m = k // 2, k % 2
                for t in range(GT):
                    last = pe.transpose(banks[:, T_BANK, t * P:(t + 1) * P], rot[:, m, t, j * P:(j + 1) * P], consts["ident"])
                last.then_inc(qk_turned, 1)

            def score(k):
                j, b = k // 2, k % 2
                pe.wait_ge(qk_copied, 2 * j + 2)
                for r in range(2):
                    if k:
                        pe.wait_ge(banded, 2 * (k - 1) + r + 1)
                    q, kk = (turned_qk[r * HD:(r + 1) * HD, j % 2, m, :] for m in range(2))
                    c = b * SEQ
                    pe.matmul(banks[:, S_BANK + r, 0:BAND], kk[:, c:c + P], q[:, c:c + BAND], start=True, stop=True)
                    pe.matmul(banks[:, S_BANK + r, BAND:SCORES], kk[:, c + P:c + SEQ], q[:, c + P:c + SEQ],
                              start=True, stop=True).then_inc(scored, 1)

            def values(h):
                pe.wait_ge(exped, 2 * (h + 1))
                if h:
                    pe.wait_ge(head_done, h)
                for b in range(GB):
                    for i in range(ST):
                        out = banks[:, V_BANK, (b * ST + i) * (HD + 1):(b * ST + i + 1) * (HD + 1)]
                        for j in range(i + 1):
                            c = (i * P if j == 0 else SEQ)
                            last = pe.matmul(out, probs[:, h % 2, b, c:c + P], v1[:, b * ST + j, h, :],
                                             start=(j == 0), stop=(j == i))
                last.then_inc(summed, 1)

            def turn_o(j):
                pe.wait_ge(head_done, 2 * j + 2)
                if j:
                    pe.wait_ge(o_copied, j)
                for t in range(GT):
                    last = pe.transpose(banks[:, O_BANK, t * P:(t + 1) * P], o[:, j % 2, t, :], consts["ident"])
                last.then_inc(o_turned, 1)

            def shift_mlp(_):
                if A:
                    pe.wait_ge(in_ready, 1)
                shift_tokens(pe, banks[:, X_BANK], consts, ym, mlp_shifted)

            def turn_mlp(_):
                pe.wait_ge(normed, GT)
                for t in range(GT):
                    last = pe.transpose(banks[:, X_BANK, t * P:(t + 1) * P], xn[:, t, :], consts["ident"])
                last.then_inc(ln_turned, 1)

            def wide(c, column, signal):
                lo, m = MLP_CHUNKS[c]
                pe.matmul(banks[0:m, X_BANK, :], w["W1"][:, column + lo:column + lo + m], xnT[:], start=True, stop=True)\
                    .then_inc(signal, 1)

            def make_gate(c):
                if c == 0:
                    pe.wait_ge(ln_ready, 1)
                    pe.wait_ge(*loaded["mlp"])
                else:
                    pe.wait_ge(gate_taken, c)
                wide(c, MLP, gated)

            def widen(c):
                if c == 0:
                    pe.wait_ge(gate_taken, CH)
                else:
                    pe.wait_ge(hidden, c)
                wide(c, 0, widened)

            def back(_):
                pe.wait_ge(hidden, CH)
                for t in range(GT):
                    for c, (lo, m) in enumerate(MLP_CHUNKS):
                        last = pe.matmul(banks[:, X_BANK, t * P:(t + 1) * P], hT[0:m, c, t * P:(t + 1) * P],
                                         w["W2"][0:m, c, :], start=(c == 0), stop=(c == CH - 1))
                last.then_inc(mlp_out_ready, 1)

            for i in range(STEPS):
                run("make_shift", i, lambda _: shift_tokens(pe, banks[:, X_BANK], consts, ya, shifted))
                run("make_turn", i, turn_in)
                run("mlp_shift", i, shift_mlp)
                run("turn_mlp", i, turn_mlp)
                run("project", i, project)
                run("gate", i, make_gate)
                run("widen", i, widen)
                run("back", i, back)
                run("turn_o", i, turn_o)
                run("score", i, score)
                run("values", i, values)
                run("turn", i, turn_qk)
            if B:
                pe.wait_ge(o_copied, PAIRS)
                pe.wait_ge(*loaded["Wo"])
                if M:
                    pe.wait_ge(joined, 1)
                elif A:
                    pe.wait_ge(in_ready, 1)
                for t in range(GT):
                    for j in range(PAIRS):
                        last = pe.matmul(banks[:, X_BANK, t * P:(t + 1) * P], oT(j)[:, t, :],
                                         w["Wo"][:, j, :], start=(j == 0), stop=(j == PAIRS - 1))
                last.then_inc(out_ready, 1)

        @block.scalar
        def _(act):
            def copy_in(_):
                act.wait_ge(in_turned, 1)
                act.copy(yT_in[:], banks[:, X_BANK, :]).then_inc(in_ready, 1)

            def take(n):
                act.wait_ge(projected, n + 1)
                if not is_qk(n):
                    v = v_number(n)
                    act.copy(v1_new[:, v // 2, (v % 2) * PAIRS:(v % 2 + 1) * PAIRS, 0:HD],
                             heads(banks[:, A_BANK + n % 2, :])).then_inc(v_copied, 1)
                    return
                k = qk_number(n)
                if k >= 4:
                    act.wait_ge(cosined, k - 3)
                    act.wait_ge(swap_done, 2 * (k - 3))
                    act.wait_ge(squared, k - 3)
                act.copy(raw[:, k % 4, :], banks[:, A_BANK + n % 2, :]).then_inc(copied, 1)
                act.wait_ge(copied, k + 1)
                if k >= 3:
                    act.wait_ge(reduced, k - 2)
                act.activation(sq[:, k % 3, :], raw[:, k % 4, :], ACT.Square).then_inc(squared, 1)

            def invert(t):
                act.wait_ge(clamped, t + 1)
                act.activation(lg[:, :, t, :], ss[:, :, t, :], ACT.Ln).then_inc(logged, 1)
                act.wait_ge(logged, t + 1)
                act.activation(inv[:, :, t, :], lg[:, :, t, :], ACT.Exp, bias=tables["up"][:], scale=-0.5).then_inc(inverted, 1)

            def copy_qk(k):
                act.wait_ge(qk_turned, k + 1)
                if k >= 4:
                    act.wait_ge(scored, 4 * (k // 2 - 1))
                act.copy(turned_qk[:, k // 2 % 2, k % 2, :], banks[:, T_BANK, :]).then_inc(qk_copied, 1)

            def exp(h):
                if h == 0 and new_peak:
                    act.wait_ge(peaked, 1)
                act.wait_ge(banded, 4 * (h // 2) + 4)
                if h >= 2:
                    act.wait_ge(summed, h - 1)
                for lo, hi, into in ((0, BAND, 0), (BAND, SCORES, SEQ)):
                    act.activation(probs[:, h % 2, :, into:into + hi - lo], logit[:, h // 2 % 2, h % 2, :, lo:hi],
                                   ACT.Exp, bias=tables["npeak"][:], scale=SCALE).then_inc(exped, 1)

            def copy_o(j):
                act.wait_ge(o_turned, j + 1)
                act.copy(oT(j), tiled(banks[:, O_BANK, :])).then_inc(o_copied, 1)

            def rstd_mlp(_):
                act.wait_ge(var_done, 1)
                act.activation(log[:], var[:], ACT.Ln).then_inc(log_done, 1)
                act.wait_ge(log_done, 1)
                act.activation(rstd[:], log[:], ACT.Exp, scale=-0.5).then_inc(rstd_done, 1)

            def copy_normed(_):
                act.wait_ge(ln_turned, 1)
                act.wait_ge(*loaded["mlp"])
                act.activation(xnT[:], banks[:, X_BANK, :], ACT.Identity, bias=w["ln_b"][:], scale=w["ln_g"][:])\
                    .then_inc(ln_ready, 1)

            def take_gate(c):
                m = MLP_CHUNKS[c][1]
                act.wait_ge(gated, c + 1)
                act.activation(gate[0:m, c, :], banks[0:m, X_BANK, :], ACT.Identity, bias=w["b1"][0:m, CH + c:CH + c + 1])\
                    .then_inc(gate_taken, 1)

            def gelu(_):
                full = sum(m == P for _, m in MLP_CHUNKS)
                rest = MLP_CHUNKS[-1][1]
                act.wait_ge(gate_taken, CH)
                act.activation(gate[:, 0:full, :], gate[:, 0:full, :], ACT.Gelu).then_inc(gelu_done, 1)
                act.activation(gate[0:rest, full, :], gate[0:rest, full, :], ACT.Gelu).then_inc(gelu_done, 1)
                act.preload_act_table_set(EXP_LN)

            if A:
                act.copy(ys[:, :, 0:D // 2], ya[:, :, 0:D // 2]).then_inc(low_half, 1)
            if M:
                act.copy(ms[:, :, 0:D // 2], ym[:, :, 0:D // 2]).then_inc(mlp_low_half, 1)
            for i in range(STEPS):
                run("make_turn", i, copy_in)
                run("turned", i, copy_qk)
                run("exp", i, exp)
                run("take", i, take)
                run("invert", i, invert)
                run("copy_o", i, copy_o)
                run("rstd", i, rstd_mlp)
                run("turned_mlp", i, copy_normed)
                run("gate_take", i, take_gate)
                run("gelu", i, gelu)

        def pool_bias(pool):
            pool.wait_ge(mlp_shifted, 1)
            pool.wait_ge(mlp_low_half, 1)
            pool.wait_ge(*loaded["mlp"])
            pool.tensor_tensor(ym, ym, w["b2"][:].unsqueeze(1).broadcast_to([P, GT, D]), ALU.add).then_inc(biased, 1)

        @block.gpsimd
        def _(pool):
            if A and new_tables:
                pool.wait_ge(tabled, 3)
            for k in range(QK if A else 0):
                t, m, half = where(k)
                pool.wait_ge(copied, k + 1)
                if k >= 3:
                    pool.wait_ge(rotated, k - 2)
                for r in range(2):
                    lo, other = slice(32 * r, 32 * r + 32), slice(32 - 32 * r, 64 - 32 * r)
                    pool.tensor_tensor(heads(swapped[:, k % 3, :])[:, :, lo], heads(raw[:, k % 4, :])[:, :, other],
                                       tables["all"][:, 2 * m + 1, t % ST, lo].unsqueeze(1)
                                       .broadcast_to([P, PAIRS, 32]), ALU.mult).then_inc(swap_done, 1)
                if M and k == 1:
                    pool_bias(pool)
            if M and not A:
                pool_bias(pool)

        @block.vector
        def _(dve):
            def cosine(n):
                if not is_qk(n):
                    return
                k = qk_number(n)
                t, m, half = where(k)
                dve.wait_ge(copied, k + 1)
                dve.tensor_tensor(part(k), heads(raw[:, k % 4, :]), tables["all"][:, 2 * m, t % ST, :].unsqueeze(1)
                                  .broadcast_to([P, PAIRS, HD]), ALU.mult).then_inc(cosined, 1)

            def rotate(n):
                if not is_qk(n):
                    return
                k = qk_number(n)
                t, m, half = where(k)
                dve.wait_ge(squared, k + 1)
                dve.tensor_reduce(ss[:, m, t, half * PAIRS:(half + 1) * PAIRS], heads(sq[:, k % 3, :]), AX_X, ALU.add)\
                    .then_inc(reduced, 1)
                dve.wait_ge(cosined, k + 1)
                dve.wait_ge(swap_done, 2 * k + 2)
                dve.tensor_tensor(part(k), part(k), heads(swapped[:, k % 3, :]), ALU.add).then_inc(rotated, 1)

            def clamp(t):
                dve.wait_ge(reduced, 4 * t + 4)
                dve.tensor_scalar(ss[:, :, t, :], ss[:, :, t, :], 1e-24, UP, ALU.max, ALU.mult).then_inc(clamped, 1)

            def make_unit(t, m):
                dve.wait_ge(inverted, t + 1)
                dve.wait_ge(rotated, 4 * t + 4)
                a = heads(rot_new[:, m, t, :])
                dve.tensor_tensor(a, a, spread(inv[:, m, t, :], HD), ALU.mult).then_inc(unit, 1)

            def mask(k):
                j, b = k // 2, k % 2
                if j >= 2:
                    dve.wait_ge(exped, 4 * (j - 1))
                for r in range(2):
                    dve.wait_ge(scored, 2 * k + r + 1)
                    dve.tensor_tensor(logit[:, j % 2, r, b, :], banks[:, S_BANK + r, 0:SCORES], consts["band"], ALU.add)\
                        .then_inc(banded, 1)

            def normalize(h):
                dve.wait_ge(summed, h + 1)
                out = banks[:, V_BANK, 0:GT * (HD + 1)].rearrange("p (t e) -> p t e", e=HD + 1)
                dve.reciprocal(rden[:, h % 2, :], out[:, :, HD]).then_inc(rden_ready, 1)
                dve.wait_ge(rden_ready, h + 1)
                if h >= 4:
                    dve.wait_ge(o_turned, h // 2 - 1)
                dve.tensor_tensor(o[:, h // 2 % 2, :, h % 2 * HD:(h % 2 + 1) * HD], out[:, :, 0:HD],
                                  spread(rden[:, h % 2, :], HD), ALU.mult).then_inc(head_done, 1)

            def copy_high(_):
                dve.wait_ge(mlp_shifted, 1)
                dve.tensor_copy(ms[:, :, D // 2:], tiled_half(banks[:, X_BANK])).then_inc(mlp_high_half, 1)

            def take_stats(_):
                dve.wait_ge(mlp_low_half, 1)
                dve.wait_ge(mlp_high_half, 1)
                for t in range(GT):
                    dve.bn_stats(stats[:, t, :], ms[:, t, :]).then_inc(stats_done, 1)

            def take_moments(_):
                dve.wait_ge(stats_done, GT)
                for t in range(GT):
                    dve.bn_aggr(moments[:, t, :], stats[:, t, :]).then_inc(moments_done, 1)

            def take_var(_):
                dve.wait_ge(moments_done, GT)
                dve.tensor_scalar(var[:], moments[:, :, 1], LN_EPS, None, ALU.add).then_inc(var_done, 1)

            def normalize_mlp(_):
                dve.wait_ge(rstd_done, 1)
                for t in range(GT):
                    dve.tensor_scalar(xn[:, t, :], ms[:, t, :], moments[:, t, 0:1], rstd[:, t:t + 1], ALU.subtract, ALU.mult)\
                        .then_inc(normed, 1)

            def hide(c):
                m = MLP_CHUNKS[c][1]
                if c == 0:
                    dve.wait_ge(gelu_done, 2)
                dve.wait_ge(widened, c + 1)
                dve.scalar_tensor_tensor(hT[0:m, c, :], banks[0:m, X_BANK, :], w["b1"][0:m, c:c + 1],
                                         gate[0:m, c, :], ALU.add, ALU.mult).then_inc(hidden, 1)

            def join(_):
                dve.wait_ge(mlp_out_ready, 1)
                dve.wait_ge(biased, 1)
                dve.tensor_tensor(ym, ym, tiled(banks[:, X_BANK, :]), ALU.add).then_inc(joined, 1)

            tiled_half = lambda bank: bank[:, 0:GT * D // 2].rearrange("p (t d) -> p t d", d=D // 2)
            scales, most = tables["scales"], tables["most"]
            if new_peak:
                dve.tensor_scalar(tables["npeak"][:], most[:, 0:1], most[:, 1:2], -QS, ALU.mult, ALU.mult).then_inc(peaked, 1)
            if new_tables:
                dve.wait_ge(*loaded["scales"])
                dve.tensor_tensor(tables["all"][:], tables["shapes"][:], scales[:].unsqueeze(2).broadcast_to([P, 4, ST, HD]),
                                  ALU.mult).then_inc(tabled, 1)
                for n in range(2):
                    dve.tensor_reduce(most[:, n:n + 1], scales[:, 2 * n, :], AX_X, ALU.max, apply_absolute_value=True)\
                        .then_inc(tabled, 1)
                dve.wait_ge(tabled, 3)
            if A:
                dve.wait_ge(shifted, 1)
                dve.tensor_copy(ys[:, :, D // 2:], tiled_half(banks[:, X_BANK])).then_inc(high_half, 1)
            for i in range(STEPS):
                run("mask", i, mask)
                run("normalize", i, normalize)
                run("high_half", i, copy_high)
                run("stats", i, take_stats)
                run("moments", i, take_moments)
                run("var", i, take_var)
                run("normalize_mlp", i, normalize_mlp)
                run("hide", i, hide)
                run("join", i, join)
                run("cosine", i, cosine)
                run("rotate", i, rotate)
                run("clamp", i, clamp)
                run("unit_q", i, lambda t: make_unit(t, 0))
                run("unit_k", i, lambda t: make_unit(t, 1))
            if B:
                dve.wait_ge(out_ready, 1)
                dve.tensor_tensor(yb, yb, tiled(banks[:, X_BANK, :]), ALU.add).then_inc(added, 1)
    restart(nc, attention + mlp)


def local_layers(nc, x, banks, consts, t, out):
    f = "L3_ffn_"
    y = x
    with ExitStack() as ctx:
        sb = lambda n, s: ctx.enter_context(nc.sbuf_tensor("local_" + n, s, F32))
        residual = out.rearrange("b (t p) d -> p (b t) d", p=P)
        lw = {"Wqkv": sb("Wqkv", [P, 3 * INNER]), "Wo": sb("Wo", [P, PAIRS, D]), "W1": sb("W1", [P, 2 * MLP]),
              "W2": sb("W2", [P, len(MLP_CHUNKS), D]), "b1": sb("b1", [P, 2 * len(MLP_CHUNKS)]), "b2": sb("b2", [P, D]),
              "ln_g": sb("ln_g", [P, 1]), "ln_b": sb("ln_b", [P, 1])}
        tables = {"scales": sb("qk_scales", [P, 4, HD]),
                  "shapes": sb("rotary", [P, 4, ST, HD]), "all": sb("rotary_scaled", [P, 4, ST, HD]),
                  "most": sb("most", [P, 2]), "npeak": sb("npeak", [P, 1]), "up": sb("up", [P, 1])}
        scales = tables["scales"]
        tmp = {n: sb(n, s) for n, s in (
            ("ys", [P, GT, D]), ("ysT", [P, GN]), ("raw", [P, 4, INNER // 2]), ("sq", [P, 3, INNER // 2]),
            ("swapped", [P, 3, INNER // 2]), ("ss", [P, 2, GT, H]), ("lg", [P, 2, GT, H]), ("inv", [P, 2, GT, H]),
            ("rot", [P, 2, 2, GT, INNER]), ("turned_qk", [P, 2, 2, GN]), ("logit", [P, 2, 2, GB, 2 * P + WINDOW]),
            ("probs", [P, 2, GB, CAUSAL]), ("v1", [P, 2, GT, H, HD + 1]), ("rden", [P, 2, GT]), ("o", [P, 2, GT, D]),
            ("mlp_ys", [P, GT, D]), ("mlp_stats", [P, GT, 6]), ("mlp_moments", [P, GT, 2]), ("mlp_var", [P, GT]),
            ("mlp_log", [P, GT]), ("mlp_rstd", [P, GT]), ("mlp_xn", [P, GT, D]), ("mlp_xnT", [P, GN]),
            ("gate", [P, len(MLP_CHUNKS), GN]))}
        filled, rotary_loaded, kept, returned = signals(nc, ctx, "filled rotary_loaded kept returned")
        attention_loaded, scales_loaded, wo_loaded, mlp_loaded = signals(nc, ctx, "attention_loaded scales_loaded wo_loaded mlp_loaded")

        with ExitStack() as inner:
            room = tmp["rot"].rearrange("p a b t n -> p (a b t n)")
            ln = LayerNorm(nc, inner, consts, banks[:, 7, :], "local_ln",
                           (room[:, 0:GN].rearrange("p (t d) -> p t d", d=D), room[:, GN:2 * GN]))
            with nc.Block() as block:
                @block.sync
                def _(sp):
                    sp.dma_start(residual, x[:]).then_inc(kept, 16)
                    sp.dma_start(tables["shapes"][:], t["rotary"]).then_inc(rotary_loaded, 16)
                    sp.wait_ge(rotary_loaded, 16)
                    sp.wait_ge(kept, 16)

                @block.scalar
                def _(act):
                    act.preload_act_table_set(EXP_LN)

                @block.vector
                def _(dve):
                    dve.memset(tables["up"][:], 16.0 * float(np.log(2.0)))
                    for r in range(2):
                        dve.memset(tmp["v1"][:, r, :, :, HD:HD + 1], 1.0)

                @block.gpsimd
                def _(pool):
                    pool.memset(tmp["probs"][:], 0.0).then_inc(filled, 1)
            with nc.Fori(0, GROUPS) as g:
                xg = x[:, bass.ds(g * GT, GT), :]
                with nc.Block() as block:
                    @block.vector
                    def _(dve):
                        ln.vector(dve, xg)
                        dve.wait_ge(ln.normed, GT)
                        dve.tensor_copy(xg, ln.xn).then_inc(ln.ready, 1)

                    @block.scalar
                    def _(act):
                        ln.scalar(act, copy=False)
                restart(nc, ln.sems)

        def moves(layer):
            at = lambda n: t[f + n][bass.ds(layer, 1)]
            scale_moves = []
            for n, name in ((0, "q_scale"), (2, "k_scale")):
                s = at(name)
                scale_moves += [(scales[:, n, :], s.broadcast_to([P, HD])),
                                (scales[:, n + 1, 0:HD // 2], s[:, HD // 2:].broadcast_to([P, HD // 2])),
                                (scales[:, n + 1, HD // 2:], s[:, 0:HD // 2].broadcast_to([P, HD // 2]))]
            full = sum(m == P for _, m in MLP_CHUNKS)
            rest = MLP_CHUNKS[-1][1]
            return {"scales": scale_moves, "attention": [(lw["Wqkv"][:], at("Wqkv").rearrange("l d n -> d (l n)"))],
                    "Wo": [(lw["Wo"][:], at("Wo").rearrange("l (j p) d -> p (l j) d", p=P))],
                    "mlp": [(lw["W1"][:], at("W1").rearrange("l d n -> d (l n)")),
                            (lw["W2"][:, 0:full, :], at("W2")[:, 0:full * P, :].rearrange("l (c p) d -> p (l c) d", p=P)),
                            (lw["W2"][0:rest, full, :], at("W2")[:, full * P:, :].rearrange("l p d -> p (l d)")),
                            (lw["b1"][:], at("b1T").rearrange("l p c -> p (l c)")), (lw["b2"][:], at("b2").broadcast_to([P, D])),
                            (lw["ln_g"][:], at("ln_g").rearrange("l d -> d l")), (lw["ln_b"][:], at("ln_b").rearrange("l d -> d l"))]}

        loaded = {n: (s, 16 * len(moves(0)[n])) for n, s in
                  (("scales", scales_loaded), ("attention", attention_loaded), ("Wo", wo_loaded), ("mlp", mlp_loaded))}

        def load(layer, *kinds):
            with nc.Block() as block:
                @block.sync
                def _(sp):
                    for kind in kinds:
                        for tile, source in moves(layer)[kind]:
                            sp.dma_start(tile, source).then_inc(loaded[kind][0], 16)

        def reload(layer, *kinds):
            restart(nc, [loaded[kind][0] for kind in kinds])
            load(layer, *kinds)

        with ExitStack() as inner:
            sems = signals(nc, inner, ATTENTION_SIGNALS), signals(nc, inner, MLP_SIGNALS)
            step = lambda *args, **more: local_step(nc, y, banks, consts, lw, loaded, tables, tmp, sems, *args, **more)

            def middle():
                with nc.Fori(0, (GROUPS - 2) // 2) as pair:
                    g = 2 * pair
                    step(g + 1, g + 2, g, 1)
                    step(g + 2, g + 3, g + 1, 0)

            load(0, "scales", "attention", "Wo")
            step(None, 0, None, 1, new_tables=True)
            step(0, 1, None, 0, new_peak=True)
            load(0, "mlp")
            with nc.Fori(0, DEPTH - 1) as layer:
                middle()
                reload(layer + 1, "scales", "attention")
                step(GROUPS - 1, 0, GROUPS - 2, 1, new_tables=True)
                reload(layer + 1, "Wo")
                step(0, 1, GROUPS - 1, 0, new_peak=True)
                reload(layer + 1, "mlp")
            middle()
            step(GROUPS - 1, None, GROUPS - 2, 1)
            step(None, None, GROUPS - 1, 0)

        back = tmp["rot"].rearrange("p a b t n -> p (a b t n)")[:, 0:TILES * D].rearrange("p (t d) -> p t d", d=D)
        with nc.Block() as block:
            @block.sync
            def _(sp):
                sp.dma_start(back, residual).then_inc(returned, 16)

            @block.vector
            def _(dve):
                dve.wait_ge(returned, 16)
                dve.tensor_tensor(x[:], y[:], back, ALU.add)


STAGES = ["favor", "router", "cosine", "int4", "mamba", "experts", "hgrn", "local"]


class Weights:

    def __init__(self, nc, ctx, outer, t, stage, prefix):
        self.nc, self.ctx, self.t, self.prefix, self.stage = nc, ctx, t, prefix, stage
        self.moves, self.tiles = [], {"loaded": signals(nc, outer, stage + "_loaded")[0]}

    def add(self, name, shape, source):
        tile = self.ctx.enter_context(self.nc.sbuf_tensor(f"{self.stage}_w_{name}", shape, F32))
        self.tiles[name] = tile
        self.moves.append((tile[:], source))
        self.tiles["total"] = 16 * len(self.moves)
        return tile

    def load(self, sp):
        for tile, source in self.moves:
            sp.dma_start(tile, source).then_inc(self.tiles["loaded"], 16)


def weights(nc, ctx, outer, t, names):
    row = lambda a: a.rearrange("(o n) -> o n", o=1)
    column = lambda a: a.rearrange("(n o) -> n o", o=1)

    made = {}
    if "favor" in names:
        favor = Weights(nc, ctx, outer, t, "favor", "L0_attn_")
        for n in ("Wq", "Wk", "Wv"):
            favor.add(n, [P, INNER], t["L0_attn_" + n])
        favor.add("Wo", [P, PAIRS, D], t["L0_attn_Wo"].rearrange("(j p) d -> p j d", p=P))
        favor.add("Wfeat", [P, NF], t["Wfeat"])
        made["favor"] = favor
    if "router" in names:
        f = "L0_ffn_"
        router = Weights(nc, ctx, outer, t, "router", f)
        router.add("W1T", [P, 512], t["L0_ffn_W1T"])
        router.add("W2T", [P, 4, D], t["L0_ffn_W2T"].rearrange("(c p) d -> p c d", p=P))
        router.add("ln_g", [P, 1], column(t[f + "ln_g"]))
        router.add("ln_b", [P, 1], column(t[f + "ln_b"]))
        router.add("RT", [P, 64], t["L0_ffn_router_WT"])
        router.add("rb", [1, 64], row(t[f + "router_b"]))
        router.add("U", [64, D], t[f + "raw_U"])
        router.add("V", [64, D], t[f + "raw_V"])
        router.add("gamma", [64, D], t[f + "gamma"].rearrange("a b d -> (a b d)").partition_broadcast(64))
        made["router"] = router
    if "cosine" in names:
        f = "L1_attn_"
        cosine = Weights(nc, ctx, outer, t, "cosine", f)
        cosine.add("Wqkv", [P, 3 * INNER], None)
        cosine.moves.pop()
        cosine.moves += [(cosine.tiles["Wqkv"][:, 0:INNER], t[f + "w_q"]), (cosine.tiles["Wqkv"][:, INNER:], t[f + "w_kv"])]
        cosine.add("Wo", [P, PAIRS, D], t[f + "w_out"].rearrange("(j p) d -> p j d", p=P))
        cosine.add("bo", [1, D], row(t[f + "b_out"]))
        cosine.add("scale", [P, H], t[f + "scale"].rearrange("a h b c -> (a h b c)").partition_broadcast(P))
        made["cosine"] = cosine
    if "int4" in names:
        f = "L1_ffn_"
        int4 = Weights(nc, ctx, outer, t, "int4", f)
        int4.add("kernel", [P, D], t[f + "kernel"])
        int4.add("bias", [1, D], row(t[f + "bias"]))
        int4.add("a", [P, 16], t[f + "a"])
        int4.add("b", [16, D], t[f + "b"])
        made["int4"] = int4
    if "mamba" in names:
        f = "L2_attn_"
        mamba = Weights(nc, ctx, outer, t, "mamba", f)
        mamba.add("Win", [P, 512], t[f + "Win"])
        mamba.add("bin", [P, 4], t[f + "binT"])
        mamba.add("Wdp", [P, 2, 8], t[f + "Wx"].rearrange("(c p) n -> p c n", p=P)[:, :, 0:8])
        mamba.add("Wbc", [P, 2, 192], t[f + "Wbc"].rearrange("(c p) n -> p c n", p=P))
        mamba.add("bdp", [8, 1], column(t[f + "bx"][0:8]))
        mamba.add("bbc", [96, 2], t[f + "bbc"])
        mamba.add("Wdt", [8, 256], t[f + "Wdt"])
        mamba.add("bdt", [P, 2], t[f + "bdtT"])
        mamba.add("A_log", [P, 2, 16], t[f + "A_log"].rearrange("(c p) n -> p c n", p=P))
        mamba.add("Dp", [P, 2], t[f + "DpT"])
        mamba.add("Wout", [P, 2, D], t[f + "Wout"].rearrange("(c p) d -> p c d", p=P))
        mamba.add("bout", [1, D], row(t[f + "bout"]))
        mamba.tiles["pick"] = t["pick"]
        made["mamba"] = mamba
    if "experts" in names:
        f = "L2_ffn_"
        experts = Weights(nc, ctx, outer, t, "experts", f)
        experts.add("Wg", [P, 8], t[f + "Wg"])
        experts.add("bg", [1, 8], row(t[f + "bg"]))
        experts.add("W1", [P, 8, 512], t[f + "W1"].rearrange("e d f -> d e f"))
        experts.add("b1", [P, 32], t[f + "b1T"])
        experts.add("W2", [P, 8, 4, D], t[f + "W2"].rearrange("e (c p) d -> p e c d", p=P))
        experts.add("b2", [8, D], t[f + "b2"])
        experts.add("gamma", [P, D], t[f + "gamma"].partition_broadcast(P))
        experts.add("beta", [P, D], t[f + "beta"].partition_broadcast(P))
        made["experts"] = experts
    if "hgrn" in names:
        f = "L3_attn_"
        hgrn = Weights(nc, ctx, outer, t, "hgrn", f)
        for n, m in (("Wq", D), ("Wk", D), ("Wv", D), ("G1", 64), ("Wo", D)):
            hgrn.add(n, [P, m], t[f + n])
        hgrn.add("G2", [64, D], t[f + "G2"])
        hgrn.add("delta", [P, 1], column(t[f + "delta"]))
        hgrn.add("norm_w", [P, 1], column(t[f + "norm_w"]))
        made["hgrn"] = hgrn
    return made


FIRST_STAGES = ("favor", "router", "cosine")
RUN = {"favor": favor_attention, "router": router_ffn, "cosine": cosine_attention, "int4": int4_linear,
       "mamba": state_space, "experts": expert_ffn, "hgrn": gated_recurrence}


def build(nc, t, out, stages):
    with ExitStack() as ctx:
        sb = lambda n, s, d=F32: ctx.enter_context(nc.sbuf_tensor(n, s, d))
        banks = ctx.enter_context(nc.psum_tensor("banks", [P, 8, 512], F32))
        x = sb("x", [P, TILES, D])
        consts = {n: sb(n, list(t[n].shape))[:] for n in ("ident", "ones", "next", "carry", "band")}
        x_loaded, consts_loaded, stored = signals(nc, ctx, "x_loaded consts_loaded stored")
        held = ctx.enter_context(ExitStack())
        consts |= {n: held.enter_context(nc.sbuf_tensor(n, list(t[n].shape), F32))[:]
                   for n in ("causal", "count", "inside", "blocks")}
        ws = weights(nc, held, ctx, t, ("router", "int4", "mamba", "hgrn"))
        early = ctx.enter_context(ExitStack())
        ws = weights(nc, early, ctx, t, ("favor", "cosine")) | ws

        with nc.Block() as block:
            @block.sync
            def _(sp):
                sp.dma_start(x[:], t["L0_attn_x"].rearrange("b (t p) d -> p (b t) d", p=P)).then_inc(x_loaded, 16)
                for n in consts:
                    sp.dma_start(consts[n], t[n]).then_inc(consts_loaded, 16)
                for name in ("favor", "router", "cosine", "int4", "mamba", "hgrn"):
                    ws[name].load(sp)
                sp.wait_ge(x_loaded, 16)
                sp.wait_ge(consts_loaded, 16 * len(consts))
        for stage in stages:
            if "experts" not in ws and stage not in FIRST_STAGES:
                early.close()
                ws |= weights(nc, held, ctx, t, ("experts",))
                with nc.Block() as block:
                    @block.sync
                    def _(sp):
                        for name in ("favor", "cosine"):
                            sp.wait_ge(ws[name].tiles["loaded"], ws[name].tiles["total"])
                        ws["experts"].load(sp)
            if stage != "local":
                RUN[stage](nc, x, banks, consts, ws[stage].tiles)
        with nc.Block() as block:
            @block.sync
            def _(sp):
                for w in ws.values():
                    sp.wait_ge(w.tiles["loaded"], w.tiles["total"])
        early.close()
        held.close()
        if "local" in stages:
            local_layers(nc, x, banks, consts, t, out)
        with nc.Block() as block:
            @block.sync
            def _(sp):
                sp.dma_start(out.rearrange("b (t p) d -> p (b t) d", p=P), x[:]).then_inc(stored, 16)
                sp.wait_ge(stored, 16)


def rotary():
    half = np.arange(0, HD, 2, dtype=np.float32)
    inv_freq = 1.0 / np.float32(10000.0) ** (half / HD)
    at = np.arange(SEQ, dtype=np.float32)
    freqs = at[:, None] * inv_freq[None, :]
    base = (half + 0.4 * HD) / (1.4 * HD)
    scale = base[None, :].astype(np.float64) ** ((at - SEQ // 2) / (WINDOW // 2))[:, None]
    cos, sin = np.cos(freqs.astype(np.float64)), np.sin(freqs.astype(np.float64))
    four = [np.concatenate([cos * s, cos * s], 1) if c else np.concatenate([-sin * s, sin * s], 1)
            for s in (scale, 1 / scale) for c in (True, False)]
    return np.ascontiguousarray(np.stack(four).reshape(4, ST, P, HD).transpose(2, 0, 1, 3)).astype(np.float32)


def shape_constants():
    i = np.arange(P)
    ahead = np.arange(P + WINDOW)[None, :] - i[:, None]
    seen = np.where((ahead >= 0) & (ahead <= WINDOW), 0.0, -1e30).astype(np.float32)
    band = np.concatenate([seen, seen[:, :P]], 1)
    tri = (i[:, None] <= i[None, :]).astype(np.float32)
    return {"ident": np.eye(P, dtype=np.float32), "causal": np.concatenate([tri, np.ones((P, P), np.float32), tri], 1),
            "ones": np.ones((P, P), np.float32),
            "pick": np.tile(np.repeat(np.eye(32, 16, dtype=np.float32), P, 1), (3, 1)),
            "count": np.tile(np.arange(8, dtype=np.float32), (P, 1)),
            "inside": np.tile((np.arange(GN) % 64 != 0).astype(np.float32), (P, 1)),
            "next": np.eye(P, k=1, dtype=np.float32),
            "carry": (np.arange(P * P).reshape(P, P) == (P - 1) * P).astype(np.float32),
            "rotary": rotary(), "band": band,
            "blocks": np.kron(np.eye(2, dtype=np.float32), np.ones((64, 64), np.float32))}


def layouts(a):
    w = {k: np.ascontiguousarray(v) for k, v in a.items()}
    w["Wfeat"] = np.concatenate([np.asarray(a["L0_attn_W_feat"]), np.full((HD, NF), -0.5, np.float32)], 0)
    for n in ("L0_ffn_W1", "L0_ffn_W2", "L0_ffn_router_W"):
        w[n + "T"] = np.ascontiguousarray(w[n].T)
    columns = [slice(8, 24)] * 6 + [slice(24, 40)] * 6
    w["L2_attn_Wbc"] = np.concatenate([w["L2_attn_Wx"][:, c] for c in columns], 1)
    w["L2_attn_bbc"] = np.ascontiguousarray(np.concatenate([w["L2_attn_bx"][c] for c in columns]).reshape(2, 96).T)
    b1 = np.zeros((DEPTH, 2, len(MLP_CHUNKS) * P), np.float32)
    b1[:, :, :MLP] = w["L3_ffn_b1"].reshape(DEPTH, 2, MLP)
    w["L3_ffn_b1T"] = np.ascontiguousarray(b1.reshape(DEPTH, -1, P).transpose(0, 2, 1))
    for n in ("L2_attn_bin", "L2_attn_bdt", "L2_attn_Dp", "L2_ffn_b1"):
        w[n + "T"] = np.ascontiguousarray(w[n].reshape(-1, P).T)
    return w


def kernel(**inputs):
    import concourse.bacc as bacc
    from concourse.bass_utils import run_bass_kernel_spmd

    nc = bacc.Bacc("TRN2", target_bir_lowering=False, num_devices=1)
    arrays = layouts({k: np.asarray(v) for k, v in inputs.items()}) | shape_constants()
    t = {n: nc.dram_tensor("in_" + n, a.shape, mybir.dt.from_np(a.dtype), kind="ExternalInput").ap() for n, a in arrays.items()}
    out = nc.dram_tensor("out", (BATCH, SEQ, D), F32, kind="ExternalOutput").ap()
    build(nc, t, out, STAGES)
    return run_bass_kernel_spmd(nc, [{"in_" + n: a for n, a in arrays.items()}], core_ids=[0]).results[0]["out"]
```
